# Optimizing a Trainium2 kernel written in Bass

```python
import numpy as np
import jax
import jax.numpy as jnp

def _softmax(x, axis=-1):
    return jax.nn.softmax(x, axis=axis)

def _gelu(x):
    return jax.nn.gelu(x, approximate=True)

def _silu(x):
    return jax.nn.silu(x)

def _sigmoid(x):
    return jax.nn.sigmoid(x)

def _layernorm(x, axis=-1, eps=1e-05):
    m = jnp.mean(x, axis=axis, keepdims=True)
    v = jnp.var(x, axis=axis, keepdims=True)
    return (x - m) / jnp.sqrt(v + eps)

def _scatter_add(tgt, idx, src, axis=0):
    return tgt.at[idx].add(src)

def _segment_sum(src, seg, n):
    return jax.ops.segment_sum(src, seg, n)
kernel_name = 'mk_adj_resnorm_d2_adj_r2_afcbfd'

def setup_inputs(seed: int=0):
    np.random.seed(seed)
    _w = jnp.asarray

    def _rec_inputs():
        import jax
        import jax.numpy as jnp
        _gk = jax.random.key(seed)
        x = -0.0002928 + 1 * jax.random.normal(jax.random.fold_in(_gk, 1), (8, 1024, 128), jnp.float32)
        _a = jax.random.bernoulli(jax.random.fold_in(_gk, 2), 0.0078125, (8, 1024, 1024))
        _a = jnp.logical_or(_a, jnp.swapaxes(_a, -1, -2))
        _a = jnp.logical_or(_a, jnp.eye(1024, dtype=bool))
        adj = _a.astype(jnp.int32)
        return (x, adj)
    x, adj = _rec_inputs()

    def _L0_gnn_setup():
        import jax, jax.numpy as jnp
        import numpy as np
        UNITS = 128
        NUM_HEADS = 8
        HEAD_DIM = UNITS // NUM_HEADS
        B, N = (8, 1024)
        key = jax.random.key(seed)
        ks = jax.random.split(key, 7)
        node_features = jax.random.normal(ks[0], (B, N, UNITS), dtype=jnp.float32)
        adjacency_matrix = jax.random.randint(ks[1], (B, N, N), 0, 2, dtype=jnp.int32)
        s = 1.0 / np.sqrt(UNITS)
        Wq = jax.random.normal(ks[2], (UNITS, UNITS), dtype=jnp.float32) * s
        Wk = jax.random.normal(ks[3], (UNITS, UNITS), dtype=jnp.float32) * s
        Wv = jax.random.normal(ks[4], (UNITS, UNITS), dtype=jnp.float32) * s
        Wo = jax.random.normal(ks[5], (UNITS, UNITS), dtype=jnp.float32) * s
        bo = jnp.zeros((UNITS,), dtype=jnp.float32)
        return {'node_features': node_features, 'adjacency_matrix': adjacency_matrix, 'Wq': Wq, 'Wk': Wk, 'Wv': Wv, 'Wo': Wo, 'bo': bo}
    _L0_gnn_all = _L0_gnn_setup()
    _L0_gnn_in = {k: v for k, v in _L0_gnn_all.items() if k in ('Wq', 'Wk', 'Wv', 'Wo', 'bo')}
    del _L0_gnn_all

    def _L1_gnn_setup():
        import jax, jax.numpy as jnp
        import numpy as np
        B, S, DIN, DOUT = (8, 1024, 128, 128)
        ALPHA = 0.2
        NEG = -9000000000000000.0
        key = jax.random.key(seed)
        k1, k2, k3, k4 = jax.random.split(key, 4)
        x = jax.random.normal(k1, (B, S, DIN), dtype=jnp.float32)
        adj = jax.random.randint(k2, (B, S, S), 0, 2, dtype=jnp.int32)
        limW = float(np.sqrt(6.0 / (DIN + DOUT)))
        lima = float(np.sqrt(6.0 / (2 * DOUT + 1)))
        W = jax.random.uniform(k3, (DOUT, DIN), jnp.float32, -limW, limW)
        a = jax.random.uniform(k4, (1, 2 * DOUT), jnp.float32, -lima, lima)
        return {'x': x, 'adj': adj, 'W': W, 'a': a}
    _L1_gnn_all = _L1_gnn_setup()
    _L1_gnn_in = {k: v for k, v in _L1_gnn_all.items() if k in ('W', 'a')}
    del _L1_gnn_all
    return {'x': x, 'adj': adj, 'L0_gnn_Wq': _L0_gnn_in['Wq'], 'L0_gnn_Wk': _L0_gnn_in['Wk'], 'L0_gnn_Wv': _L0_gnn_in['Wv'], 'L0_gnn_Wo': _L0_gnn_in['Wo'], 'L0_gnn_bo': _L0_gnn_in['bo'], 'L1_gnn_W': _L1_gnn_in['W'], 'L1_gnn_a': _L1_gnn_in['a']}

def reference(x, adj, L0_gnn_Wq, L0_gnn_Wk, L0_gnn_Wv, L0_gnn_Wo, L0_gnn_bo, L1_gnn_W, L1_gnn_a):
    import jax
    import jax.numpy as jnp

    def _L0_gnn_ref(node_features, adjacency_matrix, Wq, Wk, Wv, Wo, bo):
        import jax, jax.numpy as jnp
        import numpy as np
        UNITS = 128
        NUM_HEADS = 8
        HEAD_DIM = UNITS // NUM_HEADS
        B, N = (8, 1024)
        b, n, _ = node_features.shape
        h, d = (NUM_HEADS, HEAD_DIM)
        q = (node_features @ Wq).reshape(b, n, h, d).transpose(0, 2, 1, 3)
        k = (node_features @ Wk).reshape(b, n, h, d).transpose(0, 2, 1, 3)
        v = (node_features @ Wv).reshape(b, n, h, d).transpose(0, 2, 1, 3)
        scores = jnp.einsum('bhqd,bhkd->bhqk', q, k) / jnp.sqrt(jnp.float32(d))
        mask = adjacency_matrix[:, None, :, :] > 0
        scores = jnp.where(mask, scores, jnp.float32(-1000000000.0))
        w = jax.nn.softmax(scores, axis=-1)
        ctx = jnp.einsum('bhqk,bhkd->bhqd', w, v)
        ctx = ctx.transpose(0, 2, 1, 3).reshape(b, n, h * d)
        return ctx @ Wo + bo

    def _L1_gnn_ref(x, adj, W, a):
        import jax, jax.numpy as jnp
        import numpy as np
        B, S, DIN, DOUT = (8, 1024, 128, 128)
        ALPHA = 0.2
        NEG = -9000000000000000.0
        h = jnp.einsum('bsf,of->bso', x, W)
        a1 = a[0, :DOUT]
        a2 = a[0, DOUT:]
        f_i = h @ a1
        f_j = h @ a2
        e = f_i[:, :, None] + f_j[:, None, :]
        e = jnp.where(e >= 0, e, ALPHA * e)
        att = jnp.where(adj > 0, e, NEG)
        att = jax.nn.softmax(att, axis=2)
        h_prime = jnp.einsum('bij,bjo->bio', att, h)
        return h_prime
    x = _layernorm(x + _L0_gnn_ref(x, adj, L0_gnn_Wq, L0_gnn_Wk, L0_gnn_Wv, L0_gnn_Wo, L0_gnn_bo), axis=-1)
    x = _layernorm(x + _L1_gnn_ref(x, adj, L1_gnn_W, L1_gnn_a), axis=-1)
    return x

_drawn_inputs = setup_inputs


def setup_inputs(seed=0):
    import zlib

    import numpy as np

    out = dict(_drawn_inputs(seed))
    spreads = {'L0_gnn_bo': (0.0, 0.1)}
    factors = {}
    for name, (base, spread) in spreads.items():
        noise = np.random.default_rng([zlib.crc32(name.encode()), seed]).standard_normal(out[name].shape)
        drawn = base * np.exp(spread * noise) if base else spread * noise
        out[name] = jnp.asarray(drawn.astype(out[name].dtype))
    for name, factor in factors.items():
        out[name] = (out[name] * factor).astype(out[name].dtype)
    return out
```

```python
from contextlib import ExitStack

import concourse.bass as bass
from concourse import mybir

ALU = mybir.AluOpType
ACT = mybir.ActivationFunctionType
F32 = mybir.dt.float32
BF16 = mybir.dt.bfloat16
I32 = mybir.dt.int32
AX_X = mybir.AxisListType.X

BIG = 1.0e9
FLOOR = -1.0e8
EPS = 1e-5
ALPHA = 0.2

KPART = (0, 0, 1, 1, 0, 2)
QPART = (0, 1, 0, 1, 2, 0)
BLOCKS = len(KPART)


def build(nc, x, xT, adj, adjT, Wq, Wk, Wv, Wo, bo, W, a, out):
    B, N, D = x.shape
    H = 8
    HD = D // H
    T = N // 128
    HALF = N // 2
    CH = T // 2
    HG = 4
    NG = H // HG
    SCALE = 1.0 / float(HD) ** 0.5
    KROWS = BLOCKS * HD
    SROWS = KROWS + 3
    HW = D + 3
    VW = 32

    with ExitStack() as ctx:
        def sb(name, shape, dt):
            return ctx.enter_context(nc.sbuf_tensor(name, shape, dt))

        def sem(name):
            return ctx.enter_context(nc.semaphore(name))

        slots = [ctx.enter_context(nc.psum_tensor(f"slot{i}", [128, N], F32)) for i in range(3)]
        acc = ctx.enter_context(nc.psum_tensor("acc", [128, N], F32))

        ident = sb("ident", [128, 128], F32)
        identb = sb("identb", [128, 128], BF16)
        ones = sb("ones", [128, 128], F32)
        negones = sb("negones", [128, 128], F32)
        wq = sb("wq", [D, D], F32)
        wk = sb("wk", [D, D], F32)
        wv = sb("wv", [D, D], F32)
        wo = sb("wo", [D, D], F32)
        w_of = sb("w_of", [D, D], F32)
        acol = sb("acol", [D, 2], F32)
        a1wide = sb("a1wide", [D, D], F32)
        wh = sb("wh", [D, D + 2], F32)
        u1wide = sb("u1wide", [D, 2, D], F32)
        bo_all = sb("bo_all", [128, D], F32)
        exponent = sb("exponent", [128, T], F32)

        carrier = sb("carrier", [128, H * T + 2], F32)

        xT_sb = sb("xT_sb", [D, N], F32)
        x_sb = sb("x_sb", [128, T, D], F32)
        xb = sb("xb", [128, T, D], F32)
        raw = [sb(f"raw{i}", [128, 2, N], I32) for i in range(2)]
        biasT = sb("biasT", [128, T, N], BF16)
        biasN = sb("biasN", [128, T, N], BF16)
        rest = sb("rest", [128, N], F32)
        parts = [[sb(f"{n}part{i}", [128, N], BF16) for i in range(3)] for n in "qk"]
        qst = sb("qst", [SROWS, H, N], BF16)
        kst = sb("kst", [SROWS, H, N], BF16)
        vst = sb("vst", [128, T, H, VW], F32)
        vsum = sb("vsum", [128, H, VW], F32)
        rowmax = sb("rowmax", [128, H * T], F32)
        negmax = sb("negmax", [128, H * T], F32)
        negrest = sb("negrest", [H * T, 128], F32)
        negparts = [sb(f"negpart{i}", [H * T, 128], BF16) for i in range(3)]
        weights = sb("weights", [128, T, N], F32)
        ctxT = sb("ctxT", [128, NG, N], F32)
        ctxn = sb("ctxn", [128, T, D], F32)
        fix = sb("fix", [128, 4, H, HD], F32)
        den = sb("den", [128, T, H], F32)
        empty = sb("empty", [128, T, H], F32)
        rden = sb("rden", [128, T, H], F32)
        ctxnT = sb("ctxnT", [D, N], F32)
        y = sb("y", [128, T, D], F32)
        x1 = sb("x1", [128, T, D], F32)
        x1T = sb("x1T", [D, N], F32)
        stats = sb("stats", [128, T, 6], F32)
        meanvar = sb("meanvar", [128, T, 2], F32)
        vareps = sb("vareps", [128, T], F32)
        rstd = sb("rstd", [128, T], F32)
        hst = sb("hst", [128, T, HW], F32)
        hsum = sb("hsum", [128, HW], F32)
        running = sb("running", [128, N], F32)
        nbmax = sb("nbmax", [128, T], F32)
        shift = sb("shift", [128, T], F32)
        diag = sb("diag", [128, T, 128], F32)
        row1 = rest
        row2 = sb("row2", [128, N], F32)

        scratch = nc.dram_tensor("parts_scratch", [2, 3, H, HD, N], BF16, kind="Internal").ap()
        negscratch = nc.dram_tensor("neg_scratch", [3, H * T, 128], BF16, kind="Internal").ap()

        jobs = ["q", "k", "v", "vsum"]
        jobs += [("max", h, t) for h in range(H) for t in range(T)]
        jobs += ["negmax"]
        jobs += [("unit", g, t, i) for g in range(NG) for t in range(T) for i in range(HG)]
        jobs += ["ctx0", "ctx1", "ctxT", "wo", "x1T", "h0", "h1", "hsum", "runT", "row1", "row2",
                 "out0", "out1"]
        slot_of = {j: n % 3 for n, j in enumerate(jobs)}
        use_of = {j: n // 3 for n, j in enumerate(jobs)}
        uses = [sum(1 for j in jobs if slot_of[j] == s) for s in range(3)]
        slot_full = [sem(f"slot{i}_full") for i in range(3)]
        slot_free = [sem(f"slot{i}_free") for i in range(3)]

        def free_for(b, job):
            return slot_free[slot_of[job]], b * uses[slot_of[job]] + use_of[job]

        def full(b, job):
            return slot_full[slot_of[job]], b * uses[slot_of[job]] + use_of[job] + 1

        def read_by(b, job):
            return slot_free[slot_of[job]], b * uses[slot_of[job]] + use_of[job] + 1

        def alone(eng, at):
            eng.memset(carrier[:, at:at + 1], 0.0)

        consts_in = sem("consts_in")
        bo_in = sem("bo_in")
        consts_made = sem("consts_made")
        setup_mm = sem("setup_mm")
        setup_copied = sem("setup_copied")
        x_in = sem("x_in")
        raw_in = [sem(f"raw{i}_in") for i in range(2)]
        masks_made = sem("masks_made")
        part0_made = sem("part0_made")
        parts_made = sem("parts_made")
        parts_out = sem("parts_out")
        stacks_in = sem("stacks_in")
        vsum_made = sem("vsum_made")
        negparts_made = sem("negparts_made")
        negparts_out = sem("negparts_out")
        negmax_made = sem("negmax_made")
        units_used = sem("units_used")
        acc_full = sem("acc_full")
        acc_read = sem("acc_read")
        ctxn_made = sem("ctxn_made")
        xb_made = sem("xb_made")
        vareps_made = sem("vareps_made")
        rstd_made = sem("rstd_made")
        x1_made = sem("x1_made")
        running_made = sem("running_made")
        diag_made = sem("diag_made")
        logits_made = sem("logits_made")
        logits_masked = sem("logits_masked")
        weights_made = sem("weights_made")
        y_out = sem("y_out")
        out_done = sem("out_done")
        dve_step = sem("dve_step")
        pool_step = sem("pool_step")
        DVE_STEPS = 46
        SETUP_STEPS = 1

        block = ctx.enter_context(nc.Block())
        bo_row = bo.rearrange("(o d) -> o d", o=1)

        @block.sync
        def _(sp):
            for dst, src in ((wq, Wq), (wk, Wk), (wv, Wv), (wo, Wo), (w_of, W),
                             (acol, a.rearrange("o (c d) -> d (o c)", c=2))):
                with nc.allow_non_contiguous_dma(reason="a is 256 numbers"):
                    sp.dma_start(dst[:], src).then_inc(consts_in, 16)
            sp.dma_start(bo_all[:], bo_row.to_broadcast([128, D])).then_inc(bo_in, 16)
            def batch(b):
                sp.wait_ge(slot_full[slot_of["v"]], b * uses[slot_of["v"]])
                sp.wait_ge(xb_made, b)
                sp.dma_start(xT_sb[:], xT[b]).then_inc(x_in, 16)
                sp.dma_start(x_sb[:], x[b].rearrange("(t p) d -> p t d", p=128)).then_inc(x_in, 16)
                for c in range(2 * CH):
                    src = (adjT if c < CH else adj)[b].rearrange("(t p) n -> p t n", p=128)
                    t0 = 2 * (c % CH)
                    if c >= 2:
                        sp.wait_ge(masks_made, b * 2 * CH + c - 1)
                    else:
                        sp.wait_ge(masks_made, b * 2 * CH)
                    sp.dma_start(raw[c % 2][:], src[:, t0:t0 + 2, :]).then_inc(raw_in[c % 2], 16)
                for s in range(2):
                    sp.wait_ge(parts_made, 2 * b + s + 1)
                    for i in range(3):
                        sp.dma_start(scratch[s, i].rearrange("h d n -> (h d) n"),
                                     parts[s][i][:]).then_inc(parts_out, 16)
                sp.wait_ge(parts_out, b * 96 + 96)
                sp.wait_ge(units_used, b * H * T)
                for r in range(BLOCKS):
                    rows = slice(r * HD, (r + 1) * HD)
                    sp.dma_start(qst[rows], scratch[0, QPART[r]].rearrange("h d n -> d h n")).then_inc(stacks_in, 16)
                    sp.dma_start(kst[rows], scratch[1, KPART[r]].rearrange("h d n -> d h n")).then_inc(stacks_in, 16)
                sp.wait_ge(negparts_made, b + 1)
                for i in range(3):
                    sp.dma_start(negscratch[i], negparts[i][:]).then_inc(negparts_out, 16)
                sp.wait_ge(negparts_out, b * 48 + 48)
                sp.dma_start(qst[KROWS:SROWS],
                             negscratch.rearrange("i (h t) n -> i h (t n)", h=H)).then_inc(negmax_made, 16)
                sp.wait_ge(y_out, b + 1)
                sp.dma_start(out[b].rearrange("(t p) d -> p t d", p=128), y[:]).then_inc(out_done, 16)

            batch(0)
            with sp.Fori(1, B) as b:
                batch(b)
            sp.wait_ge(out_done, 16 * B)

        @block.tensor
        def _(pe):
            kw = dict(start=True, stop=True)
            pe.wait_ge(consts_in, 96)
            pe.wait_ge(consts_made, 2)
            pe.transpose(slots[0][:, 0:D], w_of[:], ident[:])
            pe.matmul(slots[0][:, D:D + 2], w_of[:], acol[:], **kw)
            pe.matmul(slots[0][:, 256:256 + D], w_of[:], a1wide[:], **kw).then_inc(setup_mm, 1)
            pe.wait_ge(setup_copied, 1)
            def batch(b):
                pe.wait_ge(x_in, b * 32 + 32)
                for job, w in (("q", wq), ("k", wk)):
                    pe.wait_ge(*free_for(b, job))
                    ps = slots[slot_of[job]]
                    for c in range(2):
                        cols = slice(c * HALF, (c + 1) * HALF)
                        mm = pe.matmul(ps[:, cols], w[:], xT_sb[:, cols], **kw)
                    mm.then_inc(slot_full[slot_of[job]], 1)
                pe.wait_ge(*free_for(b, "v"))
                ps = slots[slot_of["v"]]
                for t in range(T):
                    mm = pe.matmul(ps[:, t * 128:(t + 1) * 128], xT_sb[:, t * 128:(t + 1) * 128], wv[:], **kw)
                mm.then_inc(slot_full[slot_of["v"]], 1)
                pe.wait_ge(*free_for(b, "vsum"))
                ps = slots[slot_of["vsum"]]
                pe.wait_ge(*read_by(b, "v"))
                for t in range(T):
                    mm = pe.matmul(ps[:, 0:H * VW], ones[:], vst[:, t].rearrange("p h d -> p (h d)"),
                                   start=(t == 0), stop=(t == T - 1))
                mm.then_inc(slot_full[slot_of["vsum"]], 1)

                pe.wait_ge(stacks_in, b * 32 * BLOCKS + 32 * BLOCKS)
                for h in range(H):
                    for t in range(T):
                        pe.wait_ge(*free_for(b, ("max", h, t)))
                        ps = slots[slot_of[("max", h, t)]]
                        for c in range(2):
                            cols = slice(c * HALF, (c + 1) * HALF)
                            mm = pe.matmul(ps[:, cols], qst[0:KROWS, h, t * 128:(t + 1) * 128],
                                           kst[0:KROWS, h, cols], **kw)
                        mm.then_inc(slot_full[slot_of[("max", h, t)]], 1)
                pe.wait_ge(*free_for(b, "negmax"))
                ps = slots[slot_of["negmax"]]
                pe.wait_ge(dve_step, SETUP_STEPS + b * DVE_STEPS + NEG_STEP)
                mm = pe.matmul(ps[0:H * T, 0:128], negmax[:], ident[:], **kw)
                mm.then_inc(slot_full[slot_of["negmax"]], 1)

                pe.wait_ge(negmax_made, b * 16 + 16)
                pe.wait_ge(masks_made, (b + 1) * 2 * CH)

                def scores(g, t, i):
                    h = g * HG + i
                    job = ("unit", g, t, i)
                    pe.wait_ge(*free_for(b, job))
                    ps = slots[slot_of[job]]
                    for c in range(2):
                        cols = slice(c * HALF, (c + 1) * HALF)
                        pe.matmul(ps[:, cols], identb[:], biasT[:, t, cols], start=True, stop=False)
                        mm = pe.matmul(ps[:, cols], kst[:, h, t * 128:(t + 1) * 128], qst[:, h, cols],
                                       start=False, stop=True)
                    mm.then_inc(slot_full[slot_of[job]], 1)

                def context(g, t):
                    quad = g * T + t
                    for i in range(HG):
                        pe.wait_ge(*read_by(b, ("unit", g, t, i)))
                    if t == 0:
                        pe.wait_ge(acc_read, b * NG + g)
                    for c in range(2):
                        cols = slice(c * HALF, (c + 1) * HALF)
                        for i in range(HG):
                            mm = pe.matmul(acc[VW * i:VW * (i + 1), cols], vst[:, t, g * HG + i],
                                           weights[:, (HG * quad + i) % 8, cols],
                                           start=(t == 0), stop=(t == T - 1))
                    mm.then_inc(units_used, HG)

                quads = [(g, t) for g in range(NG) for t in range(T)]
                for n, (g, t) in enumerate(quads):
                    for i in range(HG):
                        scores(g, t, i)
                    if n:
                        context(*quads[n - 1])
                context(*quads[-1])

                for k in range(2):
                    job = f"ctx{k}"
                    pe.wait_ge(*free_for(b, job))
                    ps = slots[slot_of[job]]
                    pe.wait_ge(acc_read, b * NG + NG)
                    for t in range(4):
                        for g in range(NG):
                            mm = pe.transpose(ps[:, (t * NG + g) * 128:(t * NG + g + 1) * 128],
                                              ctxT[:, g, (4 * k + t) * 128:(4 * k + t + 1) * 128], ident[:])
                    mm.then_inc(slot_full[slot_of[job]], 1)
                pe.wait_ge(*free_for(b, "ctxT"))
                ps = slots[slot_of["ctxT"]]
                pe.wait_ge(ctxn_made, 2 * b + 2)
                for t in range(T):
                    mm = pe.transpose(ps[:, t * 128:(t + 1) * 128], ctxn[:, t], ident[:])
                mm.then_inc(slot_full[slot_of["ctxT"]], 1)
                pe.wait_ge(*free_for(b, "wo"))
                ps = slots[slot_of["wo"]]
                pe.wait_ge(*read_by(b, "ctxT"))
                for t in range(T):
                    mm = pe.matmul(ps[:, t * 128:(t + 1) * 128], ctxnT[:, t * 128:(t + 1) * 128], wo[:], **kw)
                mm.then_inc(slot_full[slot_of["wo"]], 1)

                pe.wait_ge(*free_for(b, "x1T"))
                ps = slots[slot_of["x1T"]]
                pe.wait_ge(x1_made, b + 1)
                for t in range(T):
                    mm = pe.transpose(ps[:, t * 128:(t + 1) * 128], x1[:, t], ident[:])
                mm.then_inc(slot_full[slot_of["x1T"]], 1)
                pe.wait_ge(*read_by(b, "x1T"))
                for k in range(2):
                    job = f"h{k}"
                    pe.wait_ge(*free_for(b, job))
                    ps = slots[slot_of[job]]
                    for t in range(4):
                        mm = pe.matmul(ps[:, t * 256:t * 256 + D + 2],
                                       x1T[:, (4 * k + t) * 128:(4 * k + t + 1) * 128], wh[:], **kw)
                    mm.then_inc(slot_full[slot_of[job]], 1)
                pe.wait_ge(*free_for(b, "hsum"))
                ps = slots[slot_of["hsum"]]
                for k in range(2):
                    pe.wait_ge(*read_by(b, f"h{k}"))
                for t in range(T):
                    mm = pe.matmul(ps[:, 0:HW], ones[:], hst[:, t], start=(t == 0), stop=(t == T - 1))
                mm.then_inc(slot_full[slot_of["hsum"]], 1)
                pe.wait_ge(*free_for(b, "runT"))
                ps = slots[slot_of["runT"]]
                pe.wait_ge(running_made, b + 1)
                for t in range(T):
                    mm = pe.transpose(ps[:, t * 128:(t + 1) * 128], running[:, t * 128:(t + 1) * 128], ident[:])
                mm.then_inc(slot_full[slot_of["runT"]], 1)
                for k in range(2):
                    job = f"row{k + 1}"
                    pe.wait_ge(*free_for(b, job))
                    ps = slots[slot_of[job]]
                    pe.wait_ge(diag_made, b + 1)
                    for c in range(2):
                        cols = slice(c * HALF, (c + 1) * HALF)
                        pe.matmul(ps[:, cols], u1wide[:, k], x1T[:, cols], start=True, stop=False)
                        mm = pe.matmul(ps[:, cols], negones[:],
                                       diag[:, 4 * c:4 * c + 4].rearrange("p t n -> p (t n)"),
                                       start=False, stop=True)
                    mm.then_inc(slot_full[slot_of[job]], 1)
                for k in range(2):
                    job = f"out{k}"
                    pe.wait_ge(*free_for(b, job))
                    ps = slots[slot_of[job]]
                    pe.wait_ge(weights_made, b * T + T)
                    for t in range(4):
                        for j in range(T):
                            mm = pe.matmul(ps[:, t * 256:t * 256 + HW],
                                           weights[:, j, (4 * k + t) * 128:(4 * k + t + 1) * 128],
                                           hst[:, j], start=(j == 0), stop=(j == T - 1))
                    mm.then_inc(slot_full[slot_of[job]], 1)

            batch(0)
            with pe.Fori(1, B) as b:
                batch(b)

        @block.scalar
        def _(act):
            act.wait_ge(setup_mm, 1)
            act.activation(wh[:], slots[0][:, 0:D + 2], ACT.Copy)
            act.activation(u1wide[:, 1], slots[0][:, 256:256 + D], ACT.Copy, scale=ALPHA)
            act.activation(u1wide[:, 0], slots[0][:, 256:256 + D], ACT.Copy).then_inc(setup_copied, 1)
            def batch(b):
                for s, job in enumerate("qk"):
                    act.wait_ge(*full(b, job))
                    ps = slots[slot_of[job]]
                    act.wait_ge(parts_out, b * 96)
                    act.activation(parts[s][0][:], ps[:], ACT.Copy).then_inc(part0_made, 1)
                act.wait_ge(*full(b, "vsum"))
                ps = slots[slot_of["vsum"]]
                act.wait_ge(ctxn_made, 2 * b)
                ins = act.activation(vsum[:].rearrange("p h d -> p (h d)"), ps[:, 0:H * VW], ACT.Copy)
                ins.then_inc(slot_free[slot_of["vsum"]], 1)
                n = 0
                for g in range(NG):
                    for t in range(T):
                        for i in range(HG):
                            act.wait_ge(*full(b, ("unit", g, t, i)))
                            ps = slots[slot_of[("unit", g, t, i)]]
                            if n >= 8:
                                act.wait_ge(units_used, b * H * T + n - 7 + (-(n - 7)) % HG)
                            else:
                                act.wait_ge(units_used, b * H * T)
                                if n == 0:
                                    act.wait_ge(y_out, b)
                            ins = act.activation(weights[:, n % 8], ps[:], ACT.Exp, scale=SCALE)
                            ins.then_inc(slot_free[slot_of[("unit", g, t, i)]], 1)
                            n += 1
                act.wait_ge(*full(b, "ctxT"))
                ps = slots[slot_of["ctxT"]]
                ins = act.activation(ctxnT[:], ps[:], ACT.Copy)
                ins.then_inc(slot_free[slot_of["ctxT"]], 1)
                act.wait_ge(*full(b, "x1T"))
                ps = slots[slot_of["x1T"]]
                ins = act.activation(x1T[:], ps[:], ACT.Copy)
                ins.then_inc(slot_free[slot_of["x1T"]], 1)
                for k in range(2):
                    act.wait_ge(*full(b, f"h{k}"))
                    ps = slots[slot_of[f"h{k}"]]
                    view = ps[:].rearrange("p (t w) -> p t w", w=256)[:, :, 0:D + 2]
                    ins = act.activation(hst[:, 4 * k:4 * k + 4, 0:D + 2], view, ACT.Copy)
                    ins.then_inc(slot_free[slot_of[f"h{k}"]], 1)
                act.wait_ge(*full(b, "hsum"))
                ps = slots[slot_of["hsum"]]
                ins = act.activation(hsum[:], ps[:, 0:HW], ACT.Copy)
                ins.then_inc(slot_free[slot_of["hsum"]], 1)
                for k, row in enumerate((row1, row2)):
                    act.wait_ge(*full(b, f"row{k + 1}"))
                    ps = slots[slot_of[f"row{k + 1}"]]
                    ins = act.activation(row[:], ps[:], ACT.Copy)
                    ins.then_inc(slot_free[slot_of[f"row{k + 1}"]], 1)
                for t in range(T):
                    act.wait_ge(logits_masked, b * T + t + 1)
                    act.activation(weights[:, t], weights[:, t], ACT.Exp).then_inc(weights_made, 1)

            batch(0)
            with act.Fori(1, B) as b:
                batch(b)

        @block.gpsimd
        def _(pool):
            pool.memset(ones[:], 1.0)
            pool.memset(negones[:], -1.0)
            pool.memset(exponent[:], -0.5).then_inc(pool_step, 1)
            pool.wait_ge(pool_step, 1)
            pool.affine_select(out=ident[:], in_=ones[:], compare_op=ALU.is_equal, fill=0.0, base=0,
                               pattern=[[-1, 128]], channel_multiplier=1).then_inc(pool_step, 1)
            pool.wait_ge(pool_step, 2)
            pool.tensor_copy(identb[:], ident[:]).then_inc(consts_made, 1)
            pool.wait_ge(bo_in, 16)
            def batch(b):
                pool.wait_ge(x_in, b * 32 + 32)
                pool.wait_ge(x1_made, b)
                pool.tensor_tensor(xb[:], x_sb[:], bo_all[:].unsqueeze(1).to_broadcast([128, T, D]),
                                   ALU.add).then_inc(xb_made, 1)
                pool.wait_ge(vareps_made, 2 * b + 1)
                pool.tensor_tensor(rstd[:], vareps[:], exponent[:], ALU.pow).then_inc(rstd_made, 1)
                for t in range(T):
                    pool.wait_ge(logits_made, b * T + t + 1)
                    pool.tensor_tensor(weights[:, t], weights[:, t], biasT[:, t],
                                       ALU.add).then_inc(logits_masked, 1)
                pool.wait_ge(vareps_made, 2 * b + 2)
                pool.tensor_tensor(rstd[:], vareps[:], exponent[:], ALU.pow).then_inc(rstd_made, 1)

            batch(0)
            with pool.Fori(1, B) as b:
                batch(b)

        @block.vector
        def _(dve):
            steps = [0]
            base = [0]

            def link(ins):
                steps[0] += 1
                ins.then_inc(dve_step, 1)
                dve.wait_ge(dve_step, base[0] + steps[0])

            dve.wait_ge(consts_in, 96)
            dve.memset(kst[KROWS:SROWS], 1.0)
            dve.memset(hst[:, :, D + 2:HW], 1.0)
            link(dve.memset(vst[:, :, :, HD:VW], 0.0))
            dve.memset(vst[:, :, :, HD:HD + 1], 1.0)
            dve.tensor_copy(a1wide[:], acol[:, 0:1].to_broadcast([D, D])).then_inc(consts_made, 1)
            assert steps[0] == SETUP_STEPS

            def layernorm(b, k, src, dst):
                for t in range(T):
                    ins = dve.bn_stats(stats[:, t], src[:, t])
                link(ins)
                alone(dve, H * T + k)
                for t in range(T):
                    ins = dve.bn_aggr(meanvar[:, t], stats[:, t])
                link(ins)
                dve.tensor_scalar(vareps[:], meanvar[:, :, 1], EPS, None, ALU.add).then_inc(vareps_made, 1)
                dve.wait_ge(rstd_made, 2 * b + k + 1)
                for t in range(T):
                    ins = dve.tensor_scalar(dst[:, t], src[:, t], meanvar[:, t, 0:1], rstd[:, t:t + 1],
                                            ALU.subtract, ALU.mult)
                return ins

            def batch(b):
                base[0] = SETUP_STEPS + b * DVE_STEPS
                steps[0] = 0
                for c in range(2 * CH):
                    dve.wait_ge(raw_in[c % 2], (b * CH + c // 2 + 1) * 16)
                    if c == 0:
                        dve.wait_ge(logits_masked, b * T)
                    t0 = 2 * (c % CH)
                    dst = (biasT if c < CH else biasN)[:, t0:t0 + 2, :]
                    dve.tensor_scalar(dst, raw[c % 2][:], 0, -BIG, ALU.is_le, ALU.mult).then_inc(masks_made, 1)
                for s, job in enumerate("qk"):
                    dve.wait_ge(*full(b, job))
                    ps = slots[slot_of[job]]
                    dve.wait_ge(part0_made, 2 * b + s + 1)
                    ins = dve.tensor_tensor(rest[:], ps[:], parts[s][0][:], ALU.subtract)
                    ins.then_inc(slot_free[slot_of[job]], 1)
                    dve.wait_ge(*read_by(b, job))
                    link(dve.tensor_copy(parts[s][1][:], rest[:]))
                    ins = dve.tensor_tensor(parts[s][2][:], rest[:], parts[s][1][:], ALU.subtract)
                    ins.then_inc(parts_made, 1)
                    dve.wait_ge(parts_made, 2 * b + s + 1)
                dve.wait_ge(*full(b, "v"))
                ps = slots[slot_of["v"]]
                ins = dve.tensor_copy(vst[:, :, :, 0:HD], ps[:].rearrange("p (t h d) -> p t h d", t=T, h=H))
                ins.then_inc(slot_free[slot_of["v"]], 1)

                for h in range(H):
                    for t in range(T):
                        dve.wait_ge(*full(b, ("max", h, t)))
                        ps = slots[slot_of[("max", h, t)]]
                        if h == 0 and t == 0:
                            link(dve.memset(rowmax[:], 0.0))
                        alone(dve, h * T + t)
                        ins = dve.tensor_tensor_reduce(ps[:], ps[:], biasN[:, t], 1.0, -3.0e38, ALU.add,
                                                       ALU.max, rowmax[:, h * T + t:h * T + t + 1])
                        ins.then_inc(slot_free[slot_of[("max", h, t)]], 1)
                for t in range(T - 3, T):
                    dve.wait_ge(*read_by(b, ("max", H - 1, t)))
                link(dve.tensor_scalar(negmax[:], rowmax[:], FLOOR, -1.0, ALU.max, ALU.mult))
                assert steps[0] == NEG_STEP, ("neg", steps[0])
                dve.wait_ge(*full(b, "negmax"))
                ps = slots[slot_of["negmax"]]
                neg = ps[0:H * T, 0:128]
                dve.wait_ge(negparts_out, b * 48)
                link(dve.tensor_copy(negparts[0][:], neg))
                ins = dve.tensor_tensor(negrest[:], neg, negparts[0][:], ALU.subtract)
                ins.then_inc(slot_free[slot_of["negmax"]], 1)
                dve.wait_ge(*read_by(b, "negmax"))
                link(dve.tensor_copy(negparts[1][:], negrest[:]))
                dve.tensor_tensor(negparts[2][:], negrest[:], negparts[1][:], ALU.subtract).then_inc(negparts_made, 1)

                for g in range(NG):
                    dve.wait_ge(units_used, b * H * T + (g + 1) * HG * T)
                    dve.tensor_copy(ctxT[:, g], acc[:]).then_inc(acc_read, 1)
                for k in range(2):
                    dve.wait_ge(*full(b, f"ctx{k}"))
                    ps = slots[slot_of[f"ctx{k}"]]
                    view = ps[:].rearrange("p (t h d) -> p t h d", t=4, h=H)
                    tt = slice(4 * k, 4 * k + 4)
                    link(dve.tensor_scalar(empty[:, tt], view[:, :, :, HD], 0.0, None, ALU.is_equal))
                    link(dve.scalar_tensor_tensor(out=den[:, tt], in0=empty[:, tt], scalar=float(N),
                                                  in1=view[:, :, :, HD], op0=ALU.mult, op1=ALU.add))
                    link(dve.reciprocal(rden[:, tt], den[:, tt]))
                    dve.wait_ge(*read_by(b, "vsum"))
                    link(dve.tensor_tensor(fix[:], empty[:, tt].unsqueeze(3).to_broadcast([128, 4, H, HD]),
                                           vsum[:, :, 0:HD].unsqueeze(1).to_broadcast([128, 4, H, HD]), ALU.mult))
                    ins = dve.tensor_tensor(fix[:], view[:, :, :, 0:HD], fix[:], ALU.add)
                    ins.then_inc(slot_free[slot_of[f"ctx{k}"]], 1)
                    dve.wait_ge(*read_by(b, f"ctx{k}"))
                    ins = dve.tensor_tensor(ctxn[:, tt].rearrange("p t (h d) -> p t h d", h=H), fix[:],
                                            rden[:, tt].unsqueeze(3).to_broadcast([128, 4, H, HD]), ALU.mult)
                    ins.then_inc(ctxn_made, 1)
                dve.wait_ge(*full(b, "wo"))
                ps = slots[slot_of["wo"]]
                dve.wait_ge(xb_made, b + 1)
                dve.wait_ge(out_done, b * 16)
                ins = dve.tensor_tensor(y[:].rearrange("p t d -> p (t d)"), ps[:],
                                        xb[:].rearrange("p t d -> p (t d)"), ALU.add)
                ins.then_inc(slot_free[slot_of["wo"]], 1)
                dve.wait_ge(*read_by(b, "wo"))
                ins = layernorm(b, 0, y, x1)
                ins.then_inc(x1_made, 1)
                for k in range(2):
                    dve.wait_ge(*read_by(b, f"h{k}"))
                link(dve.tensor_scalar(running[:], biasT[:, 0], hst[:, 0, D + 1:D + 2], None, ALU.add))
                for t in range(1, T):
                    ins = dve.scalar_tensor_tensor(out=running[:], in0=biasT[:, t], scalar=hst[:, t, D + 1:D + 2],
                                                   in1=running[:], op0=ALU.add, op1=ALU.max)
                    if t < T - 1:
                        link(ins)
                ins.then_inc(running_made, 1)
                dve.wait_ge(*full(b, "runT"))
                ps = slots[slot_of["runT"]]
                ins = dve.tensor_reduce(nbmax[:], ps[:].rearrange("p (t n) -> p t n", t=T), AX_X, ALU.max)
                ins.then_inc(slot_free[slot_of["runT"]], 1)
                dve.wait_ge(*read_by(b, "runT"))
                link(dve.tensor_tensor(nbmax[:], nbmax[:], hst[:, :, D], ALU.add))
                link(dve.scalar_tensor_tensor(out=shift[:], in0=nbmax[:], scalar=ALPHA, in1=nbmax[:],
                                              op0=ALU.mult, op1=ALU.max))
                dve.tensor_tensor(diag[:], ident[:].unsqueeze(1).to_broadcast([128, T, 128]),
                                  shift[:].unsqueeze(2).to_broadcast([128, T, 128]), ALU.mult).then_inc(diag_made, 1)
                link(dve.tensor_scalar(rden[:, :, 0], hst[:, :, D + 1], ALPHA, None, ALU.mult))
                for k in range(2):
                    dve.wait_ge(*read_by(b, f"row{k + 1}"))
                dve.wait_ge(units_used, (b + 1) * H * T)
                for t in range(T):
                    link(dve.tensor_scalar(weights[:, t], row1[:], hst[:, t, D + 1:D + 2], None, ALU.add))
                    ins = dve.scalar_tensor_tensor(out=weights[:, t], in0=row2[:], scalar=rden[:, t, 0:1],
                                                   in1=weights[:, t], op0=ALU.add, op1=ALU.max)
                    ins.then_inc(logits_made, 1)
                dve.wait_ge(*read_by(b, "hsum"))
                for k in range(2):
                    dve.wait_ge(*full(b, f"out{k}"))
                    ps = slots[slot_of[f"out{k}"]]
                    view = ps[:].rearrange("p (t w) -> p t w", w=256)
                    tt = slice(4 * k, 4 * k + 4)
                    dcol = view[:, :, D + 2]
                    link(dve.tensor_scalar(empty[:, tt, 0], dcol, 0.0, None, ALU.is_equal))
                    link(dve.scalar_tensor_tensor(out=den[:, tt, 0], in0=empty[:, tt, 0], scalar=float(N),
                                                  in1=dcol, op0=ALU.mult, op1=ALU.add))
                    link(dve.reciprocal(den[:, tt, 1], den[:, tt, 0]))
                    link(dve.tensor_tensor(empty[:, tt, 1], empty[:, tt, 0], den[:, tt, 1], ALU.mult))
                    for t in range(4):
                        u = 4 * k + t
                        ins = dve.scalar_tensor_tensor(out=y[:, u], in0=view[:, t, 0:D], scalar=den[:, u, 1:2],
                                                       in1=x1[:, u], op0=ALU.mult, op1=ALU.add)
                    ins.then_inc(slot_free[slot_of[f"out{k}"]], 1)
                    dve.wait_ge(*read_by(b, f"out{k}"))
                    for t in range(4):
                        u = 4 * k + t
                        ins = dve.scalar_tensor_tensor(out=y[:, u], in0=hsum[:, 0:D], scalar=empty[:, u, 1:2],
                                                       in1=y[:, u], op0=ALU.mult, op1=ALU.add)
                    link(ins)
                layernorm(b, 1, y, y).then_inc(y_out, 1)
                assert steps[0] == DVE_STEPS, steps[0]

            batch(0)
            with dve.Fori(1, B) as b:
                batch(b)
NEG_STEP = 4

_OUT = (8, 1024, 128)


def kernel(x, adj, L0_gnn_Wq, L0_gnn_Wk, L0_gnn_Wv, L0_gnn_Wo, L0_gnn_bo, L1_gnn_W, L1_gnn_a):
    import numpy as np
    import concourse.bacc as bacc
    from concourse.bass_utils import run_bass_kernel_spmd

    x, adj = np.asarray(x), np.asarray(adj)
    ins = {
        "x": x, "xT": np.ascontiguousarray(x.transpose(0, 2, 1)),
        "adj": adj, "adjT": np.ascontiguousarray(adj.transpose(0, 2, 1)),
        "Wq": np.asarray(L0_gnn_Wq), "Wk": np.asarray(L0_gnn_Wk), "Wv": np.asarray(L0_gnn_Wv),
        "Wo": np.asarray(L0_gnn_Wo), "bo": np.asarray(L0_gnn_bo), "W": np.asarray(L1_gnn_W),
        "a": np.asarray(L1_gnn_a),
    }
    nc = bacc.Bacc("TRN2", target_bir_lowering=False, num_devices=1)
    arrays, args = {}, []
    for name, v in ins.items():
        arrays[f"in_{name}"] = v
        args.append(nc.dram_tensor(f"in_{name}", v.shape, mybir.dt.from_np(v.dtype), kind="ExternalInput").ap())
    args.append(nc.dram_tensor("out_0", _OUT, F32, kind="ExternalOutput").ap())
    build(nc, *args)
    r = run_bass_kernel_spmd(nc, [arrays], core_ids=[0])
    return r.results[0]["out_0"]
```

```python
from contextlib import ExitStack

import concourse.bass as bass
from concourse import mybir

ALU = mybir.AluOpType
ACT = mybir.ActivationFunctionType
F32 = mybir.dt.float32
BF16 = mybir.dt.bfloat16
I32 = mybir.dt.int32
AX_X = mybir.AxisListType.X

BIG = 2.0 ** 30
FLOOR = -1.0e8
NEG_STEP = 4
EPS = 1e-5
ALPHA = 0.2
SHIFT_LIMIT = 120.0

KPART = (0, 0, 1, 1, 0, 2)
QPART = (0, 1, 0, 1, 2, 0)
BLOCKS = len(KPART)

STAGES = {
    "ctx0": "post", "ctx1": "post", "ctxT": "post", "wo": "post", "x1T": "post", "h0": "post",
    "h1": "post", "fbc": "post", "hsum": "post", "runT": "post", "mbc": "post",
    "out0": "post", "out1": "post", "out2": "post", "out3": "post",
    "v1": "own", "vsum": "own",
    "q": "prep", "k": "prep", "ck": "prep", "cq": "prep", "v0": "prep",
}
AFTER_QUAD = {
    1: ["ctx0"], 2: ["ctx1", "v1"], 3: ["ctxT", "vsum"], 4: ["wo"], 5: ["x1T"],
    6: ["h0", "h1", "fbc", "hsum"], 7: ["q"], 8: ["k"], 9: ["v0", "runT"], 10: ["mbc", "ck", "cq"],
    13: ["out0"], 14: ["out1", "out2"], 15: ["out3"],
}
PREP = ["q", "k", "ck", "cq", "v0"]
POST = [j for n in sorted(AFTER_QUAD) for j in AFTER_QUAD[n] if STAGES[j] == "post"]
OFFSET = {"post": -1, "own": 0, "prep": 1}
MASKED_BY = ["dpdp", "dpdp", "dpdp", "dpdp", "dpdp", "dpdp", "dpdp", "dpdp",
             "dpdp", "dpdp", "dpdp", "dpdp", "ddpd", "ddpd", "dpdp", "dpdp"]

RUN = (7, 7, 7, 7, 8, 8, 8, 9)
LOGITS = 9
SHIFT_BY = "pdpdpdpd"
SHIFT_LOGITS = (11, 11, 11, 11, 11, 12, 12, 12)
EXP_ATTS = (11, 11, 11, 12, 12, 12, 12, 13)
MASK_ATTS = (12, 12, 12, 12, 12, 13, 13, 13)
POW1 = 4
NORM1 = 5
LOOP_STEPS = 55


def ring_plan():
    def full_pass():
        jobs = []
        for n in range(16):
            units = [("unit", 0, 4 * n + i) for i in range(4)]
            others = [(j, OFFSET[STAGES[j]], 0) for j in AFTER_QUAD.get(n, [])]
            jobs += units + others if n < 15 else units[:1] + others + units[1:]
        return jobs
    slots = {j: n % 3 for n, j in enumerate(full_pass())}
    passes = {
        "prologue": [(j, 1, 0) for j in PREP],
        "first": [j for j in full_pass() if j[1] >= 0],
        "loop": full_pass(),
        "last": [j for j in full_pass() if j[1] <= 0],
        "epilogue": [(j, -1, 0) for j in POST],
    }
    before = {"prologue": None, "first": "prologue", "loop": "loop", "last": "loop", "epilogue": "last"}
    slot = {}
    for name, jobs in passes.items():
        for n, j in enumerate(jobs):
            slot[name, j] = n % 3 if name in ("prologue", "epilogue") else slots[j]
    holder = {}
    for name, jobs in passes.items():
        for n, j in enumerate(jobs):
            s = slot[name, j]
            here = [e for e in jobs[:n] if slot[name, e] == s]
            there = [e for e in passes[before[name]] if slot[before[name], e] == s] if before[name] else []
            if here:
                holder[name, j] = here[-1]
            elif there:
                holder[name, j] = (there[-1][0], there[-1][1] - 1, there[-1][2])
            else:
                holder[name, j] = None
    for s in range(3):
        ends = [[e for e in passes[p] if slot[p, e] == s][-1] for p in ("first", "loop")]
        assert ends[0] == ends[1], ends
    return slot, holder


def build_fast(nc, sems, needed, x, xT, adjT, Wq, Wk, Wv, Wo, bo, W, a, out):
    B, N, D = x.shape
    H = 8
    HD = D // H
    T = N // 128
    HALF = N // 2
    HG = 4
    NG = H // HG
    QUADS = NG * T
    UNITS = QUADS * HG
    QW = N // 4
    SCALE = 1.0 / float(HD) ** 0.5
    KROWS = BLOCKS * HD
    SROWS = KROWS + 1
    HW = D + 3
    VW = 32
    NORM_WEIGHT = 0.5078125
    STACK_DMAS = 2 * BLOCKS + 1
    RAW = 3
    slot, holder = ring_plan()

    with ExitStack() as ctx:
        def sb(name, shape, dt):
            return ctx.enter_context(nc.sbuf_tensor(name, shape, dt))

        def sem(name):
            return sems.enter_context(nc.semaphore(name))

        slots = [ctx.enter_context(nc.psum_tensor(f"slot{i}", [128, N], F32)) for i in range(3)]
        acc = ctx.enter_context(nc.psum_tensor("acc", [128, N], F32))

        ident = sb("ident", [128, 128], F32)
        identb = sb("identb", [128, 128], BF16)
        ones = sb("ones", [128, 128], F32)
        negonesb = sb("negonesb", [128, 128], BF16)
        headsum = sb("headsum", [128, H], BF16)
        wq = sb("wq", [D, D], F32)
        wk = sb("wk", [D, D], F32)
        wv = sb("wv", [D, D], F32)
        wo = sb("wo", [D, D], F32)
        w_of = sb("w_of", [D, D], F32)
        acol = sb("acol", [D, 2], F32)
        a1wide = sb("a1wide", [D, D], F32)
        wh = sb("wh", [D, D + 2], F32)
        u1wide = sb("u1wide", [D, D], F32)
        bo_all = sb("bo_all", [128, D], F32)
        exponent = sb("exponent", [128, T], F32)

        xT_sb = sb("xT_sb", [D, N], F32)
        raw = [sb(f"raw{i}", [128, N], I32) for i in range(RAW)]
        mask = sb("mask", [128, T, N], BF16)
        bias = sb("bias", [128, T, N], BF16)
        qst = sb("qst", [SROWS, H, N], BF16)
        kst = sb("kst", [SROWS, H, N], BF16)
        vst = sb("vst", [128, T, H, VW], F32)
        weights = sb("weights", [128, 8, N], F32)
        squares = [sb(f"{n}squares", [128, N], BF16) for n in "qk"]
        negshift = sb("negshift", [H, N], BF16)
        kmax = sb("kmax", [H, 1], F32)
        negkmax = sb("negkmax", [H, 1], F32)
        too_far = sb("too_far", [H, 1], I32)
        too_far_row = sb("too_far_row", [1, H], I32)
        carrier = sb("carrier", [128, 1], F32)
        worst_row = sb("worst_row", [H, 1], F32)
        worst = sb("worst", [H, 1], F32)
        xsum = sb("xsum", [D, 1], F32)
        xsum_wide = sb("xsum_wide", [D, 128], F32)
        vsum = sb("vsum", [128, D], F32)

        x_sb = sb("x_sb", [128, T, D], F32)
        ctxT = sb("ctxT", [128, NG, N], F32)
        fix = sb("fix", [128, 4, H, HD], F32)
        den = sb("den", [128, T, H], F32)
        empty = sb("empty", [128, T, H], F32)
        rden = sb("rden", [128, T, H], F32)
        y = sb("y", [128, T, D], F32)
        x1 = sb("x1", [128, T, D], F32)
        stats = sb("stats", [128, T, 6], F32)
        meanvar = sb("meanvar", [128, T, 2], F32)
        vareps = sb("vareps", [128, T], F32)
        rstd = sb("rstd", [128, T], F32)
        hst = sb("hst", [128, T, HW], F32)
        x1sum = sb("x1sum", [D, 1], F32)
        x1sum_wide = sb("x1sum_wide", [D, 128], F32)
        hsum = sb("hsum", [128, D + 2], F32)
        fj = [sb(f"fj_times_{n}", [128, T], F32) for n in ("rise", "alpha")]
        nbmax = sb("nbmax", [128, T], F32)
        shift = sb("shift", [128, T], F32)
        shiftb = [sb(f"shiftb{i}", [128, T], BF16) for i in range(2)]
        turn1 = sb("turn1", [128, N], F32)
        ctxn = turn1[:].rearrange("p (t d) -> p t d", t=T)
        x1T = turn1
        diag = turn1[:].bitcast(BF16).rearrange("p (i t n) -> p i t n", i=2, t=T)
        turn2 = sb("turn2", [128, N], F32)
        ctxnT = turn2
        f_all = turn2
        turn3 = sb("turn3", [128, N], F32)
        rest = turn3
        row_all = turn3
        running = y[:].rearrange("p t d -> p (t d)")
        atts = sb("atts", [128, 4, T, QW], F32)
        partmem = atts[:, 2:4].rearrange("p q t n -> p (q t n)").bitcast(BF16)
        parts = [[partmem[:, (3 * s + i) * N:(3 * s + i + 1) * N] for i in range(3)] for s in range(2)]

        scratch = nc.dram_tensor("parts_scratch", [2, 3, H, HD, N], BF16, kind="Internal").ap()
        flag_scratch = nc.dram_tensor("flag_scratch", [1, H], I32, kind="Internal").ap()
        shift_scratch = nc.dram_tensor("shift_scratch", [H, N], BF16, kind="Internal").ap()

        full = {j: sem(f"{j}_full") for j in ["unit", *STAGES]}
        taken = {j: sem(f"{j}_taken") for j in ["unit", *STAGES]}
        per = {j: UNITS if j == "unit" else 1 for j in full}

        def free_for(kind, b, job):
            was = holder[kind, job]
            if was is None:
                return taken["q"], 0
            return taken[was[0]], (b + was[1]) * per[was[0]] + was[2] + 1

        consts_in = sem("consts_in")
        consts_made = sem("consts_made")
        setup_mm = sem("setup_mm")
        setup_copied = sem("setup_copied")
        xT_in = sem("xT_in")
        x_in = sem("x_in")
        xb_made = sem("xb_made")
        raw_in = [sem(f"raw{i}_in") for i in range(RAW)]
        masks_made = sem("masks_made")
        parts_made = sem("parts_made")
        squares_made = sem("squares_made")
        parts_out = sem("parts_out")
        shift_out = sem("shift_out")
        part0_made = sem("part0_made")
        stack_in = [sem(f"stack{g}_in") for g in range(NG)]
        kmax_made = sem("kmax_made")
        xsum_made = sem("xsum_made")
        masked_dve = sem("masked_dve")
        masked_pool = sem("masked_pool")
        contexts_done = sem("contexts_done")
        acc_read = sem("acc_read")
        ctxn_made = sem("ctxn_made")
        vareps_made = sem("vareps_made")
        rstd_made = sem("rstd_made")
        x1_made = sem("x1_made")
        x1sum_made = sem("x1sum_made")
        running_made = sem("running_made")
        diag_made = sem("diag_made")
        logits_made = sem("logits_made")
        slopes_made = sem("slopes_made")
        shifted = {"p": sem("shifted_by_gpsimd"), "d": sem("shifted_by_vector")}
        atts_exp = sem("atts_exp")
        atts_made = sem("atts_made")
        y_made = sem("y_made")
        out_done = sem("out_done")
        too_far_made = sem("too_far_made")
        flags_out = sem("flags_out")
        flags_in = sem("flags_in")
        dve_step = sem("dve_step")
        pool_step = sem("pool_step")

        def shifted_for(b, j):
            e = SHIFT_BY[j]
            return shifted[e], b * SHIFT_BY.count(e) + SHIFT_BY[:j + 1].count(e)

        by = {e: sum(q.count(e) for q in MASKED_BY) for e in "dp"}

        def masked(e, n, i):
            return sum(q.count(e) for q in MASKED_BY[:n]) + MASKED_BY[n][:i + 1].count(e)

        block = ctx.enter_context(nc.Block())
        bo_row = bo.rearrange("(o d) -> o d", o=1)

        @block.sync
        def _(sp):
            def load_xT(b):
                sp.dma_start(xT_sb[:], xT[b]).then_inc(xT_in, 16)

            def load_x(b):
                sp.dma_start(x_sb[:], x[b].rearrange("(t p) d -> p t d", p=128)).then_inc(x_in, 16)

            def load_raw(b, t):
                sp.dma_start(raw[t % RAW][:], adjT[b, t * 128:(t + 1) * 128, :]).then_inc(raw_in[t % RAW], 16)

            def send_parts(b, s):
                sp.wait_ge(parts_made, 2 * b + s + 1)
                for i in range(3):
                    sp.dma_start(scratch[s, i].rearrange("h d n -> (h d) n"), parts[s][i]).then_inc(parts_out, 16)

            def send_shift(b):
                sp.wait_ge(parts_out, (b + 1) * 96)
                sp.wait_ge(taken["cq"], b + 1)
                sp.dma_start(shift_scratch, negshift[:]).then_inc(shift_out, 16)

            def load_stack(g):
                heads = slice(g * HG, (g + 1) * HG)
                for r in range(BLOCKS):
                    rows = slice(r * HD, (r + 1) * HD)
                    sp.dma_start(qst[rows, heads], scratch[0, QPART[r], heads].rearrange("h d n -> d h n")).then_inc(stack_in[g], 16)
                    sp.dma_start(kst[rows, heads], scratch[1, KPART[r], heads].rearrange("h d n -> d h n")).then_inc(stack_in[g], 16)
                sp.dma_start(qst[KROWS:SROWS, heads], shift_scratch[heads].rearrange("(o h) n -> o h n", o=1)).then_inc(stack_in[g], 16)

            load_xT(0)
            for dst, src in ((wq, Wq), (wk, Wk), (wv, Wv), (wo, Wo), (w_of, W),
                             (acol, a.rearrange("o (c d) -> d (o c)", c=2))):
                with nc.allow_non_contiguous_dma(reason="a is 256 numbers"):
                    sp.dma_start(dst[:], src).then_inc(consts_in, 16)
            sp.dma_start(bo_all[:], bo_row.to_broadcast([128, D])).then_inc(out_done, 16)
            for t in range(RAW):
                load_raw(0, t)
            for s in range(2):
                send_parts(0, s)
            send_shift(0)
            sp.wait_ge(shift_out, 16)
            load_stack(0)

            def batch(kind, b):
                sp.wait_ge(full["unit"], b * UNITS)
                load_stack(1)
                for t in range(RAW, T):
                    sp.wait_ge(masks_made, b * T + t - RAW + 1)
                    load_raw(b, t)
                if kind != "last":
                    sp.wait_ge(full["v1"], b + 1)
                    sp.wait_ge(xsum_made, b + 1)
                    load_xT(b + 1)
                    for t in range(RAW):
                        sp.wait_ge(masks_made, b * T + min(t + 7, T))
                        load_raw(b + 1, t)
                if kind != "first":
                    sp.wait_ge(taken["wo"], b)
                load_x(b)
                if kind != "last":
                    sp.wait_ge(stack_in[1], (b + 1) * 16 * STACK_DMAS)
                    for s in range(2):
                        send_parts(b + 1, s)
                    send_shift(b + 1)
                    sp.wait_ge(shift_out, (b + 2) * 16)
                    load_stack(0)
                if kind != "first":
                    store(b - 1)

            def store(b):
                sp.wait_ge(y_made, b + 1)
                sp.dma_start(out[b].rearrange("(t p) d -> p t d", p=128), y[:]).then_inc(out_done, 16)

            batch("first", 0)
            with sp.Fori(1, B - 1) as b:
                batch("loop", b)
            batch("last", B - 1)
            sp.wait_ge(too_far_made, 1)
            sp.dma_start(flag_scratch.rearrange("o h -> h o"), too_far[:]).then_inc(flags_out, 16)
            sp.wait_ge(flags_out, 16)
            sp.dma_start(too_far_row[:], flag_scratch).then_inc(flags_in, 16)
            store(B - 1)
            sp.wait_ge(out_done, 16 * (B + 1))

        @block.tensor
        def _(pe):
            kw = dict(start=True, stop=True)

            def context(b, n):
                g, t = divmod(n, T)
                for e, done in (("d", masked_dve), ("p", masked_pool)):
                    if e in MASKED_BY[n]:
                        pe.wait_ge(done, b * by[e] + masked(e, n, HG - 1))
                if t == 0:
                    pe.wait_ge(acc_read, b * NG + g)
                    pe.wait_ge(taken[f"v{g}"], b + 1)
                for c in range(2):
                    cols = slice(c * HALF, (c + 1) * HALF)
                    for i in range(HG):
                        mm = pe.matmul(acc[VW * i:VW * (i + 1), cols], vst[:, t, g * HG + i],
                                       weights[:, (HG * n + i) % 8, cols], start=(t == 0), stop=(t == T - 1))
                mm.then_inc(contexts_done, 1)

            def unit(kind, b, n, i):
                g, t = divmod(n, T)
                h = g * HG + i
                job = ("unit", 0, HG * n + i)
                ps = slots[slot[kind, job]]
                pe.wait_ge(*free_for(kind, b, job))
                for c in range(2):
                    cols = slice(c * HALF, (c + 1) * HALF)
                    mm = pe.matmul(ps[:, cols], kst[:, h, t * 128:(t + 1) * 128], qst[:, h, cols], **kw)
                mm.then_inc(full["unit"], 1)

            def job(kind, b, name):
                off = {"prologue": 1, "epilogue": -1}.get(kind, OFFSET[STAGES[name]])
                me = b + off
                ps = slots[slot[kind, (name, off, 0)]]
                pe.wait_ge(*free_for(kind, b, (name, off, 0)))
                if name in ("q", "k"):
                    if name == "q":
                        pe.wait_ge(xT_in, (me + 1) * 16)
                    for c in range(2):
                        cols = slice(c * HALF, (c + 1) * HALF)
                        mm = pe.matmul(ps[:, cols], (wq if name == "q" else wk)[:], xT_sb[:, cols], **kw)
                elif name in ("cq", "ck"):
                    s = 0 if name == "cq" else 1
                    pe.wait_ge(squares_made, 2 * me + s + 1)
                    for c in range(2):
                        cols = slice(c * HALF, (c + 1) * HALF)
                        mm = pe.matmul(ps[0:H, cols], headsum[:], squares[s][:, cols], **kw)
                elif name in ("v0", "v1"):
                    half = slice(int(name[1]) * 64, int(name[1]) * 64 + 64)
                    for t in range(T):
                        mm = pe.matmul(ps[:, t * 64:(t + 1) * 64], xT_sb[:, t * 128:(t + 1) * 128], wv[:, half], **kw)
                elif name == "vsum":
                    pe.wait_ge(xsum_made, me + 1)
                    mm = pe.matmul(ps[:, 0:D], xsum_wide[:], wv[:], **kw)
                elif name in ("ctx0", "ctx1"):
                    pe.wait_ge(acc_read, me * NG + NG)
                    for t in range(4):
                        for g in range(NG):
                            u = 4 * int(name[3]) + t
                            mm = pe.transpose(ps[:, (t * NG + g) * 128:(t * NG + g + 1) * 128],
                                              ctxT[:, g, u * 128:(u + 1) * 128], ident[:])
                elif name == "ctxT":
                    pe.wait_ge(ctxn_made, 2 * me + 2)
                    for t in range(T):
                        mm = pe.transpose(ps[:, t * 128:(t + 1) * 128], ctxn[:, t], ident[:])
                elif name == "wo":
                    pe.wait_ge(taken["ctxT"], me + 1)
                    for t in range(T):
                        mm = pe.matmul(ps[:, t * 128:(t + 1) * 128], ctxnT[:, t * 128:(t + 1) * 128], wo[:], **kw)
                elif name == "x1T":
                    pe.wait_ge(x1_made, me + 1)
                    for t in range(T):
                        mm = pe.transpose(ps[:, t * 128:(t + 1) * 128], x1[:, t], ident[:])
                elif name in ("h0", "h1"):
                    pe.wait_ge(taken["x1T"], me + 1)
                    for t in range(4):
                        u = 4 * int(name[1]) + t
                        mm = pe.matmul(ps[:, t * 256:t * 256 + D + 2], x1T[:, u * 128:(u + 1) * 128], wh[:], **kw)
                elif name == "fbc":
                    for c in range(2):
                        cols = slice(c * HALF, (c + 1) * HALF)
                        mm = pe.matmul(ps[:, cols], u1wide[:], x1T[:, cols], **kw)
                elif name == "hsum":
                    pe.wait_ge(x1sum_made, me + 1)
                    mm = pe.matmul(ps[:, 0:D + 2], x1sum_wide[:], wh[:], **kw)
                elif name == "runT":
                    pe.wait_ge(running_made, me + 1)
                    for t in range(T):
                        mm = pe.transpose(ps[:, t * 128:(t + 1) * 128], running[:, t * 128:(t + 1) * 128], ident[:])
                elif name == "mbc":
                    pe.wait_ge(diag_made, me + 1)
                    for c in range(2):
                        for i in range(2):
                            mm = pe.matmul(ps[:, c * HALF:(c + 1) * HALF], negonesb[:],
                                           diag[:, i, 4 * c:4 * c + 4].rearrange("p t n -> p (t n)"),
                                           start=(i == 0), stop=(i == 1))
                else:
                    k = int(name[3])
                    pe.wait_ge(atts_made, me * T + T)
                    for t in range(2):
                        for j in range(T):
                            mm = pe.matmul(ps[:, t * HALF:t * HALF + HW], atts[:, k, j, t * 128:(t + 1) * 128],
                                           hst[:, j], start=(j == 0), stop=(j == T - 1))
                mm.then_inc(full[name], 1)

            pe.wait_ge(consts_in, 96)
            pe.wait_ge(consts_made, 2)
            pe.transpose(acc[:, 0:D], w_of[:], ident[:])
            pe.matmul(acc[:, D:D + 2], w_of[:], acol[:], **kw)
            pe.matmul(acc[:, 256:256 + D], w_of[:], a1wide[:], **kw).then_inc(setup_mm, 1)
            for name in PREP:
                job("prologue", -1, name)
            pe.wait_ge(setup_copied, 1)

            def batch(kind, b):
                for n in range(QUADS):
                    if n % T == 0:
                        pe.wait_ge(stack_in[n // T], (b + 1) * 16 * STACK_DMAS)
                    others = [j for j in AFTER_QUAD.get(n, [])
                              if not (kind == "first" and STAGES[j] == "post")
                              and not (kind == "last" and STAGES[j] == "prep")]
                    for i in range(HG):
                        unit(kind, b, n, i)
                        if n == QUADS - 1 and i == 0:
                            context(b, n - 1)
                            for name in others:
                                job(kind, b, name)
                    if n < QUADS - 1:
                        if n:
                            context(b, n - 1)
                        elif kind != "first":
                            context(b - 1, QUADS - 1)
                        for name in others:
                            job(kind, b, name)

            batch("first", 0)
            with pe.Fori(1, B - 1) as b:
                batch("loop", b)
            batch("last", B - 1)
            context(B - 1, QUADS - 1)
            for name in POST:
                job("epilogue", B, name)

        @block.scalar
        def _(act):
            def job(kind, b, name):
                off = {"prologue": 1, "epilogue": -1}.get(kind, OFFSET[STAGES[name]])
                me = b + off
                ps = slots[slot[kind, (name, off, 0)]]
                if name in ("ctx0", "ctx1", "ck", "runT", "wo", "mbc") or name[:3] == "out":
                    return
                act.wait_ge(full[name], me + 1)
                if name in ("q", "k"):
                    s = 0 if name == "q" else 1
                    act.activation(parts[s][0], ps[:], ACT.Copy).then_inc(part0_made, 1)
                    return
                if name == "cq":
                    act.wait_ge(kmax_made, me + 1)
                    act.wait_ge(shift_out, me * 16)
                    ins = act.activation(negshift[:], ps[0:H], ACT.Identity, bias=negkmax[:], scale=-1.0)
                elif name in ("v0", "v1"):
                    g = int(name[1])
                    if kind != "prologue":
                        act.wait_ge(contexts_done, me * QUADS + (g + 1) * T - QUADS)
                    ins = act.activation(vst[:, :, g * HG:(g + 1) * HG, 0:HD],
                                         ps[:, 0:HALF].rearrange("p (t h d) -> p t h d", t=T, h=HG), ACT.Copy)
                elif name == "vsum":
                    act.wait_ge(ctxn_made, me * 2)
                    ins = act.activation(vsum[:], ps[:, 0:D], ACT.Copy)
                elif name == "ctxT":
                    ins = act.activation(ctxnT[:], ps[:], ACT.Copy)
                elif name == "x1T":
                    ins = act.activation(x1T[:], ps[:], ACT.Copy)
                elif name in ("h0", "h1"):
                    k = int(name[1])
                    view = ps[:].rearrange("p (t w) -> p t w", w=256)[:, :, 0:D + 2]
                    ins = act.activation(hst[:, 4 * k:4 * k + 4, 0:D + 2], view, ACT.Copy)
                elif name == "fbc":
                    ins = act.activation(f_all[:], ps[:], ACT.Copy)
                elif name == "hsum":
                    ins = act.activation(hsum[:], ps[:, 0:D + 2], ACT.Copy)
                ins.then_inc(taken[name], 1)

            def logits(b):
                act.wait_ge(taken["fbc"], b + 1)
                act.wait_ge(slopes_made, b + 1)
                act.wait_ge(parts_out, min_parts(b) * 96)
                for j in range(T):
                    act.activation(atts[:, :, j, :], f_all[:].rearrange("p (q n) -> p q n", q=4), ACT.Relu,
                                   bias=fj[0][:, j:j + 1], scale=1.0 - ALPHA).then_inc(logits_made, 1)

            def min_parts(b):
                return b + 3 if not (isinstance(b, int) and b + 3 > B) else B

            def exp_atts(b, j):
                act.wait_ge(*shifted_for(b, j))
                act.activation(atts[:, :, j, :], atts[:, :, j, :], ACT.Exp,
                               bias=fj[1][:, j:j + 1]).then_inc(atts_exp, 1)

            act.wait_ge(setup_mm, 1)
            act.activation(wh[:], acc[:, 0:D + 2], ACT.Copy)
            act.activation(u1wide[:], acc[:, 256:256 + D], ACT.Copy).then_inc(setup_copied, 1)
            for name in PREP:
                job("prologue", -1, name)

            def batch(kind, b):
                for n in range(QUADS):
                    for i in range(HG):
                        u = HG * n + i
                        act.wait_ge(full["unit"], b * UNITS + u + 1)
                        if i == 0 and (kind != "first" or n >= 2):
                            act.wait_ge(contexts_done, b * QUADS + n - 1)
                        act.activation(weights[:, u % 8], slots[slot[kind, ("unit", 0, u)]][:], ACT.Exp,
                                       scale=SCALE).then_inc(taken["unit"], 1)
                        if n < QUADS - 1 and i < HG - 1:
                            continue
                        if n == QUADS - 1 and i:
                            continue
                        for name in AFTER_QUAD.get(n, []):
                            if kind == "first" and STAGES[name] == "post" or kind == "last" and STAGES[name] == "prep":
                                continue
                            job(kind, b, name)
                        if kind != "first":
                            if n == LOGITS:
                                logits(b - 1)
                            for k in range(T):
                                if n == EXP_ATTS[k]:
                                    exp_atts(b - 1, k)

            batch("first", 0)
            with act.Fori(1, B - 1) as b:
                batch("loop", b)
            batch("last", B - 1)
            for name in POST:
                job("epilogue", B, name)
                if name == "hsum":
                    logits(B - 1)
                if name == "mbc":
                    for k in range(T):
                        exp_atts(B - 1, k)

        @block.gpsimd
        def _(pool):
            pool.memset(ones[:], 1.0)
            pool.memset(exponent[:], -0.5)
            pool.memset(headsum[:], NORM_WEIGHT).then_inc(pool_step, 1)
            pool.wait_ge(pool_step, 1)
            pool.affine_select(out=ident[:], in_=ones[:], compare_op=ALU.is_equal, fill=0.0, base=0,
                               pattern=[[-1, 128]], channel_multiplier=1).then_inc(pool_step, 1)
            pool.wait_ge(pool_step, 2)
            pool.affine_select(out=headsum[:], in_=headsum[:], compare_op=ALU.is_ge, fill=0.0, base=0,
                               pattern=[[-HD, H]], channel_multiplier=1).then_inc(pool_step, 1)
            pool.wait_ge(pool_step, 3)
            pool.affine_select(out=headsum[:], in_=headsum[:], compare_op=ALU.is_ge, fill=0.0, base=HD - 1,
                               pattern=[[HD, H]], channel_multiplier=-1).then_inc(pool_step, 1)
            pool.wait_ge(pool_step, 4)
            pool.tensor_copy(identb[:], ident[:]).then_inc(consts_made, 1)

            def residual(b):
                pool.wait_ge(x_in, (b + 1) * 16)
                pool.tensor_tensor(x_sb[:], x_sb[:], bo_all[:].unsqueeze(1).to_broadcast([128, T, D]),
                                   ALU.add).then_inc(xb_made, 1)

            def inverse_root(b, k):
                pool.wait_ge(vareps_made, 2 * b + k + 1)
                pool.tensor_tensor(rstd[:], vareps[:], exponent[:], ALU.pow).then_inc(rstd_made, 1)

            def shift_logits(b, j):
                if SHIFT_BY[j] != "p":
                    return
                pool.wait_ge(logits_made, b * T + j + 1)
                pool.wait_ge(taken["mbc"], b + 1)
                pool.tensor_tensor(atts[:, :, j, :], atts[:, :, j, :], row_all[:].rearrange("p (q n) -> p q n", q=4),
                                   ALU.add).then_inc(shifted["p"], 1)

            def others(kind, b, n):
                if kind != "first":
                    if n == POW1:
                        inverse_root(b - 1, 0)
                    for j in range(T):
                        if n == SHIFT_LOGITS[j]:
                            shift_logits(b - 1, j)
                if n == 14:
                    residual(b)

            pool.wait_ge(out_done, 16)

            def batch(kind, b):
                for n in range(QUADS):
                    t = n % T
                    for i in range(HG):
                        if MASKED_BY[n][i] == "p":
                            u = (HG * n + i) % 8
                            pool.wait_ge(masks_made, b * T + t + 1)
                            pool.wait_ge(taken["unit"], b * UNITS + HG * n + i + 1)
                            pool.tensor_tensor(weights[:, u], weights[:, u], mask[:, t],
                                               ALU.mult).then_inc(masked_pool, 1)
                        if i == (HG - 1 if n < QUADS - 1 else 0):
                            others(kind, b, n)
                if kind != "first":
                    inverse_root(b - 1, 1)

            batch("first", 0)
            with pool.Fori(1, B - 1) as b:
                batch("loop", b)
            batch("last", B - 1)
            inverse_root(B - 1, 0)
            for j in range(T):
                shift_logits(B - 1, j)
            inverse_root(B - 1, 1)

        @block.vector
        def _(dve):
            chain = {"n": 0, "base": 0}

            def link(ins):
                chain["n"] += 1
                ins.then_inc(dve_step, 1)
                dve.wait_ge(dve_step, chain["base"] + chain["n"])

            def make_bias(t):
                link(dve.tensor_scalar(bias[:, t], mask[:, t], 1.0, BIG, ALU.subtract, ALU.mult))

            def make_mask(b, t):
                if not isinstance(b, int) or b:
                    make_bias(t)
                m = t % RAW
                count = (T - m + RAW - 1) // RAW
                dve.wait_ge(raw_in[m], (b * count + t // RAW + 1) * 16)
                dve.tensor_scalar(mask[:, t], raw[m][:], 0, None, ALU.is_gt).then_inc(masks_made, 1)

            def split(b, s, ps):
                name = "qk"[s]
                dve.wait_ge(part0_made, 2 * b + s + 1)
                dve.wait_ge(parts_made, 2 * b + s)
                dve.tensor_tensor(rest[:], ps[:], parts[s][0], ALU.subtract).then_inc(taken[name], 1)
                dve.tensor_tensor(squares[s][:], parts[s][0], parts[s][0], ALU.mult).then_inc(squares_made, 1)
                dve.wait_ge(taken[name], b + 1)
                link(dve.tensor_copy(parts[s][1], rest[:]))
                dve.tensor_tensor(parts[s][2], rest[:], parts[s][1], ALU.subtract).then_inc(parts_made, 1)

            def divide_contexts(b, k, ps):
                view = ps[:].rearrange("p (t h d) -> p t h d", t=4, h=H)
                tt = slice(4 * k, 4 * k + 4)
                name = f"ctx{k}"
                link(dve.tensor_scalar(empty[:, tt], view[:, :, :, HD], 0.0, None, ALU.is_equal))
                link(dve.scalar_tensor_tensor(out=den[:, tt], in0=empty[:, tt], scalar=float(N),
                                              in1=view[:, :, :, HD], op0=ALU.mult, op1=ALU.add))
                dve.reciprocal(rden[:, tt], den[:, tt])
                dve.wait_ge(taken["vsum"], b + 1)
                link(dve.tensor_tensor(fix[:], empty[:, tt].unsqueeze(3).to_broadcast([128, 4, H, HD]),
                                       vsum[:].rearrange("p (h d) -> p h d", h=H).unsqueeze(1).to_broadcast([128, 4, H, HD]),
                                       ALU.mult))
                dve.tensor_tensor(fix[:], view[:, :, :, 0:HD], fix[:], ALU.add).then_inc(taken[name], 1)
                dve.wait_ge(taken[name], b + 1)
                dve.tensor_tensor(ctxn[:, tt].rearrange("p t (h d) -> p t h d", h=H), fix[:],
                                  rden[:, tt].unsqueeze(3).to_broadcast([128, 4, H, HD]), ALU.mult).then_inc(ctxn_made, 1)
                dve.wait_ge(ctxn_made, 2 * b + k + 1)

            def norm_stats(src):
                for t in range(T):
                    ins = dve.bn_stats(stats[:, t], src[:, t])
                link(ins)
                dve.memset(carrier[:], 0.0)
                for t in range(T):
                    ins = dve.bn_aggr(meanvar[:, t], stats[:, t])
                link(ins)
                dve.tensor_scalar(vareps[:], meanvar[:, :, 1], EPS, None, ALU.add).then_inc(vareps_made, 1)

            def normalise(b, k, src, dst, done):
                dve.wait_ge(rstd_made, 2 * b + k + 1)
                for t in range(T):
                    ins = dve.tensor_scalar(dst[:, t], src[:, t], meanvar[:, t, 0:1], rstd[:, t:t + 1],
                                            ALU.subtract, ALU.mult)
                ins.then_inc(done, 1)

            def run_max(b, t):
                if t == 0:
                    dve.wait_ge(taken["h1"], b + 1)
                    link(dve.tensor_scalar(running, bias[:, 0], hst[:, 0, D + 1:D + 2], None, ALU.add))
                    return
                ins = dve.scalar_tensor_tensor(out=running, in0=bias[:, t], scalar=hst[:, t, D + 1:D + 2],
                                               in1=running, op0=ALU.add, op1=ALU.max)
                if t == T - 1:
                    ins.then_inc(running_made, 1)
                else:
                    link(ins)

            def shift_logits(b, j):
                if SHIFT_BY[j] != "d":
                    return
                dve.wait_ge(logits_made, b * T + j + 1)
                dve.wait_ge(taken["mbc"], b + 1)
                dve.tensor_tensor(atts[:, :, j, :], atts[:, :, j, :], row_all[:].rearrange("p (q n) -> p q n", q=4),
                                  ALU.add).then_inc(shifted["d"], 1)

            def mask_atts(b, j):
                dve.wait_ge(atts_exp, b * T + j + 1)
                dve.scalar_tensor_tensor(out=atts[:, :, j, :], in0=bias[:, j].rearrange("p (q n) -> p q n", q=4),
                                         scalar=BIG, in1=atts[:, :, j, :], op0=ALU.add,
                                         op1=ALU.min).then_inc(atts_made, 1)

            def read_acc(b, g):
                dve.wait_ge(contexts_done, b * QUADS + (g + 1) * T)
                dve.tensor_copy(ctxT[:, g], acc[:]).then_inc(acc_read, 1)

            def job(kind, b, name):
                off = {"prologue": 1, "epilogue": -1}.get(kind, OFFSET[STAGES[name]])
                me = b + off
                ps = slots[slot[kind, (name, off, 0)]]
                if name in ("q", "k", "ctx0", "ctx1", "wo", "ck", "cq", "runT", "mbc") or name[:3] == "out":
                    if name != "cq":
                        dve.wait_ge(full[name], me + 1)
                if name in ("q", "k"):
                    split(me, 0 if name == "q" else 1, ps)
                elif name == "ck":
                    dve.tensor_reduce(kmax[:], ps[0:H], AX_X, ALU.max).then_inc(taken["ck"], 1)
                    dve.wait_ge(taken["ck"], me + 1)
                    dve.tensor_scalar(negkmax[:], kmax[:], -1.0, None, ALU.mult).then_inc(kmax_made, 1)
                elif name == "cq":
                    dve.wait_ge(taken["cq"], me + 1)
                    link(dve.tensor_reduce(worst_row[:], negshift[:], AX_X, ALU.min))
                    link(dve.tensor_tensor(worst[:], worst[:], worst_row[:], ALU.min))
                elif name in ("ctx0", "ctx1"):
                    divide_contexts(me, int(name[3]), ps)
                elif name == "mbc":
                    dve.wait_ge(taken["fbc"], me + 1)
                    dve.scalar_tensor_tensor(out=row_all[:], in0=f_all[:], scalar=ALPHA, in1=ps[:],
                                             op0=ALU.mult, op1=ALU.add).then_inc(taken["mbc"], 1)
                elif name == "hsum":
                    dve.wait_ge(taken["h1"], me + 1)
                    for i, scale in enumerate((1.0 - ALPHA, ALPHA)):
                        ins = dve.tensor_scalar(fj[i][:], hst[:, :, D + 1], scale, None, ALU.mult)
                    ins.then_inc(slopes_made, 1)
                elif name == "wo":
                    dve.wait_ge(xb_made, me + 1)
                    dve.wait_ge(out_done, (me + 1) * 16)
                    dve.tensor_tensor(y[:].rearrange("p t d -> p (t d)"), ps[:],
                                      x_sb[:].rearrange("p t d -> p (t d)"), ALU.add).then_inc(taken["wo"], 1)
                    dve.wait_ge(taken["wo"], me + 1)
                    norm_stats(y)
                elif name == "x1T":
                    dve.wait_ge(taken["x1T"], me + 1)
                    link(dve.tensor_reduce(x1sum[:], x1T[:], AX_X, ALU.add))
                    dve.tensor_copy(x1sum_wide[:], x1sum[:].to_broadcast([D, 128])).then_inc(x1sum_made, 1)
                elif name == "runT":
                    dve.tensor_reduce(nbmax[:], ps[:].rearrange("p (t n) -> p t n", t=T), AX_X,
                                      ALU.max).then_inc(taken["runT"], 1)
                    dve.wait_ge(taken["runT"], me + 1)
                    link(dve.tensor_tensor(nbmax[:], nbmax[:], hst[:, :, D], ALU.add))
                    link(dve.scalar_tensor_tensor(out=shift[:], in0=nbmax[:], scalar=ALPHA, in1=nbmax[:],
                                                  op0=ALU.mult, op1=ALU.max))
                    link(dve.tensor_copy(shiftb[0][:], shift[:]))
                    link(dve.tensor_tensor(shiftb[1][:], shift[:], shiftb[0][:], ALU.subtract))
                    for i in range(2):
                        ins = dve.tensor_tensor(diag[:, i], identb[:].unsqueeze(1).to_broadcast([128, T, 128]),
                                                shiftb[i][:].unsqueeze(2).to_broadcast([128, T, 128]), ALU.mult)
                    ins.then_inc(diag_made, 1)
                elif name[:3] == "out":
                    k = int(name[3])
                    view = ps[:].rearrange("p (t w) -> p t w", t=2)
                    tt = slice(2 * k, 2 * k + 2)
                    dcol = view[:, :, D + 2]
                    link(dve.tensor_scalar(empty[:, tt, 0], dcol, 0.0, None, ALU.is_equal))
                    link(dve.scalar_tensor_tensor(out=den[:, tt, 0], in0=empty[:, tt, 0], scalar=float(N),
                                                  in1=dcol, op0=ALU.mult, op1=ALU.add))
                    link(dve.reciprocal(den[:, tt, 1], den[:, tt, 0]))
                    link(dve.tensor_tensor(empty[:, tt, 1], empty[:, tt, 0], den[:, tt, 1], ALU.mult))
                    for t in range(2):
                        u = 2 * k + t
                        ins = dve.scalar_tensor_tensor(out=y[:, u], in0=view[:, t, 0:D], scalar=den[:, u, 1:2],
                                                       in1=x1[:, u], op0=ALU.mult, op1=ALU.add)
                    ins.then_inc(taken[name], 1)
                    dve.wait_ge(taken[name], me + 1)
                    dve.wait_ge(taken["hsum"], me + 1)
                    for t in range(2):
                        u = 2 * k + t
                        ins = dve.scalar_tensor_tensor(out=y[:, u], in0=hsum[:, 0:D], scalar=empty[:, u, 1:2],
                                                       in1=y[:, u], op0=ALU.mult, op1=ALU.add)
                    link(ins)

            dve.wait_ge(consts_in, 96)
            dve.memset(negonesb[:], -1.0)
            dve.memset(worst[:], 0.0)
            dve.memset(kst[KROWS:SROWS], 1.0)
            dve.memset(hst[:, :, D + 2:HW], 1.0)
            link(dve.memset(vst[:, :, :, HD:VW], 0.0))
            dve.memset(vst[:, :, :, HD:HD + 1], 1.0)
            dve.tensor_copy(a1wide[:], acol[:, 0:1].to_broadcast([D, D])).then_inc(consts_made, 1)
            for name in PREP:
                job("prologue", -1, name)

            def others(kind, b, n):
                if n < T - 1:
                    make_mask(b, n + 1)
                if n == 1:
                    dve.wait_ge(xT_in, (b + 1) * 16)
                    link(dve.tensor_reduce(xsum[:], xT_sb[:], AX_X, ALU.add))
                    dve.tensor_copy(xsum_wide[:], xsum[:].to_broadcast([D, 128])).then_inc(xsum_made, 1)
                if kind != "first":
                    if n == NORM1:
                        normalise(b - 1, 0, y, x1, x1_made)
                    for m in range(T):
                        if n == RUN[m]:
                            run_max(b - 1, m)
                    for j in range(T):
                        if n == SHIFT_LOGITS[j]:
                            shift_logits(b - 1, j)
                    for j in range(T):
                        if n == MASK_ATTS[j]:
                            mask_atts(b - 1, j)
                for name in AFTER_QUAD.get(n, []):
                    if kind == "first" and STAGES[name] == "post" or kind == "last" and STAGES[name] == "prep":
                        continue
                    job(kind, b, name)

            def batch(kind, b):
                for n in range(QUADS):
                    t = n % T
                    if n == 0:
                        make_mask(b, 0)
                    if n == 1 and kind != "first":
                        read_acc(b - 1, 1)
                    if n == 9:
                        read_acc(b, 0)
                    for i in range(HG):
                        if MASKED_BY[n][i] == "d":
                            u = (HG * n + i) % 8
                            dve.wait_ge(masks_made, b * T + t + 1)
                            dve.wait_ge(taken["unit"], b * UNITS + HG * n + i + 1)
                            dve.tensor_tensor(weights[:, u], weights[:, u], mask[:, t],
                                              ALU.mult).then_inc(masked_dve, 1)
                        if i == (HG - 1 if n < QUADS - 1 else 0):
                            others(kind, b, n)
                if kind != "first":
                    norm_stats(y)
                    normalise(b - 1, 1, y, y, y_made)

            batch("first", 0)
            first_steps = chain["n"]
            chain["n"] = 0
            with dve.Fori(1, B - 1) as b:
                chain["base"] = first_steps - LOOP_STEPS + b * LOOP_STEPS
                batch("loop", b)
                assert chain["n"] == LOOP_STEPS, chain["n"]
            chain["base"] = first_steps + (B - 2) * LOOP_STEPS
            chain["n"] = 0
            batch("last", B - 1)
            dve.tensor_scalar(too_far[:], worst[:], -SHIFT_LIMIT, None, ALU.is_lt).then_inc(too_far_made, 1)
            for t in range(T):
                make_bias(t)
            read_acc(B - 1, 1)
            dve.wait_ge(flags_in, 16)
            link(dve.tensor_reduce(needed[:], too_far_row[:], AX_X, ALU.max))
            for name in POST:
                job("epilogue", B, name)
                if name == "wo":
                    normalise(B - 1, 0, y, x1, x1_made)
                if name == "hsum":
                    for t in range(T):
                        run_max(B - 1, t)
                if name == "mbc":
                    for j in range(T):
                        shift_logits(B - 1, j)
                    for j in range(T):
                        mask_atts(B - 1, j)
            norm_stats(y)
            normalise(B - 1, 1, y, y, y_made)


def build_exact(nc, sems, needed, x, xT, adj, adjT, Wq, Wk, Wv, Wo, bo, W, a, out):
    B, N, D = x.shape
    H = 8
    HD = D // H
    T = N // 128
    HALF = N // 2
    CH = T // 2
    HG = 4
    NG = H // HG
    SCALE = 1.0 / float(HD) ** 0.5
    KROWS = BLOCKS * HD
    SROWS = KROWS + 3
    HW = D + 3
    VW = 32

    with ExitStack() as ctx:
        def sb(name, shape, dt):
            return ctx.enter_context(nc.sbuf_tensor(f"exact_{name}", shape, dt))

        def sem(name):
            return sems.enter_context(nc.semaphore(f"exact_{name}"))

        slots = [ctx.enter_context(nc.psum_tensor(f"exact_slot{i}", [128, N], F32)) for i in range(3)]
        acc = ctx.enter_context(nc.psum_tensor("exact_acc", [128, N], F32))

        ident = sb("ident", [128, 128], F32)
        identb = sb("identb", [128, 128], BF16)
        ones = sb("ones", [128, 128], F32)
        negones = sb("negones", [128, 128], F32)
        wq = sb("wq", [D, D], F32)
        wk = sb("wk", [D, D], F32)
        wv = sb("wv", [D, D], F32)
        wo = sb("wo", [D, D], F32)
        w_of = sb("w_of", [D, D], F32)
        acol = sb("acol", [D, 2], F32)
        a1wide = sb("a1wide", [D, D], F32)
        wh = sb("wh", [D, D + 2], F32)
        u1wide = sb("u1wide", [D, 2, D], F32)
        bo_all = sb("bo_all", [128, D], F32)
        exponent = sb("exponent", [128, T], F32)

        carrier = sb("carrier", [128, H * T + 2], F32)

        xT_sb = sb("xT_sb", [D, N], F32)
        x_sb = sb("x_sb", [128, T, D], F32)
        xb = sb("xb", [128, T, D], F32)
        raw = [sb(f"raw{i}", [128, 2, N], I32) for i in range(2)]
        biasT = sb("biasT", [128, T, N], BF16)
        biasN = sb("biasN", [128, T, N], BF16)
        rest = sb("rest", [128, N], F32)
        parts = [[sb(f"{n}part{i}", [128, N], BF16) for i in range(3)] for n in "qk"]
        qst = sb("qst", [SROWS, H, N], BF16)
        kst = sb("kst", [SROWS, H, N], BF16)
        vst = sb("vst", [128, T, H, VW], F32)
        vsum = sb("vsum", [128, H, VW], F32)
        rowmax = sb("rowmax", [128, H * T], F32)
        negmax = sb("negmax", [128, H * T], F32)
        negrest = sb("negrest", [H * T, 128], F32)
        negparts = [sb(f"negpart{i}", [H * T, 128], BF16) for i in range(3)]
        weights = sb("weights", [128, T, N], F32)
        ctxT = sb("ctxT", [128, NG, N], F32)
        ctxn = sb("ctxn", [128, T, D], F32)
        fix = sb("fix", [128, 4, H, HD], F32)
        den = sb("den", [128, T, H], F32)
        empty = sb("empty", [128, T, H], F32)
        rden = sb("rden", [128, T, H], F32)
        ctxnT = sb("ctxnT", [D, N], F32)
        y = sb("y", [128, T, D], F32)
        x1 = sb("x1", [128, T, D], F32)
        x1T = sb("x1T", [D, N], F32)
        stats = sb("stats", [128, T, 6], F32)
        meanvar = sb("meanvar", [128, T, 2], F32)
        vareps = sb("vareps", [128, T], F32)
        rstd = sb("rstd", [128, T], F32)
        hst = sb("hst", [128, T, HW], F32)
        hsum = sb("hsum", [128, HW], F32)
        running = sb("running", [128, N], F32)
        nbmax = sb("nbmax", [128, T], F32)
        shift = sb("shift", [128, T], F32)
        diag = sb("diag", [128, T, 128], F32)
        row1 = rest
        row2 = sb("row2", [128, N], F32)

        scratch = nc.dram_tensor("exact_parts_scratch", [2, 3, H, HD, N], BF16, kind="Internal").ap()
        negscratch = nc.dram_tensor("exact_neg_scratch", [3, H * T, 128], BF16, kind="Internal").ap()

        jobs = ["q", "k", "v", "vsum"]
        jobs += [("max", h, t) for h in range(H) for t in range(T)]
        jobs += ["negmax"]
        jobs += [("unit", g, t, i) for g in range(NG) for t in range(T) for i in range(HG)]
        jobs += ["ctx0", "ctx1", "ctxT", "wo", "x1T", "h0", "h1", "hsum", "runT", "row1", "row2",
                 "out0", "out1"]
        slot_of = {j: n % 3 for n, j in enumerate(jobs)}
        use_of = {j: n // 3 for n, j in enumerate(jobs)}
        uses = [sum(1 for j in jobs if slot_of[j] == s) for s in range(3)]
        slot_full = [sem(f"slot{i}_full") for i in range(3)]
        slot_free = [sem(f"slot{i}_free") for i in range(3)]

        def free_for(b, job):
            return slot_free[slot_of[job]], b * uses[slot_of[job]] + use_of[job]

        def full(b, job):
            return slot_full[slot_of[job]], b * uses[slot_of[job]] + use_of[job] + 1

        def read_by(b, job):
            return slot_free[slot_of[job]], b * uses[slot_of[job]] + use_of[job] + 1

        def alone(eng, at):
            eng.memset(carrier[:, at:at + 1], 0.0)

        consts_in = sem("consts_in")
        bo_in = sem("bo_in")
        consts_made = sem("consts_made")
        setup_mm = sem("setup_mm")
        setup_copied = sem("setup_copied")
        x_in = sem("x_in")
        raw_in = [sem(f"raw{i}_in") for i in range(2)]
        masks_made = sem("masks_made")
        part0_made = sem("part0_made")
        parts_made = sem("parts_made")
        parts_out = sem("parts_out")
        stacks_in = sem("stacks_in")
        vsum_made = sem("vsum_made")
        negparts_made = sem("negparts_made")
        negparts_out = sem("negparts_out")
        negmax_made = sem("negmax_made")
        units_used = sem("units_used")
        acc_full = sem("acc_full")
        acc_read = sem("acc_read")
        ctxn_made = sem("ctxn_made")
        xb_made = sem("xb_made")
        vareps_made = sem("vareps_made")
        rstd_made = sem("rstd_made")
        x1_made = sem("x1_made")
        running_made = sem("running_made")
        diag_made = sem("diag_made")
        logits_made = sem("logits_made")
        logits_masked = sem("logits_masked")
        weights_made = sem("weights_made")
        y_out = sem("y_out")
        out_done = sem("out_done")
        dve_step = sem("dve_step")
        pool_step = sem("pool_step")
        DVE_STEPS = 46
        SETUP_STEPS = 1

        block = ctx.enter_context(nc.Block())
        bo_row = bo.rearrange("(o d) -> o d", o=1)

        @block.sync
        def _(sp):
            run = sp.value_load(needed[:], min_val=0, max_val=1)
            with sp.If(run > 0):
                for dst, src in ((wq, Wq), (wk, Wk), (wv, Wv), (wo, Wo), (w_of, W),
                                 (acol, a.rearrange("o (c d) -> d (o c)", c=2))):
                    with nc.allow_non_contiguous_dma(reason="a is 256 numbers"):
                        sp.dma_start(dst[:], src).then_inc(consts_in, 16)
                sp.dma_start(bo_all[:], bo_row.to_broadcast([128, D])).then_inc(bo_in, 16)
                def batch(b):
                    sp.wait_ge(slot_full[slot_of["v"]], b * uses[slot_of["v"]])
                    sp.wait_ge(xb_made, b)
                    sp.dma_start(xT_sb[:], xT[b]).then_inc(x_in, 16)
                    sp.dma_start(x_sb[:], x[b].rearrange("(t p) d -> p t d", p=128)).then_inc(x_in, 16)
                    for c in range(2 * CH):
                        src = (adjT if c < CH else adj)[b].rearrange("(t p) n -> p t n", p=128)
                        t0 = 2 * (c % CH)
                        if c >= 2:
                            sp.wait_ge(masks_made, b * 2 * CH + c - 1)
                        else:
                            sp.wait_ge(masks_made, b * 2 * CH)
                        sp.dma_start(raw[c % 2][:], src[:, t0:t0 + 2, :]).then_inc(raw_in[c % 2], 16)
                    for s in range(2):
                        sp.wait_ge(parts_made, 2 * b + s + 1)
                        for i in range(3):
                            sp.dma_start(scratch[s, i].rearrange("h d n -> (h d) n"),
                                         parts[s][i][:]).then_inc(parts_out, 16)
                    sp.wait_ge(parts_out, b * 96 + 96)
                    sp.wait_ge(units_used, b * H * T)
                    for r in range(BLOCKS):
                        rows = slice(r * HD, (r + 1) * HD)
                        sp.dma_start(qst[rows], scratch[0, QPART[r]].rearrange("h d n -> d h n")).then_inc(stacks_in, 16)
                        sp.dma_start(kst[rows], scratch[1, KPART[r]].rearrange("h d n -> d h n")).then_inc(stacks_in, 16)
                    sp.wait_ge(negparts_made, b + 1)
                    for i in range(3):
                        sp.dma_start(negscratch[i], negparts[i][:]).then_inc(negparts_out, 16)
                    sp.wait_ge(negparts_out, b * 48 + 48)
                    sp.dma_start(qst[KROWS:SROWS],
                                 negscratch.rearrange("i (h t) n -> i h (t n)", h=H)).then_inc(negmax_made, 16)
                    sp.wait_ge(y_out, b + 1)
                    sp.dma_start(out[b].rearrange("(t p) d -> p t d", p=128), y[:]).then_inc(out_done, 16)

                batch(0)
                with sp.Fori(1, B) as b:
                    batch(b)
                sp.wait_ge(out_done, 16 * B)

        @block.tensor
        def _(pe):
            run = pe.value_load(needed[:], min_val=0, max_val=1)
            with pe.If(run > 0):
                kw = dict(start=True, stop=True)
                pe.wait_ge(consts_in, 96)
                pe.wait_ge(consts_made, 2)
                pe.transpose(slots[0][:, 0:D], w_of[:], ident[:])
                pe.matmul(slots[0][:, D:D + 2], w_of[:], acol[:], **kw)
                pe.matmul(slots[0][:, 256:256 + D], w_of[:], a1wide[:], **kw).then_inc(setup_mm, 1)
                pe.wait_ge(setup_copied, 1)
                def batch(b):
                    pe.wait_ge(x_in, b * 32 + 32)
                    for job, w in (("q", wq), ("k", wk)):
                        pe.wait_ge(*free_for(b, job))
                        ps = slots[slot_of[job]]
                        for c in range(2):
                            cols = slice(c * HALF, (c + 1) * HALF)
                            mm = pe.matmul(ps[:, cols], w[:], xT_sb[:, cols], **kw)
                        mm.then_inc(slot_full[slot_of[job]], 1)
                    pe.wait_ge(*free_for(b, "v"))
                    ps = slots[slot_of["v"]]
                    for t in range(T):
                        mm = pe.matmul(ps[:, t * 128:(t + 1) * 128], xT_sb[:, t * 128:(t + 1) * 128], wv[:], **kw)
                    mm.then_inc(slot_full[slot_of["v"]], 1)
                    pe.wait_ge(*free_for(b, "vsum"))
                    ps = slots[slot_of["vsum"]]
                    pe.wait_ge(*read_by(b, "v"))
                    for t in range(T):
                        mm = pe.matmul(ps[:, 0:H * VW], ones[:], vst[:, t].rearrange("p h d -> p (h d)"),
                                       start=(t == 0), stop=(t == T - 1))
                    mm.then_inc(slot_full[slot_of["vsum"]], 1)

                    pe.wait_ge(stacks_in, b * 32 * BLOCKS + 32 * BLOCKS)
                    for h in range(H):
                        for t in range(T):
                            pe.wait_ge(*free_for(b, ("max", h, t)))
                            ps = slots[slot_of[("max", h, t)]]
                            for c in range(2):
                                cols = slice(c * HALF, (c + 1) * HALF)
                                mm = pe.matmul(ps[:, cols], qst[0:KROWS, h, t * 128:(t + 1) * 128],
                                               kst[0:KROWS, h, cols], **kw)
                            mm.then_inc(slot_full[slot_of[("max", h, t)]], 1)
                    pe.wait_ge(*free_for(b, "negmax"))
                    ps = slots[slot_of["negmax"]]
                    pe.wait_ge(dve_step, SETUP_STEPS + b * DVE_STEPS + NEG_STEP)
                    mm = pe.matmul(ps[0:H * T, 0:128], negmax[:], ident[:], **kw)
                    mm.then_inc(slot_full[slot_of["negmax"]], 1)

                    pe.wait_ge(negmax_made, b * 16 + 16)
                    pe.wait_ge(masks_made, (b + 1) * 2 * CH)

                    def scores(g, t, i):
                        h = g * HG + i
                        job = ("unit", g, t, i)
                        pe.wait_ge(*free_for(b, job))
                        ps = slots[slot_of[job]]
                        for c in range(2):
                            cols = slice(c * HALF, (c + 1) * HALF)
                            pe.matmul(ps[:, cols], identb[:], biasT[:, t, cols], start=True, stop=False)
                            mm = pe.matmul(ps[:, cols], kst[:, h, t * 128:(t + 1) * 128], qst[:, h, cols],
                                           start=False, stop=True)
                        mm.then_inc(slot_full[slot_of[job]], 1)

                    def context(g, t):
                        quad = g * T + t
                        for i in range(HG):
                            pe.wait_ge(*read_by(b, ("unit", g, t, i)))
                        if t == 0:
                            pe.wait_ge(acc_read, b * NG + g)
                        for c in range(2):
                            cols = slice(c * HALF, (c + 1) * HALF)
                            for i in range(HG):
                                mm = pe.matmul(acc[VW * i:VW * (i + 1), cols], vst[:, t, g * HG + i],
                                               weights[:, (HG * quad + i) % 8, cols],
                                               start=(t == 0), stop=(t == T - 1))
                        mm.then_inc(units_used, HG)

                    quads = [(g, t) for g in range(NG) for t in range(T)]
                    for n, (g, t) in enumerate(quads):
                        for i in range(HG):
                            scores(g, t, i)
                        if n:
                            context(*quads[n - 1])
                    context(*quads[-1])

                    for k in range(2):
                        job = f"ctx{k}"
                        pe.wait_ge(*free_for(b, job))
                        ps = slots[slot_of[job]]
                        pe.wait_ge(acc_read, b * NG + NG)
                        for t in range(4):
                            for g in range(NG):
                                mm = pe.transpose(ps[:, (t * NG + g) * 128:(t * NG + g + 1) * 128],
                                                  ctxT[:, g, (4 * k + t) * 128:(4 * k + t + 1) * 128], ident[:])
                        mm.then_inc(slot_full[slot_of[job]], 1)
                    pe.wait_ge(*free_for(b, "ctxT"))
                    ps = slots[slot_of["ctxT"]]
                    pe.wait_ge(ctxn_made, 2 * b + 2)
                    for t in range(T):
                        mm = pe.transpose(ps[:, t * 128:(t + 1) * 128], ctxn[:, t], ident[:])
                    mm.then_inc(slot_full[slot_of["ctxT"]], 1)
                    pe.wait_ge(*free_for(b, "wo"))
                    ps = slots[slot_of["wo"]]
                    pe.wait_ge(*read_by(b, "ctxT"))
                    for t in range(T):
                        mm = pe.matmul(ps[:, t * 128:(t + 1) * 128], ctxnT[:, t * 128:(t + 1) * 128], wo[:], **kw)
                    mm.then_inc(slot_full[slot_of["wo"]], 1)

                    pe.wait_ge(*free_for(b, "x1T"))
                    ps = slots[slot_of["x1T"]]
                    pe.wait_ge(x1_made, b + 1)
                    for t in range(T):
                        mm = pe.transpose(ps[:, t * 128:(t + 1) * 128], x1[:, t], ident[:])
                    mm.then_inc(slot_full[slot_of["x1T"]], 1)
                    pe.wait_ge(*read_by(b, "x1T"))
                    for k in range(2):
                        job = f"h{k}"
                        pe.wait_ge(*free_for(b, job))
                        ps = slots[slot_of[job]]
                        for t in range(4):
                            mm = pe.matmul(ps[:, t * 256:t * 256 + D + 2],
                                           x1T[:, (4 * k + t) * 128:(4 * k + t + 1) * 128], wh[:], **kw)
                        mm.then_inc(slot_full[slot_of[job]], 1)
                    pe.wait_ge(*free_for(b, "hsum"))
                    ps = slots[slot_of["hsum"]]
                    for k in range(2):
                        pe.wait_ge(*read_by(b, f"h{k}"))
                    for t in range(T):
                        mm = pe.matmul(ps[:, 0:HW], ones[:], hst[:, t], start=(t == 0), stop=(t == T - 1))
                    mm.then_inc(slot_full[slot_of["hsum"]], 1)
                    pe.wait_ge(*free_for(b, "runT"))
                    ps = slots[slot_of["runT"]]
                    pe.wait_ge(running_made, b + 1)
                    for t in range(T):
                        mm = pe.transpose(ps[:, t * 128:(t + 1) * 128], running[:, t * 128:(t + 1) * 128], ident[:])
                    mm.then_inc(slot_full[slot_of["runT"]], 1)
                    for k in range(2):
                        job = f"row{k + 1}"
                        pe.wait_ge(*free_for(b, job))
                        ps = slots[slot_of[job]]
                        pe.wait_ge(diag_made, b + 1)
                        for c in range(2):
                            cols = slice(c * HALF, (c + 1) * HALF)
                            pe.matmul(ps[:, cols], u1wide[:, k], x1T[:, cols], start=True, stop=False)
                            mm = pe.matmul(ps[:, cols], negones[:],
                                           diag[:, 4 * c:4 * c + 4].rearrange("p t n -> p (t n)"),
                                           start=False, stop=True)
                        mm.then_inc(slot_full[slot_of[job]], 1)
                    for k in range(2):
                        job = f"out{k}"
                        pe.wait_ge(*free_for(b, job))
                        ps = slots[slot_of[job]]
                        pe.wait_ge(weights_made, b * T + T)
                        for t in range(4):
                            for j in range(T):
                                mm = pe.matmul(ps[:, t * 256:t * 256 + HW],
                                               weights[:, j, (4 * k + t) * 128:(4 * k + t + 1) * 128],
                                               hst[:, j], start=(j == 0), stop=(j == T - 1))
                        mm.then_inc(slot_full[slot_of[job]], 1)

                batch(0)
                with pe.Fori(1, B) as b:
                    batch(b)

        @block.scalar
        def _(act):
            run = act.value_load(needed[:], min_val=0, max_val=1)
            with act.If(run > 0):
                act.wait_ge(setup_mm, 1)
                act.activation(wh[:], slots[0][:, 0:D + 2], ACT.Copy)
                act.activation(u1wide[:, 1], slots[0][:, 256:256 + D], ACT.Copy, scale=ALPHA)
                act.activation(u1wide[:, 0], slots[0][:, 256:256 + D], ACT.Copy).then_inc(setup_copied, 1)
                def batch(b):
                    for s, job in enumerate("qk"):
                        act.wait_ge(*full(b, job))
                        ps = slots[slot_of[job]]
                        act.wait_ge(parts_out, b * 96)
                        act.activation(parts[s][0][:], ps[:], ACT.Copy).then_inc(part0_made, 1)
                    act.wait_ge(*full(b, "vsum"))
                    ps = slots[slot_of["vsum"]]
                    act.wait_ge(ctxn_made, 2 * b)
                    ins = act.activation(vsum[:].rearrange("p h d -> p (h d)"), ps[:, 0:H * VW], ACT.Copy)
                    ins.then_inc(slot_free[slot_of["vsum"]], 1)
                    n = 0
                    for g in range(NG):
                        for t in range(T):
                            for i in range(HG):
                                act.wait_ge(*full(b, ("unit", g, t, i)))
                                ps = slots[slot_of[("unit", g, t, i)]]
                                if n >= 8:
                                    act.wait_ge(units_used, b * H * T + n - 7 + (-(n - 7)) % HG)
                                else:
                                    act.wait_ge(units_used, b * H * T)
                                    if n == 0:
                                        act.wait_ge(y_out, b)
                                ins = act.activation(weights[:, n % 8], ps[:], ACT.Exp, scale=SCALE)
                                ins.then_inc(slot_free[slot_of[("unit", g, t, i)]], 1)
                                n += 1
                    act.wait_ge(*full(b, "ctxT"))
                    ps = slots[slot_of["ctxT"]]
                    ins = act.activation(ctxnT[:], ps[:], ACT.Copy)
                    ins.then_inc(slot_free[slot_of["ctxT"]], 1)
                    act.wait_ge(*full(b, "x1T"))
                    ps = slots[slot_of["x1T"]]
                    ins = act.activation(x1T[:], ps[:], ACT.Copy)
                    ins.then_inc(slot_free[slot_of["x1T"]], 1)
                    for k in range(2):
                        act.wait_ge(*full(b, f"h{k}"))
                        ps = slots[slot_of[f"h{k}"]]
                        view = ps[:].rearrange("p (t w) -> p t w", w=256)[:, :, 0:D + 2]
                        ins = act.activation(hst[:, 4 * k:4 * k + 4, 0:D + 2], view, ACT.Copy)
                        ins.then_inc(slot_free[slot_of[f"h{k}"]], 1)
                    act.wait_ge(*full(b, "hsum"))
                    ps = slots[slot_of["hsum"]]
                    ins = act.activation(hsum[:], ps[:, 0:HW], ACT.Copy)
                    ins.then_inc(slot_free[slot_of["hsum"]], 1)
                    for k, row in enumerate((row1, row2)):
                        act.wait_ge(*full(b, f"row{k + 1}"))
                        ps = slots[slot_of[f"row{k + 1}"]]
                        ins = act.activation(row[:], ps[:], ACT.Copy)
                        ins.then_inc(slot_free[slot_of[f"row{k + 1}"]], 1)
                    for t in range(T):
                        act.wait_ge(logits_masked, b * T + t + 1)
                        act.activation(weights[:, t], weights[:, t], ACT.Exp).then_inc(weights_made, 1)

                batch(0)
                with act.Fori(1, B) as b:
                    batch(b)

        @block.gpsimd
        def _(pool):
            run = pool.value_load(needed[:], min_val=0, max_val=1)
            with pool.If(run > 0):
                pool.memset(ones[:], 1.0)
                pool.memset(negones[:], -1.0)
                pool.memset(exponent[:], -0.5).then_inc(pool_step, 1)
                pool.wait_ge(pool_step, 1)
                pool.affine_select(out=ident[:], in_=ones[:], compare_op=ALU.is_equal, fill=0.0, base=0,
                                   pattern=[[-1, 128]], channel_multiplier=1).then_inc(pool_step, 1)
                pool.wait_ge(pool_step, 2)
                pool.tensor_copy(identb[:], ident[:]).then_inc(consts_made, 1)
                pool.wait_ge(bo_in, 16)
                def batch(b):
                    pool.wait_ge(x_in, b * 32 + 32)
                    pool.wait_ge(x1_made, b)
                    pool.tensor_tensor(xb[:], x_sb[:], bo_all[:].unsqueeze(1).to_broadcast([128, T, D]),
                                       ALU.add).then_inc(xb_made, 1)
                    pool.wait_ge(vareps_made, 2 * b + 1)
                    pool.tensor_tensor(rstd[:], vareps[:], exponent[:], ALU.pow).then_inc(rstd_made, 1)
                    for t in range(T):
                        pool.wait_ge(logits_made, b * T + t + 1)
                        pool.tensor_tensor(weights[:, t], weights[:, t], biasT[:, t],
                                           ALU.add).then_inc(logits_masked, 1)
                    pool.wait_ge(vareps_made, 2 * b + 2)
                    pool.tensor_tensor(rstd[:], vareps[:], exponent[:], ALU.pow).then_inc(rstd_made, 1)

                batch(0)
                with pool.Fori(1, B) as b:
                    batch(b)

        @block.vector
        def _(dve):
            run = dve.value_load(needed[:], min_val=0, max_val=1)
            with dve.If(run > 0):
                steps = [0]
                base = [0]

                def link(ins):
                    steps[0] += 1
                    ins.then_inc(dve_step, 1)
                    dve.wait_ge(dve_step, base[0] + steps[0])

                dve.wait_ge(consts_in, 96)
                dve.memset(kst[KROWS:SROWS], 1.0)
                dve.memset(hst[:, :, D + 2:HW], 1.0)
                link(dve.memset(vst[:, :, :, HD:VW], 0.0))
                dve.memset(vst[:, :, :, HD:HD + 1], 1.0)
                dve.tensor_copy(a1wide[:], acol[:, 0:1].to_broadcast([D, D])).then_inc(consts_made, 1)
                assert steps[0] == SETUP_STEPS

                def layernorm(b, k, src, dst):
                    for t in range(T):
                        ins = dve.bn_stats(stats[:, t], src[:, t])
                    link(ins)
                    alone(dve, H * T + k)
                    for t in range(T):
                        ins = dve.bn_aggr(meanvar[:, t], stats[:, t])
                    link(ins)
                    dve.tensor_scalar(vareps[:], meanvar[:, :, 1], EPS, None, ALU.add).then_inc(vareps_made, 1)
                    dve.wait_ge(rstd_made, 2 * b + k + 1)
                    for t in range(T):
                        ins = dve.tensor_scalar(dst[:, t], src[:, t], meanvar[:, t, 0:1], rstd[:, t:t + 1],
                                                ALU.subtract, ALU.mult)
                    return ins

                def batch(b):
                    base[0] = SETUP_STEPS + b * DVE_STEPS
                    steps[0] = 0
                    for c in range(2 * CH):
                        dve.wait_ge(raw_in[c % 2], (b * CH + c // 2 + 1) * 16)
                        if c == 0:
                            dve.wait_ge(logits_masked, b * T)
                        t0 = 2 * (c % CH)
                        dst = (biasT if c < CH else biasN)[:, t0:t0 + 2, :]
                        dve.tensor_scalar(dst, raw[c % 2][:], 0, -BIG, ALU.is_le, ALU.mult).then_inc(masks_made, 1)
                    for s, job in enumerate("qk"):
                        dve.wait_ge(*full(b, job))
                        ps = slots[slot_of[job]]
                        dve.wait_ge(part0_made, 2 * b + s + 1)
                        ins = dve.tensor_tensor(rest[:], ps[:], parts[s][0][:], ALU.subtract)
                        ins.then_inc(slot_free[slot_of[job]], 1)
                        dve.wait_ge(*read_by(b, job))
                        link(dve.tensor_copy(parts[s][1][:], rest[:]))
                        ins = dve.tensor_tensor(parts[s][2][:], rest[:], parts[s][1][:], ALU.subtract)
                        ins.then_inc(parts_made, 1)
                        dve.wait_ge(parts_made, 2 * b + s + 1)
                    dve.wait_ge(*full(b, "v"))
                    ps = slots[slot_of["v"]]
                    ins = dve.tensor_copy(vst[:, :, :, 0:HD], ps[:].rearrange("p (t h d) -> p t h d", t=T, h=H))
                    ins.then_inc(slot_free[slot_of["v"]], 1)

                    for h in range(H):
                        for t in range(T):
                            dve.wait_ge(*full(b, ("max", h, t)))
                            ps = slots[slot_of[("max", h, t)]]
                            if h == 0 and t == 0:
                                link(dve.memset(rowmax[:], 0.0))
                            alone(dve, h * T + t)
                            ins = dve.tensor_tensor_reduce(ps[:], ps[:], biasN[:, t], 1.0, -3.0e38, ALU.add,
                                                           ALU.max, rowmax[:, h * T + t:h * T + t + 1])
                            ins.then_inc(slot_free[slot_of[("max", h, t)]], 1)
                    for t in range(T - 3, T):
                        dve.wait_ge(*read_by(b, ("max", H - 1, t)))
                    link(dve.tensor_scalar(negmax[:], rowmax[:], FLOOR, -1.0, ALU.max, ALU.mult))
                    assert steps[0] == NEG_STEP, ("neg", steps[0])
                    dve.wait_ge(*full(b, "negmax"))
                    ps = slots[slot_of["negmax"]]
                    neg = ps[0:H * T, 0:128]
                    dve.wait_ge(negparts_out, b * 48)
                    link(dve.tensor_copy(negparts[0][:], neg))
                    ins = dve.tensor_tensor(negrest[:], neg, negparts[0][:], ALU.subtract)
                    ins.then_inc(slot_free[slot_of["negmax"]], 1)
                    dve.wait_ge(*read_by(b, "negmax"))
                    link(dve.tensor_copy(negparts[1][:], negrest[:]))
                    dve.tensor_tensor(negparts[2][:], negrest[:], negparts[1][:], ALU.subtract).then_inc(negparts_made, 1)

                    for g in range(NG):
                        dve.wait_ge(units_used, b * H * T + (g + 1) * HG * T)
                        dve.tensor_copy(ctxT[:, g], acc[:]).then_inc(acc_read, 1)
                    for k in range(2):
                        dve.wait_ge(*full(b, f"ctx{k}"))
                        ps = slots[slot_of[f"ctx{k}"]]
                        view = ps[:].rearrange("p (t h d) -> p t h d", t=4, h=H)
                        tt = slice(4 * k, 4 * k + 4)
                        link(dve.tensor_scalar(empty[:, tt], view[:, :, :, HD], 0.0, None, ALU.is_equal))
                        link(dve.scalar_tensor_tensor(out=den[:, tt], in0=empty[:, tt], scalar=float(N),
                                                      in1=view[:, :, :, HD], op0=ALU.mult, op1=ALU.add))
                        link(dve.reciprocal(rden[:, tt], den[:, tt]))
                        dve.wait_ge(*read_by(b, "vsum"))
                        link(dve.tensor_tensor(fix[:], empty[:, tt].unsqueeze(3).to_broadcast([128, 4, H, HD]),
                                               vsum[:, :, 0:HD].unsqueeze(1).to_broadcast([128, 4, H, HD]), ALU.mult))
                        ins = dve.tensor_tensor(fix[:], view[:, :, :, 0:HD], fix[:], ALU.add)
                        ins.then_inc(slot_free[slot_of[f"ctx{k}"]], 1)
                        dve.wait_ge(*read_by(b, f"ctx{k}"))
                        ins = dve.tensor_tensor(ctxn[:, tt].rearrange("p t (h d) -> p t h d", h=H), fix[:],
                                                rden[:, tt].unsqueeze(3).to_broadcast([128, 4, H, HD]), ALU.mult)
                        ins.then_inc(ctxn_made, 1)
                    dve.wait_ge(*full(b, "wo"))
                    ps = slots[slot_of["wo"]]
                    dve.wait_ge(xb_made, b + 1)
                    dve.wait_ge(out_done, b * 16)
                    ins = dve.tensor_tensor(y[:].rearrange("p t d -> p (t d)"), ps[:],
                                            xb[:].rearrange("p t d -> p (t d)"), ALU.add)
                    ins.then_inc(slot_free[slot_of["wo"]], 1)
                    dve.wait_ge(*read_by(b, "wo"))
                    ins = layernorm(b, 0, y, x1)
                    ins.then_inc(x1_made, 1)
                    for k in range(2):
                        dve.wait_ge(*read_by(b, f"h{k}"))
                    link(dve.tensor_scalar(running[:], biasT[:, 0], hst[:, 0, D + 1:D + 2], None, ALU.add))
                    for t in range(1, T):
                        ins = dve.scalar_tensor_tensor(out=running[:], in0=biasT[:, t], scalar=hst[:, t, D + 1:D + 2],
                                                       in1=running[:], op0=ALU.add, op1=ALU.max)
                        if t < T - 1:
                            link(ins)
                    ins.then_inc(running_made, 1)
                    dve.wait_ge(*full(b, "runT"))
                    ps = slots[slot_of["runT"]]
                    ins = dve.tensor_reduce(nbmax[:], ps[:].rearrange("p (t n) -> p t n", t=T), AX_X, ALU.max)
                    ins.then_inc(slot_free[slot_of["runT"]], 1)
                    dve.wait_ge(*read_by(b, "runT"))
                    link(dve.tensor_tensor(nbmax[:], nbmax[:], hst[:, :, D], ALU.add))
                    link(dve.scalar_tensor_tensor(out=shift[:], in0=nbmax[:], scalar=ALPHA, in1=nbmax[:],
                                                  op0=ALU.mult, op1=ALU.max))
                    dve.tensor_tensor(diag[:], ident[:].unsqueeze(1).to_broadcast([128, T, 128]),
                                      shift[:].unsqueeze(2).to_broadcast([128, T, 128]), ALU.mult).then_inc(diag_made, 1)
                    link(dve.tensor_scalar(rden[:, :, 0], hst[:, :, D + 1], ALPHA, None, ALU.mult))
                    for k in range(2):
                        dve.wait_ge(*read_by(b, f"row{k + 1}"))
                    dve.wait_ge(units_used, (b + 1) * H * T)
                    for t in range(T):
                        link(dve.tensor_scalar(weights[:, t], row1[:], hst[:, t, D + 1:D + 2], None, ALU.add))
                        ins = dve.scalar_tensor_tensor(out=weights[:, t], in0=row2[:], scalar=rden[:, t, 0:1],
                                                       in1=weights[:, t], op0=ALU.add, op1=ALU.max)
                        ins.then_inc(logits_made, 1)
                    dve.wait_ge(*read_by(b, "hsum"))
                    for k in range(2):
                        dve.wait_ge(*full(b, f"out{k}"))
                        ps = slots[slot_of[f"out{k}"]]
                        view = ps[:].rearrange("p (t w) -> p t w", w=256)
                        tt = slice(4 * k, 4 * k + 4)
                        dcol = view[:, :, D + 2]
                        link(dve.tensor_scalar(empty[:, tt, 0], dcol, 0.0, None, ALU.is_equal))
                        link(dve.scalar_tensor_tensor(out=den[:, tt, 0], in0=empty[:, tt, 0], scalar=float(N),
                                                      in1=dcol, op0=ALU.mult, op1=ALU.add))
                        link(dve.reciprocal(den[:, tt, 1], den[:, tt, 0]))
                        link(dve.tensor_tensor(empty[:, tt, 1], empty[:, tt, 0], den[:, tt, 1], ALU.mult))
                        for t in range(4):
                            u = 4 * k + t
                            ins = dve.scalar_tensor_tensor(out=y[:, u], in0=view[:, t, 0:D], scalar=den[:, u, 1:2],
                                                           in1=x1[:, u], op0=ALU.mult, op1=ALU.add)
                        ins.then_inc(slot_free[slot_of[f"out{k}"]], 1)
                        dve.wait_ge(*read_by(b, f"out{k}"))
                        for t in range(4):
                            u = 4 * k + t
                            ins = dve.scalar_tensor_tensor(out=y[:, u], in0=hsum[:, 0:D], scalar=empty[:, u, 1:2],
                                                           in1=y[:, u], op0=ALU.mult, op1=ALU.add)
                        link(ins)
                    layernorm(b, 1, y, y).then_inc(y_out, 1)
                    assert steps[0] == DVE_STEPS, steps[0]

                batch(0)
                with dve.Fori(1, B) as b:
                    batch(b)


def kernel(x, adj, L0_gnn_Wq, L0_gnn_Wk, L0_gnn_Wv, L0_gnn_Wo, L0_gnn_bo, L1_gnn_W, L1_gnn_a):
    import numpy as np
    import concourse.bacc as bacc
    from concourse.bass_utils import run_bass_kernel_spmd

    x, adj = np.asarray(x), np.asarray(adj)
    ins = {
        "x": x, "xT": np.ascontiguousarray(x.transpose(0, 2, 1)),
        "adj": adj, "adjT": np.ascontiguousarray(adj.transpose(0, 2, 1)),
        "Wq": np.asarray(L0_gnn_Wq), "Wk": np.asarray(L0_gnn_Wk), "Wv": np.asarray(L0_gnn_Wv),
        "Wo": np.asarray(L0_gnn_Wo), "bo": np.asarray(L0_gnn_bo), "W": np.asarray(L1_gnn_W),
        "a": np.asarray(L1_gnn_a),
    }
    nc = bacc.Bacc("TRN2", target_bir_lowering=False, num_devices=1)
    arrays, args = {}, []
    for name, v in ins.items():
        arrays[f"in_{name}"] = v
        args.append(nc.dram_tensor(f"in_{name}", v.shape, mybir.dt.from_np(v.dtype), kind="ExternalInput").ap())
    args.append(nc.dram_tensor("out_0", x.shape, F32, kind="ExternalOutput").ap())
    x_, xT, adj_, adjT, *rest = args
    with ExitStack() as outer:
        needed = outer.enter_context(nc.sbuf_tensor("needed", [1, 1], I32))
        build_fast(nc, outer, needed, x_, xT, adjT, *rest)
        build_exact(nc, outer, needed, x_, xT, adj_, adjT, *rest)
    r = run_bass_kernel_spmd(nc, [arrays], core_ids=[0])
    return r.results[0]["out_0"]
```

```python
from contextlib import ExitStack

import concourse.bass as bass
from concourse import mybir

ALU = mybir.AluOpType
ACT = mybir.ActivationFunctionType
F32 = mybir.dt.float32
BF16 = mybir.dt.bfloat16
I32 = mybir.dt.int32
AX_X = mybir.AxisListType.X

EPS = 1e-5
ALPHA = 0.2
BIG = 2.0 ** 30
FLOOR = -1.0e8
NEG_STEP = 4
FARTHEST = 60.0

KPART = (0, 0, 1, 1, 0, 2)
QPART = (0, 1, 0, 1, 2, 0)
BLOCKS = len(KPART)

STAGES = {
    "ctx0": "post", "ctx1": "post", "ctxT": "post", "wo": "post", "x1T": "post", "h0": "post",
    "h1": "post", "fjmax": "post", "fi": "post", "hsum": "post",
    "out0": "post", "out1": "post", "out2": "post", "out3": "post",
    "v1": "own", "vsum": "own",
    "q": "prep", "k": "prep", "ck": "prep", "cq": "prep", "v0": "prep",
}
AFTER_HALF = {
    2: ["ctx0"], 4: ["v1"], 5: ["ctx1"], 7: ["vsum"], 8: ["ctxT"], 9: ["wo"], 12: ["q"],
    14: ["x1T"], 15: ["k"], 16: ["h0"], 17: ["h1", "ck"], 18: ["fjmax"], 19: ["cq"],
    20: ["fi", "hsum"], 26: ["out0"], 28: ["out1"], 29: ["out2"], 30: ["out3"], 31: ["v0"],
}
PREP = ["q", "k", "ck", "cq", "v0"]
POST = [j for n in sorted(AFTER_HALF) for j in AFTER_HALF[n] if STAGES[j] == "post"]
OFFSET = {"post": -1, "own": 0, "prep": 1}
MASKED_BY = ["pdpd", "dpdp", "dppd", "pdpd", "pdpd", "pdpd", "pdpd", "pdpd",
             "pdpd", "dppd", "pdpd", "pdpd", "dpdd", "dpdd", "dpdd", "pdpd"]

EXP_ATTS = (21, 21, 21, 22, 22, 23, 23, 24)
MAX_ATTS = (21, 21, 21, 22, 22, 23, 23, 24)
MASK_ATTS = (21, 21, 22, 22, 22, 23, 23, 24)
ATTS_MASKED_BY = "ppdppdpd"
POW1 = 10
NORM1 = 11
STATS2 = 30
POW2 = 31
NORM2 = 31
RESIDUAL = 29
SPLIT = []
READ_ACC = 1
STACK1_BEFORE = 5
LOOP_STEPS = 47
CONTEXT_AFTER = [[(2, 1)], [], [], [(1, 0)]]
BUFFER = (0, 1, 2, 0, 1, 2, 0, 1, 2, 0, 1, 2, 0, 1, 2, 1)


def last_with_buffer(n):
    return next(m for m in range(n - 1, n - 17, -1) if BUFFER[m % 16] == BUFFER[n])


def contexts_left():
    return [(n - ago, half) for n in (16, 17) for places in CONTEXT_AFTER for ago, half in places if n - ago < 16]


def jobs_after(kind, half):
    return [j for j in AFTER_HALF.get(half, [])
            if not (kind == "first" and STAGES[j] == "post") and not (kind == "last" and STAGES[j] == "prep")]


def ring_plan():
    def whole_pass(kind):
        jobs = []
        for half in range(32):
            jobs += [("unit", 0, 2 * half), ("unit", 0, 2 * half + 1)]
            jobs += [(j, OFFSET[STAGES[j]], 0) for j in jobs_after(kind, half)]
        return jobs
    passes = {
        "prologue": [(j, 1, 0) for j in PREP],
        "first": whole_pass("first"),
        "loop": whole_pass("loop"),
        "last": whole_pass("last"),
        "epilogue": [(j, -1, 0) for j in POST],
    }
    before = {"prologue": None, "first": "prologue", "loop": "loop", "last": "loop", "epilogue": "last"}
    slot = {}
    for name, jobs in passes.items():
        for n, j in enumerate(jobs):
            slot[name, j] = n % 3 if name in ("prologue", "epilogue") else j[2] % 2 if j[0] == "unit" else 2
    holder = {}
    for name, jobs in passes.items():
        for n, j in enumerate(jobs):
            s = slot[name, j]
            here = [e for e in jobs[:n] if slot[name, e] == s]
            there = [e for e in passes[before[name]] if slot[before[name], e] == s] if before[name] else []
            if here:
                holder[name, j] = here[-1]
            elif there:
                holder[name, j] = (there[-1][0], there[-1][1] - 1, there[-1][2])
            else:
                holder[name, j] = None
    for s in range(3):
        ends = [[e for e in passes[p] if slot[p, e] == s][-1] for p in ("first", "loop")]
        assert ends[0] == ends[1], ends
    return slot, holder


def build_fast(nc, sems, needed, x, xT, adjT, Wq, Wk, Wv, Wo, bo, W, a, out):
    B, N, D = x.shape
    H = 8
    HD = D // H
    T = N // 128
    HALF = N // 2
    HG = 4
    NG = H // HG
    QUADS = NG * T
    UNITS = QUADS * HG
    QW = N // 4
    SCALE = 1.0 / float(HD) ** 0.5
    KROWS = BLOCKS * HD
    SROWS = KROWS + 1
    HW = D + 3
    VW = 32
    NORM_WEIGHT = 0.5078125
    STACK_DMAS = 2 * BLOCKS + 1
    RAW = 2
    slot, holder = ring_plan()

    with ExitStack() as ctx:
        def sb(name, shape, dt):
            return ctx.enter_context(nc.sbuf_tensor(name, shape, dt))

        def sem(name):
            return sems.enter_context(nc.semaphore(name))

        slots = [ctx.enter_context(nc.psum_tensor(f"slot{i}", [128, N], F32)) for i in range(3)]
        acc = ctx.enter_context(nc.psum_tensor("acc", [128, N], F32))

        ident = sb("ident", [128, 128], F32)
        ones = sb("ones", [128, 128], F32)
        headsum = sb("headsum", [128, H], BF16)
        wq = sb("wq", [D, D], F32)
        wk = sb("wk", [D, D], F32)
        wv = sb("wv", [D, D], F32)
        wo = sb("wo", [D, D], F32)
        w_of = sb("w_of", [D, D], F32)
        acol = sb("acol", [D, 2], F32)
        awide = sb("awide", [D, 2, D], F32)
        wh = sb("wh", [D, D + 2], F32)
        uwide = sb("uwide", [D, 2, D], F32)
        bo_all = sb("bo_all", [128, D], F32)
        exponent = sb("exponent", [128, T], F32)

        xT_sb = sb("xT_sb", [D, N], F32)
        raw = [sb(f"raw{i}", [128, N], I32) for i in range(RAW)]
        mask = sb("mask", [128, T, N], BF16)
        old_mask = sb("old_mask", [128, T, N], BF16)
        qst = sb("qst", [SROWS, H, N], BF16)
        kst = sb("kst", [SROWS, H, N], BF16)
        vst = sb("vst", [128, T, H, VW], F32)
        weights = sb("weights", [128, 3 * HG, N], F32)
        negshift = sb("negshift", [H, N], BF16)
        kmax = sb("kmax", [H, 1], F32)
        negkmax = sb("negkmax", [H, 1], F32)
        too_far = sb("too_far", [128, 1], I32)
        too_far_row = sb("too_far_row", [1, 128], I32)
        carrier = sb("carrier", [128, 1], F32)
        worst_row = sb("worst_row", [H, 1], F32)
        worst = sb("worst", [H, 1], F32)
        farthest = sb("farthest", [128, 1], F32)
        lowest = sb("lowest", [128, 1], F32)
        xsum = sb("xsum", [D, 1], F32)
        xsum_wide = sb("xsum_wide", [D, 128], F32)
        vsum = sb("vsum", [128, D], F32)

        x_sb = sb("x_sb", [128, T, D], F32)
        den = sb("den", [128, T, H], F32)
        empty = sb("empty", [128, T, H], F32)
        rden = sb("rden", [128, T, H], F32)
        y = sb("y", [128, T, D], F32)
        x1 = sb("x1", [128, T, D], F32)
        stats = sb("stats", [128, T, 6], F32)
        meanvar = sb("meanvar", [128, T, 2], F32)
        vareps = sb("vareps", [128, T], F32)
        rstd = sb("rstd", [128, T], F32)
        hst = sb("hst", [128, T, HW], F32)
        x1sum = sb("x1sum", [D, 1], F32)
        x1sum_wide = sb("x1sum_wide", [D, 128], F32)
        hsum = sb("hsum", [128, D + 2], F32)
        fmax = sb("fmax", [128, 1], F32)
        pivot = sb("pivot", [128, 2], F32)
        below = sb("below", [128, 2, T], F32)
        exp_below = sb("exp_below", [128, T], F32)
        atts = sb("atts", [128, 4, T, QW], F32)
        early = atts[:, 0:2].rearrange("p q t n -> p (q t n)")
        ctxT = [sb("ctxT0", [128, N], F32)[:], early[:, 0:N]]
        turn1 = early[:, N:2 * N]
        fix = early[:, 2 * N:2 * N + HALF].rearrange("p (t h d) -> p t h d", t=4, h=H)
        ctxn = turn1.rearrange("p (t d) -> p t d", t=T)
        x1T = turn1
        turn2 = sb("turn2", [128, N], F32)
        ctxnT = turn2
        exp_rise = turn2
        turn3 = sb("turn3", [128, N], F32)
        rest = turn3
        fall = turn3
        partmem = atts[:, 2:4].rearrange("p q t n -> p (q t n)").bitcast(BF16)
        parts = [[partmem[:, (3 * s + i) * N:(3 * s + i + 1) * N] for i in range(3)] for s in range(2)]
        squares = [partmem[:, (6 + s) * N:(7 + s) * N] for s in range(2)]

        scratch = nc.dram_tensor("parts_scratch", [2, 3, H, HD, N], BF16, kind="Internal").ap()
        flag_scratch = nc.dram_tensor("flag_scratch", [1, 128], I32, kind="Internal").ap()
        shift_scratch = nc.dram_tensor("shift_scratch", [H, N], BF16, kind="Internal").ap()

        full = {j: sem(f"{j}_full") for j in ["unit", *STAGES]}
        taken = {j: sem(f"{j}_taken") for j in ["unit", *STAGES]}
        per = {j: UNITS if j == "unit" else 1 for j in full}

        def free_for(kind, b, job):
            was = holder[kind, job]
            if was is None:
                return taken["q"], 0
            return taken[was[0]], (b + was[1]) * per[was[0]] + was[2] + 1

        consts_in = sem("consts_in")
        consts_made = sem("consts_made")
        setup_mm = sem("setup_mm")
        setup_copied = sem("setup_copied")
        xT_in = sem("xT_in")
        x_in = sem("x_in")
        xb_made = sem("xb_made")
        raw_in = [sem(f"raw{i}_in") for i in range(RAW)]
        masks_made = sem("masks_made")
        parts_made = sem("parts_made")
        squares_made = sem("squares_made")
        parts_out = sem("parts_out")
        shift_out = sem("shift_out")
        part0_made = sem("part0_made")
        stack_in = [sem(f"stack{g}_in") for g in range(NG)]
        kmax_made = sem("kmax_made")
        xsum_made = sem("xsum_made")
        masked_dve = sem("masked_dve")
        masked_pool = sem("masked_pool")
        contexts_done = sem("contexts_done")
        acc_read = sem("acc_read")
        ctxn_made = sem("ctxn_made")
        vareps_made = sem("vareps_made")
        rstd_made = sem("rstd_made")
        x1_made = sem("x1_made")
        x1sum_made = sem("x1sum_made")
        below_made = sem("below_made")
        rows_made = sem("rows_made")
        atts_exp = sem("atts_exp")
        atts_max = sem("atts_max")
        atts_made = {"p": sem("atts_made_by_gpsimd"), "d": sem("atts_made_by_vector")}
        y_made = sem("y_made")
        out_done = sem("out_done")
        too_far_made = sem("too_far_made")
        flags_out = sem("flags_out")
        flags_in = sem("flags_in")
        dve_step = sem("dve_step")
        pool_step = sem("pool_step")

        by = {e: sum(q.count(e) for q in MASKED_BY) for e in "dp"}

        def masked(e, n, i):
            return sum(q.count(e) for q in MASKED_BY[:n]) + MASKED_BY[n][:i + 1].count(e)

        block = ctx.enter_context(nc.Block())
        bo_row = bo.rearrange("(o d) -> o d", o=1)

        @block.sync
        def _(sp):
            def load_xT(b):
                sp.dma_start(xT_sb[:], xT[b]).then_inc(xT_in, 16)

            def load_x(b):
                sp.dma_start(x_sb[:], x[b].rearrange("(t p) d -> p t d", p=128)).then_inc(x_in, 16)

            def load_raw(b, t):
                sp.dma_start(raw[t % RAW][:], adjT[b, t * 128:(t + 1) * 128, :]).then_inc(raw_in[t % RAW], 16)

            def send_parts(b, s):
                sp.wait_ge(parts_made, 2 * b + s + 1)
                for i in range(3):
                    sp.dma_start(scratch[s, i].rearrange("h d n -> (h d) n"), parts[s][i]).then_inc(parts_out, 16)

            def send_shift(b):
                sp.wait_ge(parts_out, (b + 1) * 96)
                sp.wait_ge(taken["cq"], b + 1)
                sp.dma_start(shift_scratch, negshift[:]).then_inc(shift_out, 16)

            def load_stack(g):
                heads = slice(g * HG, (g + 1) * HG)
                for r in range(BLOCKS):
                    rows = slice(r * HD, (r + 1) * HD)
                    sp.dma_start(qst[rows, heads], scratch[0, QPART[r], heads].rearrange("h d n -> d h n")).then_inc(stack_in[g], 16)
                    sp.dma_start(kst[rows, heads], scratch[1, KPART[r], heads].rearrange("h d n -> d h n")).then_inc(stack_in[g], 16)
                sp.dma_start(qst[KROWS:SROWS, heads], shift_scratch[heads].rearrange("(o h) n -> o h n", o=1)).then_inc(stack_in[g], 16)

            load_xT(0)
            for dst, src in ((wq, Wq), (wk, Wk), (wv, Wv), (wo, Wo), (w_of, W),
                             (acol, a.rearrange("o (c d) -> d (o c)", c=2))):
                with nc.allow_non_contiguous_dma(reason="a is 256 numbers"):
                    sp.dma_start(dst[:], src).then_inc(consts_in, 16)
            sp.dma_start(bo_all[:], bo_row.to_broadcast([128, D])).then_inc(out_done, 16)
            for t in range(RAW):
                load_raw(0, t)
            for s in range(2):
                send_parts(0, s)
            send_shift(0)
            sp.wait_ge(shift_out, 16)
            load_stack(0)

            def batch(kind, b):
                sp.wait_ge(full["unit"], b * UNITS)
                for t in range(RAW, T):
                    if t == STACK1_BEFORE:
                        load_stack(1)
                    sp.wait_ge(masks_made, b * T + t - RAW + 1)
                    load_raw(b, t)
                if kind != "last":
                    sp.wait_ge(full["v1"], b + 1)
                    sp.wait_ge(xsum_made, b + 1)
                    load_xT(b + 1)
                    for t in range(RAW):
                        sp.wait_ge(masks_made, b * T + min(t + 7, T))
                        load_raw(b + 1, t)
                if kind != "first":
                    sp.wait_ge(taken["wo"], b)
                load_x(b)
                if kind != "last":
                    sp.wait_ge(stack_in[1], (b + 1) * 16 * STACK_DMAS)
                    for s in range(2):
                        send_parts(b + 1, s)
                    send_shift(b + 1)
                    sp.wait_ge(shift_out, (b + 2) * 16)
                    load_stack(0)
                if kind != "first":
                    store(b - 1)

            def store(b):
                sp.wait_ge(y_made, b + 1)
                sp.dma_start(out[b].rearrange("(t p) d -> p t d", p=128), y[:]).then_inc(out_done, 16)

            batch("first", 0)
            with sp.Fori(1, B - 1) as b:
                batch("loop", b)
            batch("last", B - 1)
            sp.wait_ge(too_far_made, 1)
            sp.dma_start(flag_scratch.rearrange("o h -> h o"), too_far[:]).then_inc(flags_out, 16)
            sp.wait_ge(flags_out, 16)
            sp.dma_start(too_far_row[:], flag_scratch).then_inc(flags_in, 16)
            store(B - 1)
            sp.wait_ge(out_done, 16 * (B + 1))

        @block.tensor
        def _(pe):
            kw = dict(start=True, stop=True)

            def context(b, n, c):
                g, t = divmod(n, T)
                if c == 0:
                    for e, done in (("d", masked_dve), ("p", masked_pool)):
                        if e in MASKED_BY[n]:
                            pe.wait_ge(done, b * by[e] + masked(e, n, HG - 1))
                    if t == 0:
                        pe.wait_ge(acc_read, b * NG + g)
                        pe.wait_ge(taken[f"v{g}"], b + 1)
                cols = slice(c * HALF, (c + 1) * HALF)
                for i in range(HG):
                    mm = pe.matmul(acc[VW * i:VW * (i + 1), cols], vst[:, t, g * HG + i],
                                   weights[:, HG * BUFFER[n] + i, cols], start=(t == 0), stop=(t == T - 1))
                if c == 1:
                    mm.then_inc(contexts_done, 1)

            def unit(kind, b, n, i):
                g, t = divmod(n, T)
                h = g * HG + i
                job = ("unit", 0, HG * n + i)
                ps = slots[slot[kind, job]]
                pe.wait_ge(*free_for(kind, b, job))
                for c in range(2):
                    cols = slice(c * HALF, (c + 1) * HALF)
                    mm = pe.matmul(ps[:, cols], kst[:, h, t * 128:(t + 1) * 128], qst[:, h, cols], **kw)
                mm.then_inc(full["unit"], 1)

            def job(kind, b, name, parts=(0, 1)):
                off = {"prologue": 1, "epilogue": -1}.get(kind, OFFSET[STAGES[name]])
                me = b + off
                ps = slots[slot[kind, (name, off, 0)]]
                mm = None
                tiles = [t for t in range(T) if t // 4 in parts]
                if 0 in parts:
                    pe.wait_ge(*free_for(kind, b, (name, off, 0)))
                if name in ("q", "k"):
                    if name == "q" and 0 in parts:
                        pe.wait_ge(xT_in, (me + 1) * 16)
                    for c in parts:
                        cols = slice(c * HALF, (c + 1) * HALF)
                        mm = pe.matmul(ps[:, cols], (wq if name == "q" else wk)[:], xT_sb[:, cols], **kw)
                elif name in ("cq", "ck"):
                    s = 0 if name == "cq" else 1
                    if 0 in parts:
                        pe.wait_ge(squares_made, 2 * me + s + 1)
                    for c in parts:
                        cols = slice(c * HALF, (c + 1) * HALF)
                        mm = pe.matmul(ps[0:H, cols], headsum[:], squares[s][:, cols], **kw)
                elif name in ("v0", "v1"):
                    half = slice(int(name[1]) * 64, int(name[1]) * 64 + 64)
                    for t in tiles:
                        mm = pe.matmul(ps[:, t * 64:(t + 1) * 64], xT_sb[:, t * 128:(t + 1) * 128], wv[:, half], **kw)
                elif name == "vsum":
                    if 1 in parts:
                        pe.wait_ge(xsum_made, me + 1)
                        mm = pe.matmul(ps[:, 0:D], xsum_wide[:], wv[:], **kw)
                elif name in ("ctx0", "ctx1"):
                    if 0 in parts:
                        pe.wait_ge(acc_read, me * NG + NG)
                    for t in [t for t in range(4) if t // 2 in parts]:
                        for g in range(NG):
                            u = 4 * int(name[3]) + t
                            mm = pe.transpose(ps[:, (t * NG + g) * 128:(t * NG + g + 1) * 128],
                                              ctxT[g][:, u * 128:(u + 1) * 128], ident[:])
                elif name == "ctxT":
                    for t in tiles:
                        if t % 4 == 0:
                            pe.wait_ge(ctxn_made, 2 * me + t // 4 + 1)
                        mm = pe.transpose(ps[:, t * 128:(t + 1) * 128], ctxn[:, t], ident[:])
                elif name == "wo":
                    if 0 in parts:
                        pe.wait_ge(taken["ctxT"], me + 1)
                    for t in tiles:
                        mm = pe.matmul(ps[:, t * 128:(t + 1) * 128], ctxnT[:, t * 128:(t + 1) * 128], wo[:], **kw)
                elif name == "x1T":
                    if 0 in parts:
                        pe.wait_ge(x1_made, me + 1)
                    for t in tiles:
                        mm = pe.transpose(ps[:, t * 128:(t + 1) * 128], x1[:, t], ident[:])
                elif name in ("h0", "h1"):
                    if 0 in parts:
                        pe.wait_ge(taken["x1T"], me + 1)
                    for t in [t for t in range(4) if t // 2 in parts]:
                        u = 4 * int(name[1]) + t
                        mm = pe.matmul(ps[:, t * 256:t * 256 + D + 2], x1T[:, u * 128:(u + 1) * 128], wh[:], **kw)
                elif name in ("fi", "fjmax"):
                    for c in parts:
                        cols = slice(c * HALF, (c + 1) * HALF)
                        mm = pe.matmul(ps[:, cols], uwide[:, 0 if name == "fi" else 1], x1T[:, cols], **kw)
                elif name == "hsum":
                    if 1 in parts:
                        pe.wait_ge(x1sum_made, me + 1)
                        mm = pe.matmul(ps[:, 0:D + 2], x1sum_wide[:], wh[:], **kw)
                else:
                    k = int(name[3])
                    if 0 in parts:
                        for e, done in atts_made.items():
                            pe.wait_ge(done, (me + 1) * ATTS_MASKED_BY.count(e))
                    for t in parts:
                        for j in range(T):
                            mm = pe.matmul(ps[:, t * HALF:t * HALF + HW], atts[:, k, j, t * 128:(t + 1) * 128],
                                           hst[:, j], start=(j == 0), stop=(j == T - 1))
                if 1 in parts:
                    mm.then_inc(full[name], 1)

            pe.wait_ge(consts_in, 96)
            pe.wait_ge(consts_made, 2)
            pe.transpose(acc[:, 0:D], w_of[:], ident[:])
            pe.matmul(acc[:, D:D + 2], w_of[:], acol[:], **kw)
            for i in range(2):
                mm = pe.matmul(acc[:, 256 + i * D:256 + (i + 1) * D], w_of[:], awide[:, i], **kw)
            mm.then_inc(setup_mm, 1)
            for name in PREP:
                job("prologue", -1, name)
            pe.wait_ge(setup_copied, 1)

            def batch(kind, b):
                for n in range(QUADS):
                    if n % T == 0:
                        pe.wait_ge(stack_in[n // T], (b + 1) * 16 * STACK_DMAS)
                    for c in range(2):
                        for i in (2 * c, 2 * c + 1):
                            unit(kind, b, n, i)
                            for ago, half in CONTEXT_AFTER[i]:
                                if n >= ago:
                                    context(b, n - ago, half)
                                elif kind != "first":
                                    context(b - 1, QUADS + n - ago, half)
                            for name in jobs_after(kind, 2 * n + c):
                                if name in SPLIT:
                                    job(kind, b, name, (i % 2,))
                                elif i % 2:
                                    job(kind, b, name)

            batch("first", 0)
            with pe.Fori(1, B - 1) as b:
                batch("loop", b)
            batch("last", B - 1)
            for n, half in contexts_left():
                context(B - 1, n, half)
            for name in POST:
                job("epilogue", B, name)

        @block.scalar
        def _(act):
            def job(kind, b, name):
                off = {"prologue": 1, "epilogue": -1}.get(kind, OFFSET[STAGES[name]])
                me = b + off
                ps = slots[slot[kind, (name, off, 0)]]
                if name in ("ctx0", "ctx1", "ck", "wo", "fjmax") or name[:3] == "out":
                    return
                act.wait_ge(full[name], me + 1)
                if name in ("q", "k"):
                    s = 0 if name == "q" else 1
                    act.activation(parts[s][0], ps[:], ACT.Copy).then_inc(part0_made, 1)
                    return
                if name == "cq":
                    act.wait_ge(kmax_made, me + 1)
                    act.wait_ge(shift_out, me * 16)
                    ins = act.activation(negshift[:], ps[0:H], ACT.Identity, bias=negkmax[:], scale=-1.0)
                elif name in ("v0", "v1"):
                    g = int(name[1])
                    if kind != "prologue":
                        act.wait_ge(contexts_done, me * QUADS + (g + 1) * T - QUADS)
                    ins = act.activation(vst[:, :, g * HG:(g + 1) * HG, 0:HD],
                                         ps[:, 0:HALF].rearrange("p (t h d) -> p t h d", t=T, h=HG), ACT.Copy)
                elif name == "vsum":
                    act.wait_ge(ctxn_made, me * 2)
                    ins = act.activation(vsum[:], ps[:, 0:D], ACT.Copy)
                elif name == "ctxT":
                    ins = act.activation(ctxnT[:], ps[:], ACT.Copy)
                elif name == "x1T":
                    ins = act.activation(x1T, ps[:], ACT.Copy)
                elif name in ("h0", "h1"):
                    k = int(name[1])
                    view = ps[:].rearrange("p (t w) -> p t w", w=256)[:, :, 0:D + 2]
                    ins = act.activation(hst[:, 4 * k:4 * k + 4, 0:D + 2], view, ACT.Copy)
                elif name == "fi":
                    act.wait_ge(below_made, me + 1)
                    act.wait_ge(parts_made, min_parts(me) * 2)
                    act.activation(fall[:], ps[:], ACT.Relu, bias=pivot[:, 0:1], scale=1.0 - ALPHA)
                    ins = act.activation(exp_rise[:], ps[:], ACT.Relu, bias=pivot[:, 1:2], scale=ALPHA - 1.0)
                elif name == "hsum":
                    ins = act.activation(hsum[:], ps[:, 0:D + 2], ACT.Copy)
                ins.then_inc(taken[name], 1)
                if name == "fi":
                    act.wait_ge(taken["fi"], me + 1)
                    act.activation(exp_rise[:], exp_rise[:], ACT.Exp, scale=-1.0)
                    act.activation(exp_below[:], below[:, 0], ACT.Exp).then_inc(rows_made, 1)

            def min_parts(b):
                return b + 3 if not (isinstance(b, int) and b + 3 > B) else B

            def read_acc(b, g):
                act.wait_ge(contexts_done, b * QUADS + (g + 1) * T)
                act.activation(ctxT[g], acc[:], ACT.Copy).then_inc(acc_read, 1)

            def exp_atts(b, j):
                if j == 0:
                    act.wait_ge(parts_out, min_parts(b) * 96)
                    act.wait_ge(full["cq"], min_parts(b))
                act.wait_ge(taken["fi"], b + 1)
                act.activation(atts[:, :, j, :], fall[:].rearrange("p (q n) -> p q n", q=4), ACT.Exp,
                               bias=below[:, 1, j:j + 1], scale=-1.0).then_inc(atts_exp, 1)

            act.wait_ge(setup_mm, 1)
            act.activation(wh[:], acc[:, 0:D + 2], ACT.Copy)
            act.activation(uwide[:].rearrange("p i d -> p (i d)"), acc[:, 256:256 + 2 * D],
                           ACT.Copy).then_inc(setup_copied, 1)
            for name in PREP:
                job("prologue", -1, name)

            def batch(kind, b):
                for n in range(QUADS):
                    for i in range(HG):
                        u = HG * n + i
                        act.wait_ge(full["unit"], b * UNITS + u + 1)
                        before = last_with_buffer(n)
                        if i == 0 and (kind != "first" or before >= 0):
                            act.wait_ge(contexts_done, b * QUADS + before + 1)
                        act.activation(weights[:, HG * BUFFER[n] + i], slots[slot[kind, ("unit", 0, u)]][:], ACT.Exp,
                                       scale=SCALE).then_inc(taken["unit"], 1)
                        if n == 1 and i == READ_ACC and kind != "first":
                            read_acc(b - 1, 1)
                        if n == 9 and i == READ_ACC:
                            read_acc(b, 0)
                        half = 2 * n + i // 2
                        if i % 2 == 0:
                            continue
                        for name in jobs_after(kind, half):
                            job(kind, b, name)
                        if kind != "first":
                            for k in range(T):
                                if half == EXP_ATTS[k]:
                                    exp_atts(b - 1, k)

            batch("first", 0)
            with act.Fori(1, B - 1) as b:
                batch("loop", b)
            batch("last", B - 1)
            read_acc(B - 1, 1)
            for name in POST:
                job("epilogue", B, name)
                if name == "fi":
                    for k in range(T):
                        exp_atts(B - 1, k)

        @block.gpsimd
        def _(pool):
            pool.memset(ones[:], 1.0)
            pool.memset(headsum[:], NORM_WEIGHT).then_inc(pool_step, 1)
            pool.wait_ge(pool_step, 1)
            pool.affine_select(out=ident[:], in_=ones[:], compare_op=ALU.is_equal, fill=0.0, base=0,
                               pattern=[[-1, 128]], channel_multiplier=1).then_inc(pool_step, 1)
            pool.wait_ge(pool_step, 2)
            pool.affine_select(out=headsum[:], in_=headsum[:], compare_op=ALU.is_ge, fill=0.0, base=0,
                               pattern=[[-HD, H]], channel_multiplier=1).then_inc(pool_step, 1)
            pool.wait_ge(pool_step, 3)
            pool.affine_select(out=headsum[:], in_=headsum[:], compare_op=ALU.is_ge, fill=0.0, base=HD - 1,
                               pattern=[[HD, H]], channel_multiplier=-1).then_inc(pool_step, 1)
            pool.wait_ge(pool_step, 4)
            pool.memset(exponent[:], -0.5).then_inc(consts_made, 1)

            def residual(b):
                pool.wait_ge(x_in, (b + 1) * 16)
                pool.tensor_tensor(x_sb[:], x_sb[:], bo_all[:].unsqueeze(1).to_broadcast([128, T, D]),
                                   ALU.add).then_inc(xb_made, 1)

            def inverse_root(b, k):
                pool.wait_ge(vareps_made, 2 * b + k + 1)
                pool.tensor_tensor(rstd[:], vareps[:], exponent[:], ALU.pow).then_inc(rstd_made, 1)

            def mask_atts(b, j):
                if ATTS_MASKED_BY[j] == "p":
                    pool.wait_ge(atts_max, b * T + j + 1)
                    pool.tensor_tensor(atts[:, :, j, :], atts[:, :, j, :],
                                       old_mask[:, j].rearrange("p (q n) -> p q n", q=4),
                                       ALU.mult).then_inc(atts_made["p"], 1)

            def others(kind, b, half):
                if kind != "first":
                    if half == POW1:
                        inverse_root(b - 1, 0)
                    for j in range(T):
                        if half == MASK_ATTS[j]:
                            mask_atts(b - 1, j)
                    if half == POW2:
                        inverse_root(b - 1, 1)
                if half == RESIDUAL:
                    residual(b)

            pool.wait_ge(out_done, 16)

            def batch(kind, b):
                for n in range(QUADS):
                    t = n % T
                    for i in range(HG):
                        if MASKED_BY[n][i] == "p":
                            u = HG * BUFFER[n] + i
                            pool.wait_ge(masks_made, b * T + t + 1)
                            pool.wait_ge(taken["unit"], b * UNITS + HG * n + i + 1)
                            pool.tensor_tensor(weights[:, u], weights[:, u], mask[:, t],
                                               ALU.mult).then_inc(masked_pool, 1)
                        if i % 2:
                            others(kind, b, 2 * n + i // 2)

            batch("first", 0)
            with pool.Fori(1, B - 1) as b:
                batch("loop", b)
            batch("last", B - 1)
            inverse_root(B - 1, 0)
            for j in range(T):
                mask_atts(B - 1, j)
            inverse_root(B - 1, 1)

        @block.vector
        def _(dve):
            chain = {"n": 0, "base": 0}

            def link(ins):
                chain["n"] += 1
                ins.then_inc(dve_step, 1)
                dve.wait_ge(dve_step, chain["base"] + chain["n"])

            def keep_mask(t):
                link(dve.tensor_copy(old_mask[:, t], mask[:, t]))

            def make_mask(b, t):
                if not isinstance(b, int) or b:
                    keep_mask(t)
                m = t % RAW
                count = (T - m + RAW - 1) // RAW
                dve.wait_ge(raw_in[m], (b * count + t // RAW + 1) * 16)
                dve.tensor_scalar(mask[:, t], raw[m][:], 0, None, ALU.is_gt).then_inc(masks_made, 1)

            def split(b, s, ps):
                name = "qk"[s]
                dve.wait_ge(part0_made, 2 * b + s + 1)
                dve.wait_ge(parts_made, 2 * b + s)
                dve.tensor_tensor(rest[:], ps[:], parts[s][0], ALU.subtract).then_inc(taken[name], 1)
                dve.tensor_tensor(squares[s], parts[s][0], parts[s][0], ALU.mult).then_inc(squares_made, 1)
                dve.wait_ge(taken[name], b + 1)
                link(dve.tensor_copy(parts[s][1], rest[:]))
                dve.tensor_tensor(parts[s][2], rest[:], parts[s][1], ALU.subtract).then_inc(parts_made, 1)

            def divide_contexts(b, k, ps):
                view = ps[:].rearrange("p (t h d) -> p t h d", t=4, h=H)
                tt = slice(4 * k, 4 * k + 4)
                name = f"ctx{k}"
                link(dve.tensor_scalar(empty[:, tt], view[:, :, :, HD], 0.0, None, ALU.is_equal))
                link(dve.scalar_tensor_tensor(out=den[:, tt], in0=empty[:, tt], scalar=float(N),
                                              in1=view[:, :, :, HD], op0=ALU.mult, op1=ALU.add))
                dve.reciprocal(rden[:, tt], den[:, tt])
                dve.wait_ge(taken["vsum"], b + 1)
                link(dve.tensor_tensor(fix, empty[:, tt].unsqueeze(3).to_broadcast([128, 4, H, HD]),
                                       vsum[:].rearrange("p (h d) -> p h d", h=H).unsqueeze(1).to_broadcast([128, 4, H, HD]),
                                       ALU.mult))
                dve.tensor_tensor(fix, view[:, :, :, 0:HD], fix, ALU.add).then_inc(taken[name], 1)
                dve.wait_ge(taken[name], b + 1)
                dve.tensor_tensor(ctxn[:, tt].rearrange("p t (h d) -> p t h d", h=H), fix,
                                  rden[:, tt].unsqueeze(3).to_broadcast([128, 4, H, HD]), ALU.mult).then_inc(ctxn_made, 1)
                dve.wait_ge(ctxn_made, 2 * b + k + 1)

            def norm_stats(src):
                for t in range(T):
                    ins = dve.bn_stats(stats[:, t], src[:, t])
                link(ins)
                dve.memset(carrier[:], 0.0)
                for t in range(T):
                    ins = dve.bn_aggr(meanvar[:, t], stats[:, t])
                link(ins)
                dve.tensor_scalar(vareps[:], meanvar[:, :, 1], EPS, None, ALU.add).then_inc(vareps_made, 1)

            def normalise(b, k, src, dst, done):
                dve.wait_ge(rstd_made, 2 * b + k + 1)
                for t in range(T):
                    ins = dve.tensor_scalar(dst[:, t], src[:, t], meanvar[:, t, 0:1], rstd[:, t:t + 1],
                                            ALU.subtract, ALU.mult)
                ins.then_inc(done, 1)

            def max_atts(b, j):
                dve.wait_ge(atts_exp, b * T + j + 1)
                dve.wait_ge(rows_made, b + 1)
                dve.scalar_tensor_tensor(out=atts[:, :, j, :], in0=exp_rise[:].rearrange("p (q n) -> p q n", q=4),
                                         scalar=exp_below[:, j:j + 1], in1=atts[:, :, j, :], op0=ALU.mult,
                                         op1=ALU.max).then_inc(atts_max, 1)

            def mask_atts(b, j):
                if ATTS_MASKED_BY[j] == "d":
                    dve.wait_ge(atts_max, b * T + j + 1)
                    dve.tensor_tensor(atts[:, :, j, :], atts[:, :, j, :],
                                      old_mask[:, j].rearrange("p (q n) -> p q n", q=4),
                                      ALU.mult).then_inc(atts_made["d"], 1)

            def job(kind, b, name):
                off = {"prologue": 1, "epilogue": -1}.get(kind, OFFSET[STAGES[name]])
                me = b + off
                ps = slots[slot[kind, (name, off, 0)]]
                if name in ("q", "k", "ctx0", "ctx1", "wo", "ck", "cq", "fjmax") or name[:3] == "out":
                    if name != "cq":
                        dve.wait_ge(full[name], me + 1)
                if name in ("q", "k"):
                    split(me, 0 if name == "q" else 1, ps)
                elif name == "ck":
                    dve.tensor_reduce(kmax[:], ps[0:H], AX_X, ALU.max).then_inc(taken["ck"], 1)
                    dve.wait_ge(taken["ck"], me + 1)
                    dve.tensor_scalar(negkmax[:], kmax[:], -1.0, None, ALU.mult).then_inc(kmax_made, 1)
                elif name == "cq":
                    dve.wait_ge(taken["cq"], me + 1)
                    link(dve.tensor_reduce(worst_row[:], negshift[:], AX_X, ALU.min))
                    link(dve.tensor_tensor(worst[:], worst[:], worst_row[:], ALU.min))
                elif name in ("ctx0", "ctx1"):
                    divide_contexts(me, int(name[3]), ps)
                elif name == "fjmax":
                    dve.tensor_reduce(fmax[:], ps[:], AX_X, ALU.max).then_inc(taken["fjmax"], 1)
                    dve.wait_ge(taken["fjmax"], me + 1)
                    for i, scale in enumerate((1.0 - ALPHA, ALPHA - 1.0)):
                        dve.tensor_scalar(pivot[:, i:i + 1], fmax[:], scale, None, ALU.mult)
                    dve.wait_ge(taken["h1"], me + 1)
                    link(dve.tensor_scalar(below[:, 0], hst[:, :, D + 1], fmax[:], None, ALU.subtract))
                    dve.tensor_scalar(below[:, 1], below[:, 0], ALPHA, None, ALU.mult).then_inc(below_made, 1)
                    link(dve.tensor_reduce(lowest[:], below[:, 0], AX_X, ALU.min))
                    link(dve.tensor_tensor(farthest[:], farthest[:], lowest[:], ALU.min))
                elif name == "wo":
                    dve.wait_ge(xb_made, me + 1)
                    dve.wait_ge(out_done, (me + 1) * 16)
                    dve.tensor_tensor(y[:].rearrange("p t d -> p (t d)"), ps[:],
                                      x_sb[:].rearrange("p t d -> p (t d)"), ALU.add).then_inc(taken["wo"], 1)
                    dve.wait_ge(taken["wo"], me + 1)
                    norm_stats(y)
                elif name == "x1T":
                    dve.wait_ge(taken["x1T"], me + 1)
                    link(dve.tensor_reduce(x1sum[:], x1T, AX_X, ALU.add))
                    dve.tensor_copy(x1sum_wide[:], x1sum[:].to_broadcast([D, 128])).then_inc(x1sum_made, 1)
                elif name[:3] == "out":
                    k = int(name[3])
                    view = ps[:].rearrange("p (t w) -> p t w", t=2)
                    tt = slice(2 * k, 2 * k + 2)
                    dcol = view[:, :, D + 2]
                    link(dve.tensor_scalar(empty[:, tt, 0], dcol, 0.0, None, ALU.is_equal))
                    link(dve.scalar_tensor_tensor(out=den[:, tt, 0], in0=empty[:, tt, 0], scalar=float(N),
                                                  in1=dcol, op0=ALU.mult, op1=ALU.add))
                    link(dve.reciprocal(den[:, tt, 1], den[:, tt, 0]))
                    link(dve.tensor_tensor(empty[:, tt, 1], empty[:, tt, 0], den[:, tt, 1], ALU.mult))
                    for t in range(2):
                        u = 2 * k + t
                        ins = dve.scalar_tensor_tensor(out=y[:, u], in0=view[:, t, 0:D], scalar=den[:, u, 1:2],
                                                       in1=x1[:, u], op0=ALU.mult, op1=ALU.add)
                    ins.then_inc(taken[name], 1)
                    dve.wait_ge(taken[name], me + 1)
                    dve.wait_ge(taken["hsum"], me + 1)
                    for t in range(2):
                        u = 2 * k + t
                        ins = dve.scalar_tensor_tensor(out=y[:, u], in0=hsum[:, 0:D], scalar=empty[:, u, 1:2],
                                                       in1=y[:, u], op0=ALU.mult, op1=ALU.add)
                    link(ins)

            dve.wait_ge(consts_in, 96)
            dve.memset(farthest[:], 0.0)
            dve.memset(worst[:], 0.0)
            dve.memset(kst[KROWS:SROWS], 1.0)
            dve.memset(hst[:, :, D + 2:HW], 1.0)
            link(dve.memset(vst[:, :, :, HD:VW], 0.0))
            dve.memset(vst[:, :, :, HD:HD + 1], 1.0)
            dve.tensor_copy(awide[:], acol[:].unsqueeze(2).to_broadcast([D, 2, D])).then_inc(consts_made, 1)
            for name in PREP:
                job("prologue", -1, name)

            def others(kind, b, half):
                if half % 2 == 0 and half // 2 < T - 1:
                    make_mask(b, half // 2 + 1)
                if half == 2:
                    dve.wait_ge(xT_in, (b + 1) * 16)
                    link(dve.tensor_reduce(xsum[:], xT_sb[:], AX_X, ALU.add))
                    dve.tensor_copy(xsum_wide[:], xsum[:].to_broadcast([D, 128])).then_inc(xsum_made, 1)
                if kind != "first":
                    if half == NORM1:
                        normalise(b - 1, 0, y, x1, x1_made)
                    for j in range(T):
                        if half == MAX_ATTS[j]:
                            max_atts(b - 1, j)
                    for j in range(T):
                        if half == MASK_ATTS[j]:
                            mask_atts(b - 1, j)
                for name in jobs_after(kind, half):
                    job(kind, b, name)
                if kind != "first" and half == STATS2:
                    norm_stats(y)
                if kind != "first" and half == NORM2:
                    normalise(b - 1, 1, y, y, y_made)

            def batch(kind, b):
                for n in range(QUADS):
                    t = n % T
                    if n == 0:
                        make_mask(b, 0)
                    for i in range(HG):
                        if MASKED_BY[n][i] == "d":
                            u = HG * BUFFER[n] + i
                            dve.wait_ge(masks_made, b * T + t + 1)
                            dve.wait_ge(taken["unit"], b * UNITS + HG * n + i + 1)
                            dve.tensor_tensor(weights[:, u], weights[:, u], mask[:, t],
                                              ALU.mult).then_inc(masked_dve, 1)
                        if i % 2:
                            others(kind, b, 2 * n + i // 2)

            batch("first", 0)
            first_steps = chain["n"]
            chain["n"] = 0
            with dve.Fori(1, B - 1) as b:
                chain["base"] = first_steps - LOOP_STEPS + b * LOOP_STEPS
                batch("loop", b)
                assert chain["n"] == LOOP_STEPS, chain["n"]
            chain["base"] = first_steps + (B - 2) * LOOP_STEPS
            chain["n"] = 0
            batch("last", B - 1)
            for t in range(T):
                keep_mask(t)
            for name in POST:
                job("epilogue", B, name)
                if name == "wo":
                    normalise(B - 1, 0, y, x1, x1_made)
                if name == "fjmax":
                    link(dve.tensor_scalar(worst[:], worst[:], 0.5, None, ALU.mult))
                    link(dve.tensor_tensor(farthest[0:H], farthest[0:H], worst[:], ALU.min))
                    dve.tensor_scalar(too_far[:], farthest[:], -FARTHEST, None, ALU.is_lt).then_inc(too_far_made, 1)
                if name == "fi":
                    for k in range(T):
                        max_atts(B - 1, k)
                    for k in range(T):
                        mask_atts(B - 1, k)
            dve.wait_ge(flags_in, 16)
            link(dve.tensor_reduce(needed[:], too_far_row[:], AX_X, ALU.max))
            norm_stats(y)
            normalise(B - 1, 1, y, y, y_made)


def build_exact(nc, sems, needed, x, xT, adj, adjT, Wq, Wk, Wv, Wo, bo, W, a, out):
    B, N, D = x.shape
    H = 8
    HD = D // H
    T = N // 128
    HALF = N // 2
    CH = T // 2
    HG = 4
    NG = H // HG
    SCALE = 1.0 / float(HD) ** 0.5
    KROWS = BLOCKS * HD
    SROWS = KROWS + 3
    HW = D + 3
    VW = 32

    with ExitStack() as ctx:
        def sb(name, shape, dt):
            return ctx.enter_context(nc.sbuf_tensor(f"exact_{name}", shape, dt))

        def sem(name):
            return sems.enter_context(nc.semaphore(f"exact_{name}"))

        slots = [ctx.enter_context(nc.psum_tensor(f"exact_slot{i}", [128, N], F32)) for i in range(3)]
        acc = ctx.enter_context(nc.psum_tensor("exact_acc", [128, N], F32))

        ident = sb("ident", [128, 128], F32)
        identb = sb("identb", [128, 128], BF16)
        ones = sb("ones", [128, 128], F32)
        negones = sb("negones", [128, 128], F32)
        wq = sb("wq", [D, D], F32)
        wk = sb("wk", [D, D], F32)
        wv = sb("wv", [D, D], F32)
        wo = sb("wo", [D, D], F32)
        w_of = sb("w_of", [D, D], F32)
        acol = sb("acol", [D, 2], F32)
        a1wide = sb("a1wide", [D, D], F32)
        wh = sb("wh", [D, D + 2], F32)
        u1wide = sb("u1wide", [D, 2, D], F32)
        bo_all = sb("bo_all", [128, D], F32)
        exponent = sb("exponent", [128, T], F32)

        carrier = sb("carrier", [128, H * T + 2], F32)

        xT_sb = sb("xT_sb", [D, N], F32)
        x_sb = sb("x_sb", [128, T, D], F32)
        xb = sb("xb", [128, T, D], F32)
        raw = [sb(f"raw{i}", [128, 2, N], I32) for i in range(2)]
        biasT = sb("biasT", [128, T, N], BF16)
        biasN = sb("biasN", [128, T, N], BF16)
        rest = sb("rest", [128, N], F32)
        parts = [[sb(f"{n}part{i}", [128, N], BF16) for i in range(3)] for n in "qk"]
        qst = sb("qst", [SROWS, H, N], BF16)
        kst = sb("kst", [SROWS, H, N], BF16)
        vst = sb("vst", [128, T, H, VW], F32)
        vsum = sb("vsum", [128, H, VW], F32)
        rowmax = sb("rowmax", [128, H * T], F32)
        negmax = sb("negmax", [128, H * T], F32)
        negrest = sb("negrest", [H * T, 128], F32)
        negparts = [sb(f"negpart{i}", [H * T, 128], BF16) for i in range(3)]
        weights = sb("weights", [128, T, N], F32)
        ctxT = sb("ctxT", [128, NG, N], F32)
        ctxn = sb("ctxn", [128, T, D], F32)
        fix = sb("fix", [128, 4, H, HD], F32)
        den = sb("den", [128, T, H], F32)
        empty = sb("empty", [128, T, H], F32)
        rden = sb("rden", [128, T, H], F32)
        ctxnT = sb("ctxnT", [D, N], F32)
        y = sb("y", [128, T, D], F32)
        x1 = sb("x1", [128, T, D], F32)
        x1T = sb("x1T", [D, N], F32)
        stats = sb("stats", [128, T, 6], F32)
        meanvar = sb("meanvar", [128, T, 2], F32)
        vareps = sb("vareps", [128, T], F32)
        rstd = sb("rstd", [128, T], F32)
        hst = sb("hst", [128, T, HW], F32)
        hsum = sb("hsum", [128, HW], F32)
        running = sb("running", [128, N], F32)
        nbmax = sb("nbmax", [128, T], F32)
        shift = sb("shift", [128, T], F32)
        diag = sb("diag", [128, T, 128], F32)
        row1 = rest
        row2 = sb("row2", [128, N], F32)

        scratch = nc.dram_tensor("exact_parts_scratch", [2, 3, H, HD, N], BF16, kind="Internal").ap()
        negscratch = nc.dram_tensor("exact_neg_scratch", [3, H * T, 128], BF16, kind="Internal").ap()

        jobs = ["q", "k", "v", "vsum"]
        jobs += [("max", h, t) for h in range(H) for t in range(T)]
        jobs += ["negmax"]
        jobs += [("unit", g, t, i) for g in range(NG) for t in range(T) for i in range(HG)]
        jobs += ["ctx0", "ctx1", "ctxT", "wo", "x1T", "h0", "h1", "hsum", "runT", "row1", "row2",
                 "out0", "out1"]
        slot_of = {j: n % 3 for n, j in enumerate(jobs)}
        use_of = {j: n // 3 for n, j in enumerate(jobs)}
        uses = [sum(1 for j in jobs if slot_of[j] == s) for s in range(3)]
        slot_full = [sem(f"slot{i}_full") for i in range(3)]
        slot_free = [sem(f"slot{i}_free") for i in range(3)]

        def free_for(b, job):
            return slot_free[slot_of[job]], b * uses[slot_of[job]] + use_of[job]

        def full(b, job):
            return slot_full[slot_of[job]], b * uses[slot_of[job]] + use_of[job] + 1

        def read_by(b, job):
            return slot_free[slot_of[job]], b * uses[slot_of[job]] + use_of[job] + 1

        def alone(eng, at):
            eng.memset(carrier[:, at:at + 1], 0.0)

        consts_in = sem("consts_in")
        bo_in = sem("bo_in")
        consts_made = sem("consts_made")
        setup_mm = sem("setup_mm")
        setup_copied = sem("setup_copied")
        x_in = sem("x_in")
        raw_in = [sem(f"raw{i}_in") for i in range(2)]
        masks_made = sem("masks_made")
        part0_made = sem("part0_made")
        parts_made = sem("parts_made")
        parts_out = sem("parts_out")
        stacks_in = sem("stacks_in")
        vsum_made = sem("vsum_made")
        negparts_made = sem("negparts_made")
        negparts_out = sem("negparts_out")
        negmax_made = sem("negmax_made")
        units_used = sem("units_used")
        acc_full = sem("acc_full")
        acc_read = sem("acc_read")
        ctxn_made = sem("ctxn_made")
        xb_made = sem("xb_made")
        vareps_made = sem("vareps_made")
        rstd_made = sem("rstd_made")
        x1_made = sem("x1_made")
        running_made = sem("running_made")
        diag_made = sem("diag_made")
        logits_made = sem("logits_made")
        logits_masked = sem("logits_masked")
        weights_made = sem("weights_made")
        y_out = sem("y_out")
        out_done = sem("out_done")
        dve_step = sem("dve_step")
        pool_step = sem("pool_step")
        DVE_STEPS = 46
        SETUP_STEPS = 1

        block = ctx.enter_context(nc.Block())
        bo_row = bo.rearrange("(o d) -> o d", o=1)

        @block.sync
        def _(sp):
            run = sp.value_load(needed[:], min_val=0, max_val=1)
            with sp.If(run > 0):
                for dst, src in ((wq, Wq), (wk, Wk), (wv, Wv), (wo, Wo), (w_of, W),
                                 (acol, a.rearrange("o (c d) -> d (o c)", c=2))):
                    with nc.allow_non_contiguous_dma(reason="a is 256 numbers"):
                        sp.dma_start(dst[:], src).then_inc(consts_in, 16)
                sp.dma_start(bo_all[:], bo_row.to_broadcast([128, D])).then_inc(bo_in, 16)
                def batch(b):
                    sp.wait_ge(slot_full[slot_of["v"]], b * uses[slot_of["v"]])
                    sp.wait_ge(xb_made, b)
                    sp.dma_start(xT_sb[:], xT[b]).then_inc(x_in, 16)
                    sp.dma_start(x_sb[:], x[b].rearrange("(t p) d -> p t d", p=128)).then_inc(x_in, 16)
                    for c in range(2 * CH):
                        src = (adjT if c < CH else adj)[b].rearrange("(t p) n -> p t n", p=128)
                        t0 = 2 * (c % CH)
                        if c >= 2:
                            sp.wait_ge(masks_made, b * 2 * CH + c - 1)
                        else:
                            sp.wait_ge(masks_made, b * 2 * CH)
                        sp.dma_start(raw[c % 2][:], src[:, t0:t0 + 2, :]).then_inc(raw_in[c % 2], 16)
                    for s in range(2):
                        sp.wait_ge(parts_made, 2 * b + s + 1)
                        for i in range(3):
                            sp.dma_start(scratch[s, i].rearrange("h d n -> (h d) n"),
                                         parts[s][i][:]).then_inc(parts_out, 16)
                    sp.wait_ge(parts_out, b * 96 + 96)
                    sp.wait_ge(units_used, b * H * T)
                    for r in range(BLOCKS):
                        rows = slice(r * HD, (r + 1) * HD)
                        sp.dma_start(qst[rows], scratch[0, QPART[r]].rearrange("h d n -> d h n")).then_inc(stacks_in, 16)
                        sp.dma_start(kst[rows], scratch[1, KPART[r]].rearrange("h d n -> d h n")).then_inc(stacks_in, 16)
                    sp.wait_ge(negparts_made, b + 1)
                    for i in range(3):
                        sp.dma_start(negscratch[i], negparts[i][:]).then_inc(negparts_out, 16)
                    sp.wait_ge(negparts_out, b * 48 + 48)
                    sp.dma_start(qst[KROWS:SROWS],
                                 negscratch.rearrange("i (h t) n -> i h (t n)", h=H)).then_inc(negmax_made, 16)
                    sp.wait_ge(y_out, b + 1)
                    sp.dma_start(out[b].rearrange("(t p) d -> p t d", p=128), y[:]).then_inc(out_done, 16)

                batch(0)
                with sp.Fori(1, B) as b:
                    batch(b)
                sp.wait_ge(out_done, 16 * B)

        @block.tensor
        def _(pe):
            run = pe.value_load(needed[:], min_val=0, max_val=1)
            with pe.If(run > 0):
                kw = dict(start=True, stop=True)
                pe.wait_ge(consts_in, 96)
                pe.wait_ge(consts_made, 2)
                pe.transpose(slots[0][:, 0:D], w_of[:], ident[:])
                pe.matmul(slots[0][:, D:D + 2], w_of[:], acol[:], **kw)
                pe.matmul(slots[0][:, 256:256 + D], w_of[:], a1wide[:], **kw).then_inc(setup_mm, 1)
                pe.wait_ge(setup_copied, 1)
                def batch(b):
                    pe.wait_ge(x_in, b * 32 + 32)
                    for job, w in (("q", wq), ("k", wk)):
                        pe.wait_ge(*free_for(b, job))
                        ps = slots[slot_of[job]]
                        for c in range(2):
                            cols = slice(c * HALF, (c + 1) * HALF)
                            mm = pe.matmul(ps[:, cols], w[:], xT_sb[:, cols], **kw)
                        mm.then_inc(slot_full[slot_of[job]], 1)
                    pe.wait_ge(*free_for(b, "v"))
                    ps = slots[slot_of["v"]]
                    for t in range(T):
                        mm = pe.matmul(ps[:, t * 128:(t + 1) * 128], xT_sb[:, t * 128:(t + 1) * 128], wv[:], **kw)
                    mm.then_inc(slot_full[slot_of["v"]], 1)
                    pe.wait_ge(*free_for(b, "vsum"))
                    ps = slots[slot_of["vsum"]]
                    pe.wait_ge(*read_by(b, "v"))
                    for t in range(T):
                        mm = pe.matmul(ps[:, 0:H * VW], ones[:], vst[:, t].rearrange("p h d -> p (h d)"),
                                       start=(t == 0), stop=(t == T - 1))
                    mm.then_inc(slot_full[slot_of["vsum"]], 1)

                    pe.wait_ge(stacks_in, b * 32 * BLOCKS + 32 * BLOCKS)
                    for h in range(H):
                        for t in range(T):
                            pe.wait_ge(*free_for(b, ("max", h, t)))
                            ps = slots[slot_of[("max", h, t)]]
                            for c in range(2):
                                cols = slice(c * HALF, (c + 1) * HALF)
                                mm = pe.matmul(ps[:, cols], qst[0:KROWS, h, t * 128:(t + 1) * 128],
                                               kst[0:KROWS, h, cols], **kw)
                            mm.then_inc(slot_full[slot_of[("max", h, t)]], 1)
                    pe.wait_ge(*free_for(b, "negmax"))
                    ps = slots[slot_of["negmax"]]
                    pe.wait_ge(dve_step, SETUP_STEPS + b * DVE_STEPS + NEG_STEP)
                    mm = pe.matmul(ps[0:H * T, 0:128], negmax[:], ident[:], **kw)
                    mm.then_inc(slot_full[slot_of["negmax"]], 1)

                    pe.wait_ge(negmax_made, b * 16 + 16)
                    pe.wait_ge(masks_made, (b + 1) * 2 * CH)

                    def scores(g, t, i):
                        h = g * HG + i
                        job = ("unit", g, t, i)
                        pe.wait_ge(*free_for(b, job))
                        ps = slots[slot_of[job]]
                        for c in range(2):
                            cols = slice(c * HALF, (c + 1) * HALF)
                            pe.matmul(ps[:, cols], identb[:], biasT[:, t, cols], start=True, stop=False)
                            mm = pe.matmul(ps[:, cols], kst[:, h, t * 128:(t + 1) * 128], qst[:, h, cols],
                                           start=False, stop=True)
                        mm.then_inc(slot_full[slot_of[job]], 1)

                    def context(g, t):
                        quad = g * T + t
                        for i in range(HG):
                            pe.wait_ge(*read_by(b, ("unit", g, t, i)))
                        if t == 0:
                            pe.wait_ge(acc_read, b * NG + g)
                        for c in range(2):
                            cols = slice(c * HALF, (c + 1) * HALF)
                            for i in range(HG):
                                mm = pe.matmul(acc[VW * i:VW * (i + 1), cols], vst[:, t, g * HG + i],
                                               weights[:, (HG * quad + i) % 8, cols],
                                               start=(t == 0), stop=(t == T - 1))
                        mm.then_inc(units_used, HG)

                    quads = [(g, t) for g in range(NG) for t in range(T)]
                    for n, (g, t) in enumerate(quads):
                        for i in range(HG):
                            scores(g, t, i)
                        if n:
                            context(*quads[n - 1])
                    context(*quads[-1])

                    for k in range(2):
                        job = f"ctx{k}"
                        pe.wait_ge(*free_for(b, job))
                        ps = slots[slot_of[job]]
                        pe.wait_ge(acc_read, b * NG + NG)
                        for t in range(4):
                            for g in range(NG):
                                mm = pe.transpose(ps[:, (t * NG + g) * 128:(t * NG + g + 1) * 128],
                                                  ctxT[:, g, (4 * k + t) * 128:(4 * k + t + 1) * 128], ident[:])
                        mm.then_inc(slot_full[slot_of[job]], 1)
                    pe.wait_ge(*free_for(b, "ctxT"))
                    ps = slots[slot_of["ctxT"]]
                    pe.wait_ge(ctxn_made, 2 * b + 2)
                    for t in range(T):
                        mm = pe.transpose(ps[:, t * 128:(t + 1) * 128], ctxn[:, t], ident[:])
                    mm.then_inc(slot_full[slot_of["ctxT"]], 1)
                    pe.wait_ge(*free_for(b, "wo"))
                    ps = slots[slot_of["wo"]]
                    pe.wait_ge(*read_by(b, "ctxT"))
                    for t in range(T):
                        mm = pe.matmul(ps[:, t * 128:(t + 1) * 128], ctxnT[:, t * 128:(t + 1) * 128], wo[:], **kw)
                    mm.then_inc(slot_full[slot_of["wo"]], 1)

                    pe.wait_ge(*free_for(b, "x1T"))
                    ps = slots[slot_of["x1T"]]
                    pe.wait_ge(x1_made, b + 1)
                    for t in range(T):
                        mm = pe.transpose(ps[:, t * 128:(t + 1) * 128], x1[:, t], ident[:])
                    mm.then_inc(slot_full[slot_of["x1T"]], 1)
                    pe.wait_ge(*read_by(b, "x1T"))
                    for k in range(2):
                        job = f"h{k}"
                        pe.wait_ge(*free_for(b, job))
                        ps = slots[slot_of[job]]
                        for t in range(4):
                            mm = pe.matmul(ps[:, t * 256:t * 256 + D + 2],
                                           x1T[:, (4 * k + t) * 128:(4 * k + t + 1) * 128], wh[:], **kw)
                        mm.then_inc(slot_full[slot_of[job]], 1)
                    pe.wait_ge(*free_for(b, "hsum"))
                    ps = slots[slot_of["hsum"]]
                    for k in range(2):
                        pe.wait_ge(*read_by(b, f"h{k}"))
                    for t in range(T):
                        mm = pe.matmul(ps[:, 0:HW], ones[:], hst[:, t], start=(t == 0), stop=(t == T - 1))
                    mm.then_inc(slot_full[slot_of["hsum"]], 1)
                    pe.wait_ge(*free_for(b, "runT"))
                    ps = slots[slot_of["runT"]]
                    pe.wait_ge(running_made, b + 1)
                    for t in range(T):
                        mm = pe.transpose(ps[:, t * 128:(t + 1) * 128], running[:, t * 128:(t + 1) * 128], ident[:])
                    mm.then_inc(slot_full[slot_of["runT"]], 1)
                    for k in range(2):
                        job = f"row{k + 1}"
                        pe.wait_ge(*free_for(b, job))
                        ps = slots[slot_of[job]]
                        pe.wait_ge(diag_made, b + 1)
                        for c in range(2):
                            cols = slice(c * HALF, (c + 1) * HALF)
                            pe.matmul(ps[:, cols], u1wide[:, k], x1T[:, cols], start=True, stop=False)
                            mm = pe.matmul(ps[:, cols], negones[:],
                                           diag[:, 4 * c:4 * c + 4].rearrange("p t n -> p (t n)"),
                                           start=False, stop=True)
                        mm.then_inc(slot_full[slot_of[job]], 1)
                    for k in range(2):
                        job = f"out{k}"
                        pe.wait_ge(*free_for(b, job))
                        ps = slots[slot_of[job]]
                        pe.wait_ge(weights_made, b * T + T)
                        for t in range(4):
                            for j in range(T):
                                mm = pe.matmul(ps[:, t * 256:t * 256 + HW],
                                               weights[:, j, (4 * k + t) * 128:(4 * k + t + 1) * 128],
                                               hst[:, j], start=(j == 0), stop=(j == T - 1))
                        mm.then_inc(slot_full[slot_of[job]], 1)

                batch(0)
                with pe.Fori(1, B) as b:
                    batch(b)

        @block.scalar
        def _(act):
            run = act.value_load(needed[:], min_val=0, max_val=1)
            with act.If(run > 0):
                act.wait_ge(setup_mm, 1)
                act.activation(wh[:], slots[0][:, 0:D + 2], ACT.Copy)
                act.activation(u1wide[:, 1], slots[0][:, 256:256 + D], ACT.Copy, scale=ALPHA)
                act.activation(u1wide[:, 0], slots[0][:, 256:256 + D], ACT.Copy).then_inc(setup_copied, 1)
                def batch(b):
                    for s, job in enumerate("qk"):
                        act.wait_ge(*full(b, job))
                        ps = slots[slot_of[job]]
                        act.wait_ge(parts_out, b * 96)
                        act.activation(parts[s][0][:], ps[:], ACT.Copy).then_inc(part0_made, 1)
                    act.wait_ge(*full(b, "vsum"))
                    ps = slots[slot_of["vsum"]]
                    act.wait_ge(ctxn_made, 2 * b)
                    ins = act.activation(vsum[:].rearrange("p h d -> p (h d)"), ps[:, 0:H * VW], ACT.Copy)
                    ins.then_inc(slot_free[slot_of["vsum"]], 1)
                    n = 0
                    for g in range(NG):
                        for t in range(T):
                            for i in range(HG):
                                act.wait_ge(*full(b, ("unit", g, t, i)))
                                ps = slots[slot_of[("unit", g, t, i)]]
                                if n >= 8:
                                    act.wait_ge(units_used, b * H * T + n - 7 + (-(n - 7)) % HG)
                                else:
                                    act.wait_ge(units_used, b * H * T)
                                    if n == 0:
                                        act.wait_ge(y_out, b)
                                ins = act.activation(weights[:, n % 8], ps[:], ACT.Exp, scale=SCALE)
                                ins.then_inc(slot_free[slot_of[("unit", g, t, i)]], 1)
                                n += 1
                    act.wait_ge(*full(b, "ctxT"))
                    ps = slots[slot_of["ctxT"]]
                    ins = act.activation(ctxnT[:], ps[:], ACT.Copy)
                    ins.then_inc(slot_free[slot_of["ctxT"]], 1)
                    act.wait_ge(*full(b, "x1T"))
                    ps = slots[slot_of["x1T"]]
                    ins = act.activation(x1T[:], ps[:], ACT.Copy)
                    ins.then_inc(slot_free[slot_of["x1T"]], 1)
                    for k in range(2):
                        act.wait_ge(*full(b, f"h{k}"))
                        ps = slots[slot_of[f"h{k}"]]
                        view = ps[:].rearrange("p (t w) -> p t w", w=256)[:, :, 0:D + 2]
                        ins = act.activation(hst[:, 4 * k:4 * k + 4, 0:D + 2], view, ACT.Copy)
                        ins.then_inc(slot_free[slot_of[f"h{k}"]], 1)
                    act.wait_ge(*full(b, "hsum"))
                    ps = slots[slot_of["hsum"]]
                    ins = act.activation(hsum[:], ps[:, 0:HW], ACT.Copy)
                    ins.then_inc(slot_free[slot_of["hsum"]], 1)
                    for k, row in enumerate((row1, row2)):
                        act.wait_ge(*full(b, f"row{k + 1}"))
                        ps = slots[slot_of[f"row{k + 1}"]]
                        ins = act.activation(row[:], ps[:], ACT.Copy)
                        ins.then_inc(slot_free[slot_of[f"row{k + 1}"]], 1)
                    for t in range(T):
                        act.wait_ge(logits_masked, b * T + t + 1)
                        act.activation(weights[:, t], weights[:, t], ACT.Exp).then_inc(weights_made, 1)

                batch(0)
                with act.Fori(1, B) as b:
                    batch(b)

        @block.gpsimd
        def _(pool):
            run = pool.value_load(needed[:], min_val=0, max_val=1)
            with pool.If(run > 0):
                pool.memset(ones[:], 1.0)
                pool.memset(negones[:], -1.0)
                pool.memset(exponent[:], -0.5).then_inc(pool_step, 1)
                pool.wait_ge(pool_step, 1)
                pool.affine_select(out=ident[:], in_=ones[:], compare_op=ALU.is_equal, fill=0.0, base=0,
                                   pattern=[[-1, 128]], channel_multiplier=1).then_inc(pool_step, 1)
                pool.wait_ge(pool_step, 2)
                pool.tensor_copy(identb[:], ident[:]).then_inc(consts_made, 1)
                pool.wait_ge(bo_in, 16)
                def batch(b):
                    pool.wait_ge(x_in, b * 32 + 32)
                    pool.wait_ge(x1_made, b)
                    pool.tensor_tensor(xb[:], x_sb[:], bo_all[:].unsqueeze(1).to_broadcast([128, T, D]),
                                       ALU.add).then_inc(xb_made, 1)
                    pool.wait_ge(vareps_made, 2 * b + 1)
                    pool.tensor_tensor(rstd[:], vareps[:], exponent[:], ALU.pow).then_inc(rstd_made, 1)
                    for t in range(T):
                        pool.wait_ge(logits_made, b * T + t + 1)
                        pool.tensor_tensor(weights[:, t], weights[:, t], biasT[:, t],
                                           ALU.add).then_inc(logits_masked, 1)
                    pool.wait_ge(vareps_made, 2 * b + 2)
                    pool.tensor_tensor(rstd[:], vareps[:], exponent[:], ALU.pow).then_inc(rstd_made, 1)

                batch(0)
                with pool.Fori(1, B) as b:
                    batch(b)

        @block.vector
        def _(dve):
            run = dve.value_load(needed[:], min_val=0, max_val=1)
            with dve.If(run > 0):
                steps = [0]
                base = [0]

                def link(ins):
                    steps[0] += 1
                    ins.then_inc(dve_step, 1)
                    dve.wait_ge(dve_step, base[0] + steps[0])

                dve.wait_ge(consts_in, 96)
                dve.memset(kst[KROWS:SROWS], 1.0)
                dve.memset(hst[:, :, D + 2:HW], 1.0)
                link(dve.memset(vst[:, :, :, HD:VW], 0.0))
                dve.memset(vst[:, :, :, HD:HD + 1], 1.0)
                dve.tensor_copy(a1wide[:], acol[:, 0:1].to_broadcast([D, D])).then_inc(consts_made, 1)
                assert steps[0] == SETUP_STEPS

                def layernorm(b, k, src, dst):
                    for t in range(T):
                        ins = dve.bn_stats(stats[:, t], src[:, t])
                    link(ins)
                    alone(dve, H * T + k)
                    for t in range(T):
                        ins = dve.bn_aggr(meanvar[:, t], stats[:, t])
                    link(ins)
                    dve.tensor_scalar(vareps[:], meanvar[:, :, 1], EPS, None, ALU.add).then_inc(vareps_made, 1)
                    dve.wait_ge(rstd_made, 2 * b + k + 1)
                    for t in range(T):
                        ins = dve.tensor_scalar(dst[:, t], src[:, t], meanvar[:, t, 0:1], rstd[:, t:t + 1],
                                                ALU.subtract, ALU.mult)
                    return ins

                def batch(b):
                    base[0] = SETUP_STEPS + b * DVE_STEPS
                    steps[0] = 0
                    for c in range(2 * CH):
                        dve.wait_ge(raw_in[c % 2], (b * CH + c // 2 + 1) * 16)
                        if c == 0:
                            dve.wait_ge(logits_masked, b * T)
                        t0 = 2 * (c % CH)
                        dst = (biasT if c < CH else biasN)[:, t0:t0 + 2, :]
                        dve.tensor_scalar(dst, raw[c % 2][:], 0, -BIG, ALU.is_le, ALU.mult).then_inc(masks_made, 1)
                    for s, job in enumerate("qk"):
                        dve.wait_ge(*full(b, job))
                        ps = slots[slot_of[job]]
                        dve.wait_ge(part0_made, 2 * b + s + 1)
                        ins = dve.tensor_tensor(rest[:], ps[:], parts[s][0][:], ALU.subtract)
                        ins.then_inc(slot_free[slot_of[job]], 1)
                        dve.wait_ge(*read_by(b, job))
                        link(dve.tensor_copy(parts[s][1][:], rest[:]))
                        ins = dve.tensor_tensor(parts[s][2][:], rest[:], parts[s][1][:], ALU.subtract)
                        ins.then_inc(parts_made, 1)
                        dve.wait_ge(parts_made, 2 * b + s + 1)
                    dve.wait_ge(*full(b, "v"))
                    ps = slots[slot_of["v"]]
                    ins = dve.tensor_copy(vst[:, :, :, 0:HD], ps[:].rearrange("p (t h d) -> p t h d", t=T, h=H))
                    ins.then_inc(slot_free[slot_of["v"]], 1)

                    for h in range(H):
                        for t in range(T):
                            dve.wait_ge(*full(b, ("max", h, t)))
                            ps = slots[slot_of[("max", h, t)]]
                            if h == 0 and t == 0:
                                link(dve.memset(rowmax[:], 0.0))
                            alone(dve, h * T + t)
                            ins = dve.tensor_tensor_reduce(ps[:], ps[:], biasN[:, t], 1.0, -3.0e38, ALU.add,
                                                           ALU.max, rowmax[:, h * T + t:h * T + t + 1])
                            ins.then_inc(slot_free[slot_of[("max", h, t)]], 1)
                    for t in range(T - 3, T):
                        dve.wait_ge(*read_by(b, ("max", H - 1, t)))
                    link(dve.tensor_scalar(negmax[:], rowmax[:], FLOOR, -1.0, ALU.max, ALU.mult))
                    assert steps[0] == NEG_STEP, ("neg", steps[0])
                    dve.wait_ge(*full(b, "negmax"))
                    ps = slots[slot_of["negmax"]]
                    neg = ps[0:H * T, 0:128]
                    dve.wait_ge(negparts_out, b * 48)
                    link(dve.tensor_copy(negparts[0][:], neg))
                    ins = dve.tensor_tensor(negrest[:], neg, negparts[0][:], ALU.subtract)
                    ins.then_inc(slot_free[slot_of["negmax"]], 1)
                    dve.wait_ge(*read_by(b, "negmax"))
                    link(dve.tensor_copy(negparts[1][:], negrest[:]))
                    dve.tensor_tensor(negparts[2][:], negrest[:], negparts[1][:], ALU.subtract).then_inc(negparts_made, 1)

                    for g in range(NG):
                        dve.wait_ge(units_used, b * H * T + (g + 1) * HG * T)
                        dve.tensor_copy(ctxT[:, g], acc[:]).then_inc(acc_read, 1)
                    for k in range(2):
                        dve.wait_ge(*full(b, f"ctx{k}"))
                        ps = slots[slot_of[f"ctx{k}"]]
                        view = ps[:].rearrange("p (t h d) -> p t h d", t=4, h=H)
                        tt = slice(4 * k, 4 * k + 4)
                        link(dve.tensor_scalar(empty[:, tt], view[:, :, :, HD], 0.0, None, ALU.is_equal))
                        link(dve.scalar_tensor_tensor(out=den[:, tt], in0=empty[:, tt], scalar=float(N),
                                                      in1=view[:, :, :, HD], op0=ALU.mult, op1=ALU.add))
                        link(dve.reciprocal(rden[:, tt], den[:, tt]))
                        dve.wait_ge(*read_by(b, "vsum"))
                        link(dve.tensor_tensor(fix[:], empty[:, tt].unsqueeze(3).to_broadcast([128, 4, H, HD]),
                                               vsum[:, :, 0:HD].unsqueeze(1).to_broadcast([128, 4, H, HD]), ALU.mult))
                        ins = dve.tensor_tensor(fix[:], view[:, :, :, 0:HD], fix[:], ALU.add)
                        ins.then_inc(slot_free[slot_of[f"ctx{k}"]], 1)
                        dve.wait_ge(*read_by(b, f"ctx{k}"))
                        ins = dve.tensor_tensor(ctxn[:, tt].rearrange("p t (h d) -> p t h d", h=H), fix[:],
                                                rden[:, tt].unsqueeze(3).to_broadcast([128, 4, H, HD]), ALU.mult)
                        ins.then_inc(ctxn_made, 1)
                    dve.wait_ge(*full(b, "wo"))
                    ps = slots[slot_of["wo"]]
                    dve.wait_ge(xb_made, b + 1)
                    dve.wait_ge(out_done, b * 16)
                    ins = dve.tensor_tensor(y[:].rearrange("p t d -> p (t d)"), ps[:],
                                            xb[:].rearrange("p t d -> p (t d)"), ALU.add)
                    ins.then_inc(slot_free[slot_of["wo"]], 1)
                    dve.wait_ge(*read_by(b, "wo"))
                    ins = layernorm(b, 0, y, x1)
                    ins.then_inc(x1_made, 1)
                    for k in range(2):
                        dve.wait_ge(*read_by(b, f"h{k}"))
                    link(dve.tensor_scalar(running[:], biasT[:, 0], hst[:, 0, D + 1:D + 2], None, ALU.add))
                    for t in range(1, T):
                        ins = dve.scalar_tensor_tensor(out=running[:], in0=biasT[:, t], scalar=hst[:, t, D + 1:D + 2],
                                                       in1=running[:], op0=ALU.add, op1=ALU.max)
                        if t < T - 1:
                            link(ins)
                    ins.then_inc(running_made, 1)
                    dve.wait_ge(*full(b, "runT"))
                    ps = slots[slot_of["runT"]]
                    ins = dve.tensor_reduce(nbmax[:], ps[:].rearrange("p (t n) -> p t n", t=T), AX_X, ALU.max)
                    ins.then_inc(slot_free[slot_of["runT"]], 1)
                    dve.wait_ge(*read_by(b, "runT"))
                    link(dve.tensor_tensor(nbmax[:], nbmax[:], hst[:, :, D], ALU.add))
                    link(dve.scalar_tensor_tensor(out=shift[:], in0=nbmax[:], scalar=ALPHA, in1=nbmax[:],
                                                  op0=ALU.mult, op1=ALU.max))
                    dve.tensor_tensor(diag[:], ident[:].unsqueeze(1).to_broadcast([128, T, 128]),
                                      shift[:].unsqueeze(2).to_broadcast([128, T, 128]), ALU.mult).then_inc(diag_made, 1)
                    link(dve.tensor_scalar(rden[:, :, 0], hst[:, :, D + 1], ALPHA, None, ALU.mult))
                    for k in range(2):
                        dve.wait_ge(*read_by(b, f"row{k + 1}"))
                    dve.wait_ge(units_used, (b + 1) * H * T)
                    for t in range(T):
                        link(dve.tensor_scalar(weights[:, t], row1[:], hst[:, t, D + 1:D + 2], None, ALU.add))
                        ins = dve.scalar_tensor_tensor(out=weights[:, t], in0=row2[:], scalar=rden[:, t, 0:1],
                                                       in1=weights[:, t], op0=ALU.add, op1=ALU.max)
                        ins.then_inc(logits_made, 1)
                    dve.wait_ge(*read_by(b, "hsum"))
                    for k in range(2):
                        dve.wait_ge(*full(b, f"out{k}"))
                        ps = slots[slot_of[f"out{k}"]]
                        view = ps[:].rearrange("p (t w) -> p t w", w=256)
                        tt = slice(4 * k, 4 * k + 4)
                        dcol = view[:, :, D + 2]
                        link(dve.tensor_scalar(empty[:, tt, 0], dcol, 0.0, None, ALU.is_equal))
                        link(dve.scalar_tensor_tensor(out=den[:, tt, 0], in0=empty[:, tt, 0], scalar=float(N),
                                                      in1=dcol, op0=ALU.mult, op1=ALU.add))
                        link(dve.reciprocal(den[:, tt, 1], den[:, tt, 0]))
                        link(dve.tensor_tensor(empty[:, tt, 1], empty[:, tt, 0], den[:, tt, 1], ALU.mult))
                        for t in range(4):
                            u = 4 * k + t
                            ins = dve.scalar_tensor_tensor(out=y[:, u], in0=view[:, t, 0:D], scalar=den[:, u, 1:2],
                                                           in1=x1[:, u], op0=ALU.mult, op1=ALU.add)
                        ins.then_inc(slot_free[slot_of[f"out{k}"]], 1)
                        dve.wait_ge(*read_by(b, f"out{k}"))
                        for t in range(4):
                            u = 4 * k + t
                            ins = dve.scalar_tensor_tensor(out=y[:, u], in0=hsum[:, 0:D], scalar=empty[:, u, 1:2],
                                                           in1=y[:, u], op0=ALU.mult, op1=ALU.add)
                        link(ins)
                    layernorm(b, 1, y, y).then_inc(y_out, 1)
                    assert steps[0] == DVE_STEPS, steps[0]

                batch(0)
                with dve.Fori(1, B) as b:
                    batch(b)


def kernel(x, adj, L0_gnn_Wq, L0_gnn_Wk, L0_gnn_Wv, L0_gnn_Wo, L0_gnn_bo, L1_gnn_W, L1_gnn_a):
    import numpy as np
    import concourse.bacc as bacc
    from concourse.bass_utils import run_bass_kernel_spmd

    x, adj = np.asarray(x), np.asarray(adj)
    ins = {
        "x": x, "xT": np.ascontiguousarray(x.transpose(0, 2, 1)),
        "adj": adj, "adjT": np.ascontiguousarray(adj.transpose(0, 2, 1)),
        "Wq": np.asarray(L0_gnn_Wq), "Wk": np.asarray(L0_gnn_Wk), "Wv": np.asarray(L0_gnn_Wv),
        "Wo": np.asarray(L0_gnn_Wo), "bo": np.asarray(L0_gnn_bo), "W": np.asarray(L1_gnn_W),
        "a": np.asarray(L1_gnn_a),
    }
    nc = bacc.Bacc("TRN2", target_bir_lowering=False, num_devices=1)
    arrays, args = {}, []
    for name, v in ins.items():
        arrays[f"in_{name}"] = v
        args.append(nc.dram_tensor(f"in_{name}", v.shape, mybir.dt.from_np(v.dtype), kind="ExternalInput").ap())
    args.append(nc.dram_tensor("out_0", x.shape, F32, kind="ExternalOutput").ap())
    x_, xT, adj_, adjT, *rest = args
    with ExitStack() as outer:
        needed = outer.enter_context(nc.sbuf_tensor("needed", [1, 1], I32))
        build_fast(nc, outer, needed, x_, xT, adjT, *rest)
        build_exact(nc, outer, needed, x_, xT, adj_, adjT, *rest)
    r = run_bass_kernel_spmd(nc, [arrays], core_ids=[0])
    return r.results[0]["out_0"]
```
